# Optimizing a Trainium2 kernel written in Bass

```python
import numpy as np
import jax
import jax.numpy as jnp

def _softmax(x, axis=-1):
    return jax.nn.softmax(x, axis=axis)

def _gelu(x):
    return jax.nn.gelu(x, approximate=True)

def _silu(x):
    return jax.nn.silu(x)

def _sigmoid(x):
    return jax.nn.sigmoid(x)

def _layernorm(x, axis=-1, eps=1e-05):
    m = jnp.mean(x, axis=axis, keepdims=True)
    v = jnp.var(x, axis=axis, keepdims=True)
    return (x - m) / jnp.sqrt(v + eps)

def _scatter_add(tgt, idx, src, axis=0):
    return tgt.at[idx].add(src)

def _segment_sum(src, seg, n):
    return jax.ops.segment_sum(src, seg, n)
kernel_name = 'mk_decoder_postln_d1_seqx_r2_5a76fd'

def setup_inputs(seed: int=0):
    np.random.seed(seed)
    _w = jnp.asarray

    def _rec_inputs():
        import jax
        import jax.numpy as jnp
        _rk = jax.random.key(seed)
        x = 7.22e-05 + 1 * jax.random.normal(jax.random.fold_in(_rk, 1), (2, 2048, 512), jnp.float32)
        _lenS = 2048 - jax.random.randint(jax.random.fold_in(_rk, 7), (2,), 0, max(1, 2048 // 4) + 1, jnp.int32)
        _lenS2 = 154 - jax.random.randint(jax.random.fold_in(_rk, 8), (2,), 0, max(1, 154 // 4) + 1, jnp.int32)
        _ctx_1024P = jax.random.normal(jax.random.fold_in(_rk, 11), (2, 16, 512), jnp.float32)
        _ctx_1024c = jax.random.dirichlet(jax.random.fold_in(_rk, 511), 0.3 * jnp.ones((16,), jnp.float32), (2, 154))
        _ctx_1024t = jnp.einsum('bsk,bkd->bsd', _ctx_1024c, _ctx_1024P)
        _ctx_1024t = _ctx_1024t * jax.lax.rsqrt(jnp.mean(jnp.square(_ctx_1024t)) + 1e-12) * 0.953939
        ctx_1024 = 4.13588e-05 + 0.999923 * (_ctx_1024t + 0.3 * jax.random.normal(jax.random.fold_in(_rk, 611), (2, 154, 512), jnp.float32))
        _validS = jnp.arange(2048)[None, :] < _lenS[:, None]
        _validS2 = jnp.arange(154)[None, :] < _lenS2[:, None]
        _causal = jnp.tril(jnp.ones((2048, 2048), dtype=bool))
        mask_SxS2_bk0 = jnp.logical_not(jnp.broadcast_to(_validS2[0:1, :], (2048, 154)))
        return (x, ctx_1024, mask_SxS2_bk0)
    x, ctx_1024, mask_SxS2_bk0 = _rec_inputs()

    def _L0_attn_setup():
        import jax, jax.numpy as jnp
        import numpy as np
        CHUNK = 64
        HEADS = 16

        def _chunk_mask(T, cs):
            idx = jnp.arange(T)
            blk = idx // cs * cs
            qb = blk[:, None]
            kb = blk[None, :]
            masked = (qb >= kb) & (idx[None, :] - idx[:, None] - 2 * (kb - qb) >= 1)
            return masked
        key = jax.random.key(seed)
        ks = jax.random.split(key, 6)
        B, T, C = (2, 1024, 512)
        w = 0.02
        return {'x': jax.random.normal(ks[0], (B, T, C), jnp.float32), 'Wq': jax.random.normal(ks[1], (C, C), jnp.float32) * w, 'bq': jnp.zeros((C,), jnp.float32), 'Wk': jax.random.normal(ks[2], (C, C), jnp.float32) * w, 'bk': jnp.zeros((C,), jnp.float32), 'Wv': jax.random.normal(ks[3], (C, C), jnp.float32) * w, 'bv': jnp.zeros((C,), jnp.float32), 'Wo': jax.random.normal(ks[4], (C, C), jnp.float32) * w, 'bo': jnp.zeros((C,), jnp.float32), 'attn_scale': jnp.full((1,), 1.0 / np.sqrt(C // HEADS), jnp.float32)}
    _L0_attn_all = _L0_attn_setup()
    _L0_attn_in = {k: v for k, v in _L0_attn_all.items() if k in ('Wq', 'bq', 'Wk', 'bk', 'Wv', 'bv', 'Wo', 'bo', 'attn_scale')}
    del _L0_attn_all

    def _L0_xattn_setup():
        import jax, jax.numpy as jnp
        import numpy as np
        D_MODEL = 512
        NUM_HEADS = 16
        D_K = D_MODEL // NUM_HEADS
        B, S = (4, 1024)
        key = jax.random.key(seed)
        ks = jax.random.split(key, 12)
        std = 1.0 / np.sqrt(D_MODEL)
        inp = {'q': jax.random.normal(ks[0], (B, S, D_MODEL), dtype=jnp.float32), 'k': jax.random.normal(ks[1], (B, S, D_MODEL), dtype=jnp.float32), 'v': jax.random.normal(ks[2], (B, S, D_MODEL), dtype=jnp.float32), 'mask': jnp.tril(jnp.ones((S, S), dtype=bool)), 'wq': jax.random.normal(ks[3], (D_MODEL, D_MODEL), dtype=jnp.float32) * std, 'bq': jnp.zeros((D_MODEL,), dtype=jnp.float32), 'wk': jax.random.normal(ks[4], (D_MODEL, D_MODEL), dtype=jnp.float32) * std, 'bk': jnp.zeros((D_MODEL,), dtype=jnp.float32), 'wv': jax.random.normal(ks[5], (D_MODEL, D_MODEL), dtype=jnp.float32) * std, 'bv': jnp.zeros((D_MODEL,), dtype=jnp.float32), 'wo': jax.random.normal(ks[6], (D_MODEL, D_MODEL), dtype=jnp.float32) * std, 'bo': jnp.zeros((D_MODEL,), dtype=jnp.float32)}
        return inp
    _L0_xattn_all = _L0_xattn_setup()
    _L0_xattn_in = {k: v for k, v in _L0_xattn_all.items() if k in ('wq', 'bq', 'wk', 'bk', 'wv', 'bv', 'wo', 'bo')}
    del _L0_xattn_all

    def _L0_ffn_setup():
        import jax, jax.numpy as jnp
        import numpy as np
        E, K, NG, TG = (64, 8, 8, 4)
        CAP = 512
        SCALE = 2.5

        def _route(x_flat, gate_weight, e_bias):
            T = x_flat.shape[0]
            logits = x_flat.astype(jnp.float32) @ gate_weight.astype(jnp.float32).T
            scores = jax.nn.sigmoid(logits)
            sfc = scores + e_bias[None, :]
            group_scores = jax.lax.top_k(sfc.reshape(T, NG, E // NG), 2)[0].sum(-1)
            _, gidx = jax.lax.top_k(group_scores, TG)
            gmask = jnp.zeros((T, NG), jnp.float32).at[jnp.arange(T)[:, None], gidx].set(1.0)
            smask = jnp.repeat(gmask, E // NG, axis=1)
            tmp = jnp.where(smask > 0, sfc, 0.0)
            _, topk_idx = jax.lax.top_k(tmp, K)
            topk_w = jnp.take_along_axis(scores, topk_idx, axis=1)
            topk_w = topk_w / (topk_w.sum(-1, keepdims=True) + 1e-20)
            return (topk_idx, topk_w * SCALE)

        def _moe_forward(hidden_states, gate_weight, e_bias, w1, w2, w3, shared_gate, shared_up, shared_down):
            B, S, H = hidden_states.shape
            T = B * S
            x = hidden_states.reshape(T, H)
            topk_idx, topk_w = _route(x, gate_weight, e_bias)
            Sk = T * K
            flat_e = topk_idx.reshape(-1)
            order = jnp.argsort(flat_e)
            sorted_e = flat_e[order]
            counts = jax.ops.segment_sum(jnp.ones((Sk,), jnp.int32), flat_e, num_segments=E)
            offsets = jnp.cumsum(counts) - counts
            pos = jnp.arange(Sk) - offsets[sorted_e]
            tok_sorted = x[order // K]
            xe = jnp.zeros((E, CAP, H), x.dtype).at[sorted_e, pos].set(tok_sorted, mode='drop')
            h = jax.nn.silu(jnp.einsum('ech,efh->ecf', xe, w1)) * jnp.einsum('ech,efh->ecf', xe, w3)
            ye = jnp.einsum('ecf,ehf->ech', h, w2)
            pos_c = jnp.minimum(pos, CAP - 1)
            vals = ye[sorted_e, pos_c]
            vals = jnp.where((pos < CAP)[:, None], vals, 0.0)
            flat_w = topk_w.reshape(-1)[order].astype(vals.dtype)
            flat_t = (jnp.arange(Sk) // K)[order]
            out = jax.ops.segment_sum(vals * flat_w[:, None], flat_t, num_segments=T)
            shared = jax.nn.silu(x @ shared_gate.T) * (x @ shared_up.T) @ shared_down.T
            return (out + shared).reshape(B, S, H)
        key = jax.random.key(seed)
        ks = jax.random.split(key, 9)
        B, S, H, F = (1, 1024, 512, 256)
        bound = 1.0 / 32.0
        return {'hidden_states': jax.random.normal(ks[0], (B, S, H), jnp.float32), 'gate_weight': jax.random.uniform(ks[1], (E, H), jnp.float32, -bound, bound), 'e_bias': jnp.zeros((E,), jnp.float32), 'w1': jax.random.normal(ks[2], (E, F, H), jnp.float32) * 0.02, 'w2': jax.random.normal(ks[3], (E, H, F), jnp.float32) * 0.02, 'w3': jax.random.normal(ks[4], (E, F, H), jnp.float32) * 0.02, 'shared_gate': jax.random.normal(ks[5], (2 * F, H), jnp.float32) * 0.02, 'shared_up': jax.random.normal(ks[6], (2 * F, H), jnp.float32) * 0.02, 'shared_down': jax.random.normal(ks[7], (H, 2 * F), jnp.float32) * 0.02}
    _L0_ffn_all = _L0_ffn_setup()
    _L0_ffn_in = {k: v for k, v in _L0_ffn_all.items() if k in ('gate_weight', 'e_bias', 'w1', 'w2', 'w3', 'shared_gate', 'shared_up', 'shared_down')}
    del _L0_ffn_all
    return {'x': x, 'ctx_1024': ctx_1024, 'mask_SxS2_bk0': mask_SxS2_bk0, 'L0_attn_Wq': _L0_attn_in['Wq'], 'L0_attn_bq': _L0_attn_in['bq'], 'L0_attn_Wk': _L0_attn_in['Wk'], 'L0_attn_bk': _L0_attn_in['bk'], 'L0_attn_Wv': _L0_attn_in['Wv'], 'L0_attn_bv': _L0_attn_in['bv'], 'L0_attn_Wo': _L0_attn_in['Wo'], 'L0_attn_bo': _L0_attn_in['bo'], 'L0_attn_attn_scale': _L0_attn_in['attn_scale'], 'L0_xattn_wq': _L0_xattn_in['wq'], 'L0_xattn_bq': _L0_xattn_in['bq'], 'L0_xattn_wk': _L0_xattn_in['wk'], 'L0_xattn_bk': _L0_xattn_in['bk'], 'L0_xattn_wv': _L0_xattn_in['wv'], 'L0_xattn_bv': _L0_xattn_in['bv'], 'L0_xattn_wo': _L0_xattn_in['wo'], 'L0_xattn_bo': _L0_xattn_in['bo'], 'L0_ffn_gate_weight': _L0_ffn_in['gate_weight'], 'L0_ffn_e_bias': _L0_ffn_in['e_bias'], 'L0_ffn_w1': _L0_ffn_in['w1'], 'L0_ffn_w2': _L0_ffn_in['w2'], 'L0_ffn_w3': _L0_ffn_in['w3'], 'L0_ffn_shared_gate': _L0_ffn_in['shared_gate'], 'L0_ffn_shared_up': _L0_ffn_in['shared_up'], 'L0_ffn_shared_down': _L0_ffn_in['shared_down']}

def reference(x, ctx_1024, mask_SxS2_bk0, L0_attn_Wq, L0_attn_bq, L0_attn_Wk, L0_attn_bk, L0_attn_Wv, L0_attn_bv, L0_attn_Wo, L0_attn_bo, L0_attn_attn_scale, L0_xattn_wq, L0_xattn_bq, L0_xattn_wk, L0_xattn_bk, L0_xattn_wv, L0_xattn_bv, L0_xattn_wo, L0_xattn_bo, L0_ffn_gate_weight, L0_ffn_e_bias, L0_ffn_w1, L0_ffn_w2, L0_ffn_w3, L0_ffn_shared_gate, L0_ffn_shared_up, L0_ffn_shared_down):
    import jax
    import jax.numpy as jnp

    def _L0_attn_ref(x, Wq, bq, Wk, bk, Wv, bv, Wo, bo, attn_scale):
        import jax, jax.numpy as jnp
        import numpy as np
        CHUNK = 64
        HEADS = 16

        def _chunk_mask(T, cs):
            idx = jnp.arange(T)
            blk = idx // cs * cs
            qb = blk[:, None]
            kb = blk[None, :]
            masked = (qb >= kb) & (idx[None, :] - idx[:, None] - 2 * (kb - qb) >= 1)
            return masked
        B, T, C = x.shape
        H = HEADS
        D = C // H
        q = (x @ Wq.T + bq).reshape(B, T, H, D)
        k = (x @ Wk.T + bk).reshape(B, T, H, D)
        v = (x @ Wv.T + bv).reshape(B, T, H, D)
        scores = jnp.einsum('bqhd,bkhd->bhqk', q, k) * attn_scale[0]
        mask = _chunk_mask(T, CHUNK)
        scores = jnp.where(mask[None, None], -jnp.inf, scores)
        attn = jax.nn.softmax(scores, axis=-1)
        out = jnp.einsum('bhqk,bkhd->bqhd', attn, v).reshape(B, T, C)
        return out @ Wo.T + bo

    def _L0_xattn_ref(q, k, v, mask, wq, bq, wk, bk, wv, bv, wo, bo):
        import jax, jax.numpy as jnp
        import numpy as np
        D_MODEL = 512
        NUM_HEADS = 16
        D_K = D_MODEL // NUM_HEADS
        B, S = (4, 1024)
        b, s, d = q.shape

        def proj(x, w, bias):
            return (x @ w.T + bias).reshape(b, -1, NUM_HEADS, D_K).transpose(0, 2, 1, 3)
        qh = proj(q, wq, bq)
        kh = proj(k, wk, bk)
        vh = proj(v, wv, bv)
        scale = 1.0 / np.sqrt(D_K)
        scores = jnp.einsum('bhqd,bhkd->bhqk', qh, kh) * scale
        scores = jnp.where(mask[None, None, :, :], scores, -1000000000.0)
        probs = jax.nn.softmax(scores, axis=-1)
        out = jnp.einsum('bhqk,bhkd->bhqd', probs, vh)
        out = out.transpose(0, 2, 1, 3).reshape(b, s, d)
        return out @ wo.T + bo

    def _L0_ffn_ref(hidden_states, gate_weight, e_bias, w1, w2, w3, shared_gate, shared_up, shared_down):
        import jax, jax.numpy as jnp
        import numpy as np
        E, K, NG, TG = (64, 8, 8, 4)
        CAP = 512
        SCALE = 2.5

        def _route(x_flat, gate_weight, e_bias):
            T = x_flat.shape[0]
            logits = x_flat.astype(jnp.float32) @ gate_weight.astype(jnp.float32).T
            scores = jax.nn.sigmoid(logits)
            sfc = scores + e_bias[None, :]
            group_scores = jax.lax.top_k(sfc.reshape(T, NG, E // NG), 2)[0].sum(-1)
            _, gidx = jax.lax.top_k(group_scores, TG)
            gmask = jnp.zeros((T, NG), jnp.float32).at[jnp.arange(T)[:, None], gidx].set(1.0)
            smask = jnp.repeat(gmask, E // NG, axis=1)
            tmp = jnp.where(smask > 0, sfc, 0.0)
            _, topk_idx = jax.lax.top_k(tmp, K)
            topk_w = jnp.take_along_axis(scores, topk_idx, axis=1)
            topk_w = topk_w / (topk_w.sum(-1, keepdims=True) + 1e-20)
            return (topk_idx, topk_w * SCALE)

        def _moe_forward(hidden_states, gate_weight, e_bias, w1, w2, w3, shared_gate, shared_up, shared_down):
            B, S, H = hidden_states.shape
            T = B * S
            x = hidden_states.reshape(T, H)
            topk_idx, topk_w = _route(x, gate_weight, e_bias)
            Sk = T * K
            flat_e = topk_idx.reshape(-1)
            order = jnp.argsort(flat_e)
            sorted_e = flat_e[order]
            counts = jax.ops.segment_sum(jnp.ones((Sk,), jnp.int32), flat_e, num_segments=E)
            offsets = jnp.cumsum(counts) - counts
            pos = jnp.arange(Sk) - offsets[sorted_e]
            tok_sorted = x[order // K]
            xe = jnp.zeros((E, CAP, H), x.dtype).at[sorted_e, pos].set(tok_sorted, mode='drop')
            h = jax.nn.silu(jnp.einsum('ech,efh->ecf', xe, w1)) * jnp.einsum('ech,efh->ecf', xe, w3)
            ye = jnp.einsum('ecf,ehf->ech', h, w2)
            pos_c = jnp.minimum(pos, CAP - 1)
            vals = ye[sorted_e, pos_c]
            vals = jnp.where((pos < CAP)[:, None], vals, 0.0)
            flat_w = topk_w.reshape(-1)[order].astype(vals.dtype)
            flat_t = (jnp.arange(Sk) // K)[order]
            out = jax.ops.segment_sum(vals * flat_w[:, None], flat_t, num_segments=T)
            shared = jax.nn.silu(x @ shared_gate.T) * (x @ shared_up.T) @ shared_down.T
            return (out + shared).reshape(B, S, H)
        return _moe_forward(hidden_states, gate_weight, e_bias, w1, w2, w3, shared_gate, shared_up, shared_down)
    x = _layernorm(x + _L0_attn_ref(x, L0_attn_Wq, L0_attn_bq, L0_attn_Wk, L0_attn_bk, L0_attn_Wv, L0_attn_bv, L0_attn_Wo, L0_attn_bo, L0_attn_attn_scale), axis=-1)
    x = _layernorm(x + _L0_xattn_ref(x, ctx_1024, ctx_1024, mask_SxS2_bk0, L0_xattn_wq, L0_xattn_bq, L0_xattn_wk, L0_xattn_bk, L0_xattn_wv, L0_xattn_bv, L0_xattn_wo, L0_xattn_bo), axis=-1)
    x = _layernorm(x + _L0_ffn_ref(x, L0_ffn_gate_weight, L0_ffn_e_bias, L0_ffn_w1, L0_ffn_w2, L0_ffn_w3, L0_ffn_shared_gate, L0_ffn_shared_up, L0_ffn_shared_down), axis=-1)
    return x

_drawn_inputs = setup_inputs


def setup_inputs(seed=0):
    import zlib

    import numpy as np

    out = dict(_drawn_inputs(seed))
    spreads = {'L0_attn_bq': (0.0, 0.8),
     'L0_attn_bk': (0.0, 2.0),
     'L0_attn_bv': (0.0, 0.1),
     'L0_attn_bo': (0.0, 0.1),
     'L0_xattn_bq': (0.0, 0.308),
     'L0_xattn_bk': (0.0, 2.0),
     'L0_xattn_bv': (0.0, 0.1),
     'L0_xattn_bo': (0.0, 0.1),
     'L0_ffn_e_bias': (0.0, 0.878)}
    factors = {'L0_attn_Wq': 8.0,
     'L0_attn_Wk': 8.0,
     'L0_attn_Wv': 4.641,
     'L0_ffn_gate_weight': 4.119,
     'L0_ffn_w1': 3.538,
     'L0_ffn_w2': 3.44,
     'L0_ffn_w3': 3.439}
    for name, (base, spread) in spreads.items():
        noise = np.random.default_rng([zlib.crc32(name.encode()), seed]).standard_normal(out[name].shape)
        drawn = base * np.exp(spread * noise) if base else spread * noise
        out[name] = jnp.asarray(drawn.astype(out[name].dtype))
    for name, factor in factors.items():
        out[name] = (out[name] * factor).astype(out[name].dtype)
    return out
```

```python
from contextlib import ExitStack, contextmanager

import concourse.bass as bass
from concourse import mybir

F32 = mybir.dt.float32
F32R = mybir.dt.float32r
BF16 = mybir.dt.bfloat16
ALU = mybir.AluOpType
ACT = mybir.ActivationFunctionType
AX = mybir.AxisListType
P = 128

BATCH, SEQ, DM = 2, 2048, 512
HEADS, HD = 16, 32
KT = DM // P
GH = P // HD
NG = HEADS // GH
CH = 512
NC = SEQ // CH
NKB = SEQ // P
QB = CH // P
NEG = -1.0e30
LOWEST = -3.0e38


@contextmanager
def own_semaphores(nc, prefix):
    handles = []

    def sem(name):
        handles.append(nc.alloc_semaphore(name=prefix + name))
        return handles[-1]

    yield sem
    nc.all_engine_barrier()
    nc.clear_and_free_semaphores(handles)
    nc.all_engine_barrier()


def kept_semaphore(nc, sems, name):
    return sems.enter_context(nc.semaphore("kept_" + name))


def apart(eng, passed):
    eng.sem_inc(passed, 1)


def self_attention(nc, sems, xT, wqT, wkT, wvT, bq, bk, bv, scale, aT, ye):
    ITERS = BATCH * NG

    def chunk_q(c):
        return NC - 1 - c

    def kbs(c):
        return list(range(NKB - 1, QB * chunk_q(c) - 1, -1))

    def width(c, kb):
        j = kb - QB * chunk_q(c)
        return min((j + 1) * P, CH)

    def units(c):
        return [(kb, h) for kb in kbs(c) for h in range(GH)]

    def segments(c):
        return [(j, h, s) for j in range(QB) for h in range(GH) for s in range(c + 1)]

    NU = sum(len(units(c)) for c in range(NC))
    first_unit = [sum(len(units(b)) for b in range(c)) for c in range(NC)]
    def due(c, u):
        n, m = len(units(c)), len(segments(c + 1))
        return range(u * m // n, (u + 1) * m // n)
    order = []
    def plan_proj(c):
        order.extend([("k", c), ("q", c), ("v", c)])
    def plan_max(c):
        order.extend(("m", c, i) for i in range(len(segments(c))))
    plan_proj(0); plan_proj(1); plan_max(0); order.append(("s", 0)); plan_proj(2)
    plan_max(1); order.append(("s", 1)); plan_proj(3)
    plan_max(2); order.append(("s", 2)); plan_max(3); order.append(("s", 3))
    NWB = 3
    work = {key: i for i, key in enumerate(order)}
    NW = len(order)
    uses = [len(range(b, NW, NWB)) for b in range(NWB)]
    NSB = 3
    NPB = 4
    NDIST = 6 * GH * 16
    ZR = 2048
    ZB = ye.shape[0] * DM // (P * ZR * ITERS * NC)
    ye_blocks = ye.rearrange("(b p r) d -> b p (r d)", p=P, r=ZR // DM)

    with ExitStack() as ctx:
        def sb(name, shape, dt=F32):
            return ctx.enter_context(nc.sbuf_tensor("sa_" + name, shape, dt))

        sem = ctx.enter_context(own_semaphores(nc, "sa_"))
        passed = sem("passed")

        xt = sb("xt", [P, 2, KT, CH])
        wraw = sb("wraw", [P, 3, KT, P])
        wq = sb("wq", [P, KT, P])
        bias = sb("bias", [P, 2])
        bqs = sb("bqs", [P, 1])
        bvb = sb("bvb", [P, P])
        scl = sb("scl", [P, 1])
        hi = sb("hi", [P, 2, 2, CH], F32R)
        lo = sb("lo", [P, 2, 2, CH], F32R)
        qparts = sb("qparts", [P, GH, SEQ], F32R)
        kparts = sb("kparts", [P, GH, SEQ], F32R)
        values = sb("values", [P, NKB, GH, HD])
        ones = sb("ones", [P, HD])
        probs = sb("probs", [P, NPB, CH])
        pmax = sb("pmax", [P, QB * GH, NC])
        mrow = sb("mrow", [P, QB * GH])
        mhi = sb("mhi", [P, QB * GH], F32R)
        mcol = sb("mcol", [P, QB, GH, HD])
        rden = sb("rden", [P, CH])
        oT = sb("oT", [P, 2, CH])
        identb = sb("identb", [P, P], BF16)
        identf = sb("identf", [P, P])
        maskS = sb("maskS", [P, P], BF16)
        maskT = sb("maskT", [P, P], BF16)
        zeros = sb("zeros", [P, ZR])
        wbank = [ctx.enter_context(nc.psum_tensor(f"sa_w{i}", [P, CH], F32)) for i in range(NWB)]
        sbank = [ctx.enter_context(nc.psum_tensor(f"sa_s{i}", [P, CH], F32)) for i in range(NSB)]
        pvbank = [ctx.enter_context(nc.psum_tensor(f"sa_pv{i}", [P, CH], F32)) for i in range(2)]

        consts_set = sem("consts_set"); pool_step = sem("pool_step")
        w_loaded = sem("w_loaded"); w_used = sem("w_used"); bias_used = sem("bias_used"); scl_loaded = sem("scl_loaded")
        wq_scaled = sem("wq_scaled"); wdone = sem("wdone")
        x_loaded = [sem(f"x_loaded{i}") for i in range(2)]; x_used = sem("x_used")
        work_ready = sem("work_ready"); work_free = [sem(f"work_free{i}") for i in range(NWB)]
        hi_ready = sem("hi_ready"); lo_ready = sem("lo_ready"); stage_free = sem("stage_free")
        v_ready = sem("v_ready")
        ye_clear = sem("ye_clear")
        spread = [sem(f"spread{i}") for i in range(NC)]
        max_done = sem("max_done"); mstep = sem("mstep"); mcol_ready = sem("mcol_ready")
        shift_ready = sem("shift_ready"); mcol_free = sem("mcol_free")
        s_ready = sem("s_ready"); exp_done = sem("exp_done"); pv_done = sem("pv_done")
        pv_free = sem("pv_free"); rden_ready = sem("rden_ready"); o_ready = sem("o_ready")
        o_free = sem("o_free"); o_stored = kept_semaphore(nc, sems, "o_stored")
        block = ctx.enter_context(nc.Block())

        def batch_group(i):
            return i // NG, i % NG

        @block.sync
        def _(sp):
            sp.wait_ge(consts_set, 1)
            sp.dma_start(scl[:], scale.partition_broadcast(P)).then_inc(scl_loaded, 16)
            with sp.Fori(0, ITERS) as it:
                g = sp.snap(it % NG)
                b = sp.snap(it // NG)

                def load_x(c):
                    sp.wait_ge(x_used, it * NC + (c + 1))
                    apart(sp, passed)
                    sp.dma_start(xt[:, c % 2], xT[b, :, :, chunk_q(c) * CH:(chunk_q(c) + 1) * CH]).then_inc(x_loaded[c % 2], 16)

                def spread_parts(c):
                    cols = slice(chunk_q(c) * CH, (chunk_q(c) + 1) * CH)
                    sp.wait_ge(lo_ready, it * (2 * NC) + 2 * (c + 1))
                    for t, dst, parts in ((0, kparts, (hi, lo, hi)), (1, qparts, (hi, hi, lo))):
                        for h in range(GH):
                            for p, src in enumerate(parts):
                                sp.dma_start(dst[HD * p:HD * (p + 1), h, cols].bitcast(F32),
                                             src[HD * h:HD * (h + 1), t, c % 2, :].bitcast(F32)).then_inc(spread[c], 16)

                def clear_rows(c):
                    for z in range(ZB):
                        sp.dma_start(ye_blocks[it * (NC * ZB) + (c * ZB + z)], zeros[:]).then_inc(ye_clear, 16)

                sp.wait_ge(w_used, it + 1)
                sp.wait_ge(bias_used, it + 1)
                for n, w in enumerate((wqT, wkT, wvT)):
                    sp.dma_start(wraw[:, n], w[g]).then_inc(w_loaded, 16)
                for n, v in enumerate((bq, bk)):
                    sp.dma_start(bias[:, n:n + 1], v[g]).then_inc(w_loaded, 16)
                sp.dma_start(bvb[:], bv[g].partition_broadcast(P)).then_inc(w_loaded, 16)
                load_x(0)
                load_x(1)
                sp.wait_ge(pv_done, it * NU + NPB)
                spread_parts(0)
                clear_rows(0)
                load_x(2)
                spread_parts(1)
                clear_rows(1)
                load_x(3)
                spread_parts(2)
                clear_rows(2)
                spread_parts(3)
                clear_rows(3)

            sp.wait_ge(ye_clear, ITERS * NC * ZB * 16)

        @block.gpsimd
        def _(pool):
            n = 0
            def step(ins):
                nonlocal n
                n += 1
                ins.then_inc(pool_step, 1)
                pool.wait_ge(pool_step, n)
            for t in (identb, identf, maskS, maskT, mcol):
                step(pool.memset(t[:], 0.0))
            step(pool.memset(zeros[:], 0.0))
            step(pool.memset(pmax[:], LOWEST))
            step(pool.memset(ones[:], 1.0))
            for t in (qparts, kparts):
                step(pool.memset(t[3 * HD:P].bitcast(F32), 0.0))
            step(pool.memset(kparts[3 * HD:3 * HD + 2].bitcast(F32), 1.0))
            for t in (identb, identf):
                step(pool.affine_select(out=t[:], in_=t[:], compare_op=ALU.not_equal, fill=1.0, base=0,
                                        pattern=[[-1, P]], channel_multiplier=1))
            H = P // 2
            step(pool.memset(maskS[H:P, 0:H], NEG))
            step(pool.memset(maskT[0:H, H:P], NEG))
            for a in (0, H):
                v = maskS[a:a + H, a:a + H]
                step(pool.affine_select(out=v, in_=v, compare_op=ALU.is_ge, fill=NEG, base=0,
                                        pattern=[[-1, H]], channel_multiplier=1))
                v = maskT[a:a + H, a:a + H]
                step(pool.affine_select(out=v, in_=v, compare_op=ALU.is_ge, fill=NEG, base=0,
                                        pattern=[[1, H]], channel_multiplier=-1))
            pool.sem_inc(consts_set, 1)
            with pool.Fori(0, ITERS) as it:
                g = pool.snap(it % NG)
                b = pool.snap(it // NG)

                def spread_seen(c):
                    pool.wait_ge(spread[c], it * NDIST + NDIST)
                    pool.sem_inc(stage_free, 1)

                def store(c):
                    pool.wait_ge(o_ready, it * NC + (c + 1))
                    pool.dma_start(aT[g, :, ][:, bass.ds(b * SEQ + chunk_q(c) * CH, CH)], oT[:, c % 2]).then_inc(o_stored, 16)
                    pool.wait_ge(o_stored, it * (16 * NC) + 16 * (c + 1))
                    pool.sem_inc(o_free, 1)

                spread_seen(0)
                spread_seen(1)
                spread_seen(2)
                store(0)
                spread_seen(3)
                store(1)
                store(2)
                store(3)

        @block.tensor
        def _(pe):
            pe.sem_inc(pv_done, NPB)
            pe.sem_inc(x_used, 2)
            pe.sem_inc(w_used, 1)
            pe.wait_ge(consts_set, 1)
            with pe.Fori(0, ITERS) as it:
                def bank(key):
                    w = work[key]
                    b = w % NWB
                    pe.wait_ge(work_free[b], it * uses[b] + (w // NWB + 1))
                    return wbank[b]

                def proj(c):
                    pe.wait_ge(x_loaded[c % 2], it * 32 + 16 * (c // 2 + 1))
                    if c == 0:
                        pe.wait_ge(w_loaded, it * 96 + 96)
                        pe.wait_ge(wq_scaled, it * 2 + 2)
                    for name, w in (("k", wraw[:, 1]), ("q", wq)):
                        ps = bank((name, c))
                        for k in range(KT):
                            mm = nc.tensor.matmul(ps[:], w[:, k, :], xt[:, c % 2, k, :], start=k == 0, stop=k == KT - 1)
                        mm.then_inc(work_ready, 1)
                    ps = bank(("v", c))
                    for t in range(QB):
                        for k in range(KT):
                            mm = nc.tensor.matmul(ps[:, t * P:(t + 1) * P], xt[:, c % 2, k, t * P:(t + 1) * P],
                                                  wraw[:, 2, k, :], start=k == 0, stop=k == KT - 1)
                    mm.then_inc(work_ready, 1)
                    pe.wait_ge(work_ready, it * NW + (work[("v", c)] + 1))
                    pe.sem_inc(x_used, 1)
                    if c == NC - 1:
                        pe.sem_inc(w_used, 1)

                def max_segment(c, i):
                    j, h, s = segments(c)[i]
                    q0 = chunk_q(c) * CH + j * P
                    k0 = q0 + s * CH
                    w = min(CH, SEQ - k0)
                    ps = bank(("m", c, i))
                    mm = nc.tensor.matmul(ps[:, 0:w], qparts[0:3 * HD, h, q0:q0 + P], kparts[0:3 * HD, h, k0:k0 + w],
                                          start=True, stop=s != 0)
                    if s == 0:
                        mm = nc.tensor.matmul(ps[:, 0:P], identb[:], maskS[:], start=False, stop=True)
                    mm.then_inc(work_ready, 1)

                def shift(c):
                    ps = bank(("s", c))
                    pe.wait_ge(mcol_ready, it * NC + (c + 1))
                    for j in range(QB):
                        mm = nc.tensor.transpose(ps[:, j * P:(j + 1) * P], mcol[:, j].rearrange("p h d -> p (h d)"), identf[:])
                    mm.then_inc(work_ready, 1)

                def scores(c, u):
                    kb, h = units(c)[u]
                    n = first_unit[c] + u
                    w = width(c, kb)
                    q0 = chunk_q(c) * CH
                    if u == 0:
                        pe.wait_ge(shift_ready, it * (NC * GH) + GH * (c + 1))
                    pe.wait_ge(exp_done, it * NU + (n + 1))
                    ps = sbank[n % NSB]
                    diag = kb < QB * (chunk_q(c) + 1)
                    mm = nc.tensor.matmul(ps[:, 0:w], kparts[:, h, kb * P:(kb + 1) * P], qparts[:, h, q0:q0 + w],
                                          start=True, stop=not diag)
                    if diag:
                        mm = nc.tensor.matmul(ps[:, w - P:w], identb[:], maskT[:], start=False, stop=True)
                    mm.then_inc(s_ready, 1)

                def weighted(c, u):
                    kb, h = units(c)[u]
                    n = first_unit[c] + u
                    w = width(c, kb)
                    if u == 0:
                        pe.wait_ge(pv_free, it * NC + (c + 1))
                        pe.wait_ge(v_ready, it * NC + (c + 1))
                    pe.wait_ge(exp_done, it * NU + (NSB + n + 1))
                    a = HD * h
                    first, last = kb == NKB - 1, kb == QB * chunk_q(c)
                    nc.tensor.matmul(pvbank[0][a:a + HD, 0:w], values[:, kb, h, :], probs[:, n % NPB, 0:w],
                                     start=first, stop=last)
                    nc.tensor.matmul(pvbank[1][a:a + HD, 0:w], ones[:], probs[:, n % NPB, 0:w],
                                     start=first, stop=last).then_inc(pv_done, 1)

                def attend(c):
                    n = len(units(c))
                    LAG = 2
                    for u in range(n + LAG):
                        if u < n:
                            scores(c, u)
                            if c + 1 < NC:
                                for i in due(c, u):
                                    max_segment(c + 1, i)
                        if u >= LAG:
                            weighted(c, u - LAG)
                    if c + 1 < NC:
                        shift(c + 1)

                proj(0)
                proj(1)
                pe.wait_ge(spread[0], it * NDIST + NDIST)
                for i in range(len(segments(0))):
                    max_segment(0, i)
                shift(0)
                proj(2)
                pe.wait_ge(spread[1], it * NDIST + NDIST)
                attend(0)
                proj(3)
                pe.wait_ge(spread[2], it * NDIST + NDIST)
                attend(1)
                pe.wait_ge(spread[3], it * NDIST + NDIST)
                attend(2)
                attend(3)

        @block.scalar
        def _(act):
            act.sem_inc(exp_done, NSB)
            with act.Fori(0, ITERS) as it:
                def proj(c):
                    act.wait_ge(stage_free, it * NC + (c + 1))
                    for t, name in enumerate(("k", "q")):
                        w = work[(name, c)]
                        act.wait_ge(work_ready, it * NW + (w + 1))
                        if c == 0 and t == 1:
                            act.wait_ge(wq_scaled, it * 2 + 2)
                        nc.scalar.activation(hi[:, t, c % 2], wbank[w % NWB][:], ACT.Identity,
                                             bias=bias[:, 1:2] if t == 0 else bqs[:]).then_inc(hi_ready, 1)

                def shift(c):
                    w = work[("s", c)]
                    act.wait_ge(work_ready, it * NW + (w + 1))
                    cols = slice(chunk_q(c) * CH, (chunk_q(c) + 1) * CH)
                    for h in range(GH):
                        nc.scalar.copy(qparts[3 * HD:P, h, cols], wbank[w % NWB][HD * h:HD * (h + 1), :]).then_inc(shift_ready, 1)
                    act.wait_ge(shift_ready, it * (NC * GH) + GH * (c + 1))
                    act.sem_inc(work_free[w % NWB], 1)

                def attend(c):
                    for u, (kb, h) in enumerate(units(c)):
                        n = first_unit[c] + u
                        w = width(c, kb)
                        act.wait_ge(s_ready, it * NU + (n + 1))
                        act.wait_ge(pv_done, it * NU + (n + 1))
                        nc.scalar.activation(probs[:, n % NPB, 0:w], sbank[n % NSB][:, 0:w], ACT.Exp).then_inc(exp_done, 1)
                    if c + 1 < NC:
                        shift(c + 1)

                proj(0)
                proj(1)
                shift(0)
                proj(2)
                attend(0)
                proj(3)
                attend(1)
                attend(2)
                attend(3)

        @block.vector
        def _(dve):
            for b in range(NWB):
                dve.sem_inc(work_free[b], 1)
            dve.sem_inc(pv_free, 1)
            dve.sem_inc(bias_used, 1)
            dve.sem_inc(o_free, 2)
            dve.sem_inc(stage_free, 2)
            dve.wait_ge(consts_set, 1)
            dve.wait_ge(scl_loaded, 16)
            with dve.Fori(0, ITERS) as it:
                def proj(c):
                    if c == 0:
                        dve.wait_ge(w_loaded, it * 96 + 96)
                        dve.tensor_scalar(wq[:], wraw[:, 0], scl[:], None, ALU.mult).then_inc(wq_scaled, 1)
                        dve.tensor_scalar(bqs[:], bias[:, 0:1], scl[:], None, ALU.mult).then_inc(wq_scaled, 1)
                        dve.wait_ge(wq_scaled, it * 2 + 2)
                    for t, name in enumerate(("k", "q")):
                        w = work[(name, c)]
                        dve.wait_ge(hi_ready, it * (2 * NC) + (2 * c + t + 1))
                        dve.scalar_tensor_tensor(out=lo[:, t, c % 2], in0=wbank[w % NWB][:],
                                                 scalar=bias[:, 1:2] if t == 0 else bqs[:], in1=hi[:, t, c % 2],
                                                 op0=ALU.add, op1=ALU.subtract).then_inc(lo_ready, 1)
                        dve.wait_ge(lo_ready, it * (2 * NC) + (2 * c + t + 1))
                        dve.sem_inc(work_free[w % NWB], 1)
                    w = work[("v", c)]
                    dve.wait_ge(work_ready, it * NW + (w + 1))
                    if c == 0:
                        dve.wait_ge(pv_done, it * NU + NPB)
                    kb = chunk_q(c) * QB
                    dve.tensor_tensor(values[:, kb:kb + QB],
                                      wbank[w % NWB][:].rearrange("p (t h d) -> p t h d", t=QB, h=GH),
                                      bvb[:].rearrange("p (h d) -> p h d", h=GH).unsqueeze(1).broadcast_to([P, QB, GH, HD]),
                                      ALU.add).then_inc(v_ready, 1)
                    dve.wait_ge(v_ready, it * NC + (c + 1))
                    dve.sem_inc(work_free[w % NWB], 1)
                    if c == NC - 1:
                        dve.sem_inc(bias_used, 1)

                def max_segment(c, i):
                    j, h, s = segments(c)[i]
                    width_ = min(CH, SEQ - chunk_q(c) * CH - j * P - s * CH)
                    w = work[("m", c, i)]
                    dve.wait_ge(work_ready, it * NW + (w + 1))
                    dve.tensor_reduce(pmax[:, j * GH + h, s:s + 1], wbank[w % NWB][:, 0:width_], AX.X,
                                      ALU.max).then_inc(work_free[w % NWB], 1)

                def row_max(c):
                    last = work[("m", c, len(segments(c)) - 1)]
                    for w in range(last - NWB + 1, last + 1):
                        dve.wait_ge(work_free[w % NWB], it * uses[w % NWB] + (w // NWB + 2))
                    dve.tensor_reduce(mrow[:], pmax[:, :, 0:c + 1], AX.X, ALU.max).then_inc(mstep, 1)
                    dve.wait_ge(mstep, it * (3 * NC) + 3 * c + 1)
                    dve.tensor_scalar(mhi[:], mrow[:], -1.0, None, ALU.mult).then_inc(mstep, 1)
                    dve.wait_ge(mstep, it * (3 * NC) + 3 * c + 2)
                    hi32 = mhi[:].bitcast(F32).rearrange("p (j h) -> p j h", j=QB)
                    dve.tensor_copy(mcol[:, :, :, 0], hi32).then_inc(mstep, 1)
                    dve.scalar_tensor_tensor(out=mcol[:, :, :, 1], in0=mrow[:].rearrange("p (j h) -> p j h", j=QB),
                                             scalar=-1.0, in1=hi32, op0=ALU.mult, op1=ALU.subtract).then_inc(mcol_ready, 1)
                    dve.wait_ge(mstep, it * (3 * NC) + 3 * c + 3)

                def normalize(c):
                    dve.wait_ge(pv_done, it * NU + (NPB + first_unit[c] + len(units(c))))
                    dve.wait_ge(o_free, it * NC + (c + 1))
                    dve.reciprocal(rden[:], pvbank[1][:]).then_inc(rden_ready, 1)
                    dve.wait_ge(rden_ready, it * NC + (c + 1))
                    dve.tensor_tensor(oT[:, c % 2], pvbank[0][:], rden[:], ALU.mult).then_inc(o_ready, 1)
                    dve.wait_ge(o_ready, it * NC + (c + 1))
                    dve.sem_inc(pv_free, 1)

                proj(0)
                proj(1)
                for i in range(len(segments(0))):
                    max_segment(0, i)
                row_max(0)
                proj(2)
                for c in range(NC):
                    if c == 1:
                        proj(3)
                    if c + 1 < NC:
                        for i in range(len(segments(c + 1))):
                            max_segment(c + 1, i)
                        row_max(c + 1)
                    normalize(c)


I32 = mybir.dt.int32
U8 = mybir.dt.uint8
CTX = 154
NT = BATCH * SEQ // P
TPB = SEQ // P
EPS = 1.0e-5
E_, TOPK, NGRP, EG, TG, CAP, FF = 64, 8, 8, 8, 4, 512, 256
REST = CTX - P
LEAD = TAIL = 3


def each_tile(eng, body):
    for t in range(LEAD):
        body(t, t % 2)
    with eng.Fori(0, (NT - LEAD - TAIL) // 2) as i:
        for s in range(2):
            body(eng.snap(i * 2 + (LEAD + s)), (LEAD + s) % 2)
    for t in range(NT - TAIL, NT):
        body(t, t % 2)


def before_end(t, ahead=0):
    return not isinstance(t, int) or t + ahead < NT


def wait(eng, sem, value):
    if not isinstance(value, int) or value > 0:
        eng.wait_ge(sem, value)


def alternate(eng, sem, t, s, ahead=0):
    n = t // 2 if isinstance(t, int) else (t - s) // 2
    eng.wait_ge(sem[s], n * 16 * ahead + 16 * ahead)


def out_proj_norm(nc, sems, aT, x, woT, bo, x1, x1T):
    with ExitStack() as ctx:
        def sb(name, shape, dt=F32):
            return ctx.enter_context(nc.sbuf_tensor("on_" + name, shape, dt))

        sem = ctx.enter_context(own_semaphores(nc, "on_"))
        passed = sem("passed")
        wo = sb("wo", [P, KT, DM]); bob = sb("bob", [P, DM])
        identf = sb("identf", [P, P])
        at = sb("at", [P, 2, KT, P]); xr = sb("xr", [P, 2, DM]); xb = sb("xb", [P, 2, DM])
        y = sb("y", [P, 2, DM]); stats = sb("stats", [P, 2, 6]); mv = sb("mv", [P, 2, 2])
        rstd = sb("rstd", [P, 2]); std = sb("std", [P, 2]); eps = sb("eps", [P, 1])
        xn = sb("xn", [P, 2, DM]); xnT = sb("xnT", [P, 2, KT, P])
        ops = [ctx.enter_context(nc.psum_tensor(f"on_o{i}", [P, DM], F32)) for i in range(2)]
        tps = [ctx.enter_context(nc.psum_tensor(f"on_t{i}", [P, DM], F32)) for i in range(2)]
        w_in = sem("w_in"); ident_set = sem("ident_set"); a_in = [sem(f"a_in{i}") for i in range(2)]
        x_in = [sem(f"x_in{i}") for i in range(2)]
        o_done = sem("o_done"); xb_done = sem("xb_done"); y_done = sem("y_done"); nstep = sem("nstep"); mv_done = sem("mv_done"); std_done = sem("std_done"); rstd_done = sem("rstd_done")
        xn_done = sem("xn_done"); t_done = sem("t_done"); xnT_done = sem("xnT_done")
        xn_out = [sem(f"xn_out{i}") for i in range(2)]; xnT_out = [sem(f"xnT_out{i}") for i in range(2)]
        block = ctx.enter_context(nc.Block())

        def fetched(eng, sems, t, s):
            eng.wait_ge(sems[s], ((t - s) // 2) * 16 + 16)

        def stored(eng, sems, t, s):
            if isinstance(t, int) and t < 2:
                return
            eng.wait_ge(sems[s], ((t - s) // 2) * 16)

        @block.sync
        def _(sp):
            sp.dma_start(wo[:], woT).then_inc(w_in, 16)
            sp.dma_start(bob[:], bo.partition_broadcast(P)).then_inc(w_in, 16)
            def body(t, s):
                wait(sp, o_done, t - 1)
                sp.dma_start(at[:, s], aT.rearrange("k p t -> p k t")[:, :, bass.ds(t * P, P)]).then_inc(a_in[s], 16)
                wait(sp, xb_done, t - 1)
                sp.dma_start(xr[:, s], x[bass.ds(t * P, P), :]).then_inc(x_in[s], 16)
            each_tile(sp, body)

        @block.gpsimd
        def _(pool):
            pool.memset(identf[:], 0.0).then_inc(ident_set, 1)
            pool.memset(eps[:], EPS).then_inc(ident_set, 1)
            pool.wait_ge(ident_set, 2)
            pool.affine_select(out=identf[:], in_=identf[:], compare_op=ALU.not_equal, fill=1.0, base=0,
                               pattern=[[-1, P]], channel_multiplier=1).then_inc(ident_set, 1)
            pool.wait_ge(w_in, 32)
            def add(t, s):
                fetched(pool, x_in, t, s)
                wait(pool, y_done, t - 1)
                pool.tensor_tensor(xb[:, s], xr[:, s], bob[:], ALU.add).then_inc(xb_done, 1)

            def body(t, s):
                if isinstance(t, int) and t == 0:
                    add(t, s)
                if before_end(t, 1):
                    add(t + 1, 1 - s)
            each_tile(pool, body)

        @block.tensor
        def _(pe):
            pe.wait_ge(w_in, 32)
            pe.wait_ge(ident_set, 3)
            def product(t, s):
                fetched(pe, a_in, t, s)
                wait(pe, y_done, t - 1)
                for k in range(KT):
                    mm = nc.tensor.matmul(ops[s][:], at[:, s, k], wo[:, k], start=k == 0, stop=k == KT - 1)
                mm.then_inc(o_done, 1)
            def turn(t, s):
                pe.wait_ge(xn_done, t + 1)
                wait(pe, xnT_done, t - 1)
                for k in range(KT):
                    mm = nc.tensor.transpose(tps[s][:, k * P:(k + 1) * P], xn[:, s, k * P:(k + 1) * P], identf[:])
                mm.then_inc(t_done, 1)
            product(0, 0)
            def body(t, s):
                if before_end(t, 1):
                    product(t + 1, 1 - s)
                turn(t, s)
            each_tile(pe, body)

        @block.vector
        def _(dve):
            def body(t, s):
                dve.wait_ge(o_done, t + 1)
                dve.wait_ge(xb_done, t + 1)
                dve.tensor_tensor(y[:, s], ops[s][:], xb[:, s], ALU.add).then_inc(y_done, 1)
                dve.wait_ge(y_done, t + 1)
                dve.bn_stats(stats[:, s], y[:, s]).then_inc(nstep, 1)
                dve.wait_ge(nstep, t + 1)
                apart(dve, passed)
                dve.bn_aggr(mv[:, s], stats[:, s]).then_inc(mv_done, 1)
                dve.wait_ge(std_done, t + 1)
                dve.reciprocal(rstd[:, s:s + 1], std[:, s:s + 1]).then_inc(rstd_done, 1)
                dve.wait_ge(rstd_done, t + 1)
                stored(dve, xn_out, t, s)
                wait(dve, t_done, t - 1)
                dve.tensor_scalar(xn[:, s], y[:, s], mv[:, s, 0:1], rstd[:, s:s + 1], ALU.subtract, ALU.mult).then_inc(xn_done, 1)
            each_tile(dve, body)

        @block.scalar
        def _(act):
            act.wait_ge(ident_set, 3)
            def body(t, s):
                act.wait_ge(mv_done, t + 1)
                nc.scalar.activation(std[:, s:s + 1], mv[:, s, 1:2], ACT.Sqrt, bias=eps[:]).then_inc(std_done, 1)
                act.wait_ge(xn_done, t + 1)
                act.dma_start(x1[bass.ds(t * P, P), :], xn[:, s]).then_inc(xn_out[s], 16)
                act.wait_ge(t_done, t + 1)
                stored(act, xnT_out, t, s)
                nc.scalar.copy(xnT[:, s].rearrange("p k t -> p (k t)"), tps[s][:]).then_inc(xnT_done, 1)
                act.wait_ge(xnT_done, t + 1)
                act.dma_start(x1T[t], xnT[:, s]).then_inc(xnT_out[s], 16)
            each_tile(act, body)
            for s in range(2):
                act.wait_ge(xn_out[s], 16 * (NT // 2))
                act.wait_ge(xnT_out[s], 16 * (NT // 2))


def fetched(eng, sems, t, s, n=1):
    eng.wait_ge(sems[s], ((t - s) // 2) * (16 * n) + 16 * n)


def stored(eng, sems, t, s, n=1):
    if not isinstance(t, int) or t >= 2:
        eng.wait_ge(sems[s], ((t - s) // 2) * (16 * n))


def cross_attention(nc, sems, ctxT, mask, wqT, wkT, wvT, woT, bq, bk, bv, bo, x1, x1T, x2, x2T):
    HP = 2
    NSC = HEADS // HP
    KEEP, DROP = 3.0e38, -1.0e9
    with ExitStack() as ctx:
        def sb(name, shape, dt=F32):
            return ctx.enter_context(nc.sbuf_tensor("xa_" + name, shape, dt))

        sem = ctx.enter_context(own_semaphores(nc, "xa_"))
        passed = sem("passed")

        def ps(name):
            return ctx.enter_context(nc.psum_tensor("xa_" + name, [P, 512], F32))
        wq = sb("wq", [P, KT, DM]); wo = sb("wo", [P, KT, DM])
        kz = sb("kz", [P, BATCH, NG, GH, CTX])
        vmain = sb("vmain", [P, BATCH, DM]); vrest = sb("vrest", [P, BATCH, NG, P])
        bqb = sb("bqb", [P, NG]); bkb = sb("bkb", [P, NG]); bvb = sb("bvb", [P, DM]); bob = sb("bob", [P, DM])
        identf = sb("identf", [P, P]); eps = sb("eps", [P, 1])
        xT = sb("xT", [P, 2, KT, P]); xr = sb("xr", [P, 2, DM]); xb = sb("xb", [P, 2, DM])
        mk = sb("mk", [P, 2, CTX], U8); cap = sb("cap", [P, 2, CTX])
        qT = sb("qT", [P, 2, NG, P])
        sm = sb("sm", [P, 2, HEADS, CTX])
        nmax = sb("nmax", [P, 2, HEADS]); rsum = sb("rsum", [P, 2, HEADS]); rrec = sb("rrec", [P, 2, HEADS])
        pmain = sb("pmain", [P, HEADS, P]); prest = sb("prest", [P, HEADS * REST])
        ptm = sb("ptm", [P, HEADS, P]); ptr = sb("ptr", [P, NG, P])
        oT = sb("oT", [P, NG, P])
        y = sb("y", [P, 2, DM]); stats = sb("stats", [P, 2, 6]); mv = sb("mv", [P, 2, 2])
        std = sb("std", [P, 2]); rstd = sb("rstd", [P, 2])
        xn = sb("xn", [P, 2, DM]); xnT = sb("xnT", [P, 2, KT, P])
        qps = ps("qps"); sps = [ps(f"sps{i}") for i in range(2)]; tps = [ps(f"tps{i}") for i in range(2)]
        pvps = ps("pvps"); ops = ps("ops"); nps = ps("nps")

        w_in = sem("w_in"); consts = sem("consts"); pool_step = sem("pool_step")
        kw_in = sem("kw_in")
        kv_done = sem("kv_done"); kv_out = sem("kv_out"); vr_moved = sem("vr_moved"); vr_in = sem("vr_in")
        xT_in = [sem(f"xT_in{i}") for i in range(2)]; x_in = [sem(f"x_in{i}") for i in range(2)]
        q_done = sem("q_done"); qT_done = sem("qT_done"); s_done = sem("s_done"); sm_done = sem("sm_done")
        cap_done = sem("cap_done"); xb_done = sem("xb_done"); max_done = sem("max_done"); exp_done = sem("exp_done")
        rec_done = sem("rec_done"); pm_done = sem("pm_done"); pt_done = sem("pt_done")
        ptm_out = sem("ptm_out"); ptr_out = sem("ptr_out"); pv_done = sem("pv_done"); oT_done = sem("oT_done")
        o_done = sem("o_done"); y_done = sem("y_done"); nstep = sem("nstep"); mv_done = sem("mv_done")
        std_done = sem("std_done"); rstd_done = sem("rstd_done"); xn_done = sem("xn_done")
        t_done = sem("t_done"); xnT_done = sem("xnT_done")
        xn_out = [sem(f"xn_out{i}") for i in range(2)]; xnT_out = [sem(f"xnT_out{i}") for i in range(2)]

        wk = sm[:, 0].rearrange("p h c -> p (h c)")[:, 0:KT * DM].rearrange("p (k n) -> p k n", k=KT)
        wv = sm[:, 1].rearrange("p h c -> p (h c)")[:, 0:KT * DM].rearrange("p (k n) -> p k n", k=KT)
        cx = pmain[:].rearrange("p h k -> p (h k)")[:, 0:BATCH * KT * CTX].rearrange("p (b k c) -> p b k c", b=BATCH, k=KT)
        vtmp = y

        def batch_of(t):
            return t // TPB

        with nc.Block() as block:
            @block.sync
            def _(sp):
                sp.dma_start(wk, wkT).then_inc(kw_in, 16)
                sp.dma_start(wv, wvT).then_inc(kw_in, 16)
                for b in range(BATCH):
                    sp.dma_start(cx[:, b], ctxT[b]).then_inc(kw_in, 16)
                sp.dma_start(bkb[:], bk).then_inc(kw_in, 16)
                sp.dma_start(bvb[:], bv.partition_broadcast(P)).then_inc(kw_in, 16)
                sp.dma_start(bqb[:], bq).then_inc(w_in, 16)
                sp.dma_start(wq[:], wqT).then_inc(w_in, 16)
                sp.dma_start(wo[:], woT).then_inc(w_in, 16)
                sp.dma_start(bob[:], bo.partition_broadcast(P)).then_inc(w_in, 16)
                for b in range(BATCH):
                    sp.wait_ge(kv_out, NG * (b + 1) + b * 2 + 2)
                    sp.wait_ge(consts, 1)
                    for g in range(NG):
                        for h in range(GH):
                            sp.dma_start(vrest[REST * h:REST * (h + 1), b, g, HD * h:HD * (h + 1)],
                                         vtmp[0:REST, b, g * P + HD * h:g * P + HD * (h + 1)]).then_inc(vr_in, 16)
                sp.wait_ge(vr_in, BATCH * HEADS * 16)
                sp.wait_ge(w_in, 64)

            @block.gpsimd
            def _(pool):
                n = 0
                def step(ins):
                    nonlocal n
                    n += 1
                    ins.then_inc(pool_step, 1)
                    pool.wait_ge(pool_step, n)
                step(pool.memset(kz[:], 0.0))
                step(pool.memset(vrest[:], 0.0))
                step(pool.memset(eps[:], EPS))
                step(pool.memset(identf[:], 0.0))
                step(pool.affine_select(out=identf[:], in_=identf[:], compare_op=ALU.not_equal, fill=1.0, base=0,
                                        pattern=[[-1, P]], channel_multiplier=1))
                pool.sem_inc(consts, 1)

            @block.tensor
            def _(pe):
                pe.wait_ge(kw_in, 96)
                n = 0
                banks = [qps, sps[0], sps[1], tps[0], tps[1], pvps, ops, nps]
                for b in range(BATCH):
                    for g in range(NG):
                        if n >= 6:
                            pe.wait_ge(kv_out, n - 5)
                        for k in range(KT):
                            mm = nc.tensor.matmul(banks[n % 6][:, 0:CTX], wk[:, k, g * P:(g + 1) * P], cx[:, b, k],
                                                  start=k == 0, stop=k == KT - 1)
                        mm.then_inc(kv_done, 1)
                        n += 1
                    for m, (a, z) in enumerate(((0, P), (P, CTX))):
                        if n >= 6:
                            pe.wait_ge(kv_out, n - 5)
                        for k in range(KT):
                            mm = nc.tensor.matmul(banks[n % 6][0:z - a, :], cx[:, b, k, a:z], wv[:, k],
                                                  start=k == 0, stop=k == KT - 1)
                        mm.then_inc(kv_done, 1)
                        n += 1

            @block.vector
            def _(dve):
                banks = [qps, sps[0], sps[1], tps[0], tps[1], pvps, ops, nps]
                dve.wait_ge(kw_in, 96)
                dve.wait_ge(consts, 1)
                n = 0
                for b in range(BATCH):
                    for g in range(NG):
                        dve.wait_ge(kv_done, n + 1)
                        for h in range(GH):
                            r = slice(HD * h, HD * (h + 1))
                            op = dve.tensor_scalar(kz[r, b, g, h], banks[n % 6][r, 0:CTX], bkb[r, g:g + 1],
                                                   float(HD) ** -0.5, ALU.add, ALU.mult)
                        op.then_inc(kv_out, 1)
                        n += 1
                    dve.wait_ge(kv_done, n + 1)
                    dve.tensor_tensor(vmain[:, b], banks[n % 6][:], bvb[:], ALU.add).then_inc(kv_out, 1)
                    n += 1
                    dve.wait_ge(kv_done, n + 1)
                    dve.tensor_tensor(vtmp[0:REST, b], banks[n % 6][0:REST], bvb[0:REST], ALU.add).then_inc(kv_out, 1)
                    n += 1
                dve.wait_ge(kv_out, n)

        block = ctx.enter_context(nc.Block())

        @block.sync
        def _(sp):
            def body(t, s):
                wait(sp, q_done, t - 1)
                sp.dma_start(xT[:, s], x1T[t]).then_inc(xT_in[s], 16)
                wait(sp, xb_done, t - 1)
                sp.dma_start(xr[:, s], x1[bass.ds(t * P, P), :]).then_inc(x_in[s], 16)
                sp.dma_start(mk[:, s], mask[bass.ds((t % TPB) * P, P), :]).then_inc(x_in[s], 16)
            each_tile(sp, body)

        @block.gpsimd
        def _(pool):
            def caps(t, s):
                fetched(pool, x_in, t, s, 2)
                wait(pool, sm_done, (t - 1) * NSC)
                apart(pool, passed)
                pool.tensor_scalar(cap[:, s], mk[:, s], KEEP, DROP, ALU.mult, ALU.add).then_inc(cap_done, 1)

            def normalise(t, s):
                wait(pool, pt_done, t * 5)
                pool.wait_ge(exp_done, (t + 1) * HEADS)
                pool.wait_ge(rec_done, t + 1)
                pool.tensor_tensor(pmain[:], sm[:, s, :, 0:P], rrec[:, s].unsqueeze(2).broadcast_to([P, HEADS, P]),
                                   ALU.mult).then_inc(pm_done, 1)
                pool.tensor_tensor(prest[:].rearrange("p (h c) -> p h c", h=HEADS), sm[:, s, :, P:CTX],
                                   rrec[:, s].unsqueeze(2).broadcast_to([P, HEADS, REST]), ALU.mult).then_inc(pm_done, 1)

            def add_bias(t, s):
                fetched(pool, x_in, t, s, 2)
                wait(pool, y_done, t - 1)
                pool.tensor_tensor(xb[:, s], xr[:, s], bob[:], ALU.add).then_inc(xb_done, 1)

            def body(t, s):
                if before_end(t, 2):
                    caps(t + 2, s)
                if before_end(t, 1):
                    normalise(t + 1, 1 - s)
                    add_bias(t + 1, 1 - s)
            for t in range(2):
                caps(t, t)
            normalise(0, 0)
            add_bias(0, 0)
            each_tile(pool, body)

        @block.tensor
        def _(pe):
            def queries(t, s):
                fetched(pe, xT_in, t, s)
                wait(pe, qT_done, t)
                for g in range(NG):
                    for k in range(KT):
                        mm = nc.tensor.matmul(qps[:, g * P:(g + 1) * P], wq[:, k, g * P:(g + 1) * P], xT[:, s, k],
                                              start=k == 0, stop=k == KT - 1)
                mm.then_inc(q_done, 1)

            def scores(t, s, b):
                pe.wait_ge(qT_done, t + 1)
                for n in range(NSC):
                    wait(pe, sm_done, t * NSC + (n - 1))
                    g, h = n // 2, 2 * (n % 2)
                    nc.tensor.matmul(sps[n % 2][:, 0:HP * CTX], qT[:, s, g], kz[:, b, g, h:h + HP].rearrange("p h c -> p (h c)"),
                                     start=True, stop=True).then_inc(s_done, 1)

            def turn_probabilities(t):
                pe.wait_ge(pm_done, (t + 1) * 2)
                for n in range(4):
                    if n >= 2:
                        pe.wait_ge(ptm_out, t * 4 + (n - 1))
                    for h in range(GH):
                        mm = nc.tensor.transpose(tps[n % 2][:, h * P:(h + 1) * P], pmain[:, GH * n + h], identf[:])
                    mm.then_inc(pt_done, 1)
                wait(pe, xnT_done, t - 1)
                for g in range(NG):
                    mm = nc.tensor.transpose(nps[0:GH * REST, g * P:(g + 1) * P],
                                             prest[:, g * GH * REST:(g + 1) * GH * REST], identf[:])
                mm.then_inc(pt_done, 1)

            def mix(t, b):
                wait(pe, oT_done, t)
                pe.wait_ge(ptm_out, (t + 1) * 4)
                pe.wait_ge(ptr_out, t + 1)
                for g in range(NG):
                    for h in range(GH):
                        r = HD * h
                        nc.tensor.matmul(pvps[r:r + HD, g * P:(g + 1) * P], vmain[:, b, g * P + r:g * P + r + HD],
                                         ptm[:, GH * g + h], start=True, stop=False, skip_group_check=True)
                    mm = nc.tensor.matmul(pvps[:, g * P:(g + 1) * P], vrest[0:GH * REST, b, g], ptr[0:GH * REST, g],
                                          start=False, stop=True, skip_group_check=True)
                mm.then_inc(pv_done, 1)

            def project(t):
                pe.wait_ge(oT_done, t + 1)
                wait(pe, y_done, t)
                for k in range(KT):
                    mm = nc.tensor.matmul(ops[:], oT[:, k], wo[:, k], start=k == 0, stop=k == KT - 1)
                mm.then_inc(o_done, 1)

            def turn(t, s):
                pe.wait_ge(xn_done, t + 1)
                for k in range(KT):
                    mm = nc.tensor.transpose(nps[:, k * P:(k + 1) * P], xn[:, s, k * P:(k + 1) * P], identf[:])
                mm.then_inc(t_done, 1)

            for t in range(2):
                queries(t, t)
                scores(t, t, 0)

            def body(t, s, b, ahead):
                turn_probabilities(t)
                if before_end(t, 2):
                    queries(t + 2, s)
                mix(t, b)
                if before_end(t, 2):
                    scores(t + 2, s, ahead)
                if not isinstance(t, int) or t > 0:
                    turn(t - 1, 1 - s)
                project(t)
            each_tile_by_batch(pe, body)
            turn(NT - 1, (NT - 1) % 2)

        @block.vector
        def _(dve):
            def take_queries(t, s):
                dve.wait_ge(q_done, t + 1)
                wait(dve, s_done, (t - 1) * NSC)
                dve.tensor_tensor(qT[:, s], qps[:].rearrange("p (g t) -> p g t", g=NG),
                                  bqb[:].unsqueeze(2).broadcast_to([P, NG, P]), ALU.add).then_inc(qT_done, 1)

            def take_scores(t, s):
                dve.wait_ge(cap_done, t + 1)
                wait(dve, pm_done, (t - 1) * 2)
                for half in range(2):
                    for n in range(half * NSC // 2, (half + 1) * NSC // 2):
                        dve.wait_ge(s_done, t * NSC + (n + 1))
                        dve.tensor_tensor(sm[:, s, HP * n:HP * (n + 1)],
                                          sps[n % 2][:, 0:HP * CTX].rearrange("p (h c) -> p h c", h=HP),
                                          cap[:, s].unsqueeze(1).broadcast_to([P, HP, CTX]), ALU.min).then_inc(sm_done, 1)
                    r = slice(half * HEADS // 2, (half + 1) * HEADS // 2)
                    dve.wait_ge(sm_done, t * NSC + (half + 1) * NSC // 2)
                    dve.tensor_reduce(nmax[:, s, r], sm[:, s, r], AX.X, ALU.max, negate=True).then_inc(max_done, 1)

            def reciprocals(t, s):
                dve.wait_ge(exp_done, (t + 1) * HEADS)
                dve.reciprocal(rrec[:, s], rsum[:, s]).then_inc(rec_done, 1)

            def add_and_measure(t, s):
                dve.wait_ge(o_done, t + 1)
                dve.wait_ge(xb_done, t + 1)
                dve.tensor_tensor(y[:, s], ops[:], xb[:, s], ALU.add).then_inc(y_done, 1)
                dve.wait_ge(y_done, t + 1)
                dve.bn_stats(stats[:, s], y[:, s]).then_inc(nstep, 1)
                dve.wait_ge(nstep, t + 1)
                apart(dve, passed)
                dve.bn_aggr(mv[:, s], stats[:, s]).then_inc(mv_done, 1)

            def norm(t, s):
                dve.wait_ge(std_done, t + 1)
                dve.reciprocal(rstd[:, s:s + 1], std[:, s:s + 1]).then_inc(rstd_done, 1)
                dve.wait_ge(rstd_done, t + 1)
                stored(dve, xn_out, t, s)
                wait(dve, t_done, t - 1)
                dve.tensor_scalar(xn[:, s], y[:, s], mv[:, s, 0:1], rstd[:, s:s + 1], ALU.subtract, ALU.mult).then_inc(xn_done, 1)

            def body(t, s):
                later = not isinstance(t, int) or t > 0
                wait(dve, pv_done, t)
                for n in range(4):
                    dve.wait_ge(pt_done, t * 5 + (n + 1))
                    dve.tensor_copy(ptm[:, GH * n:GH * (n + 1)].rearrange("p h t -> p (h t)"), tps[n % 2][:]).then_inc(ptm_out, 1)
                    if n == 0 and before_end(t, 1):
                        reciprocals(t + 1, 1 - s)
                    if n == 1 and later:
                        add_and_measure(t - 1, 1 - s)
                dve.wait_ge(pt_done, t * 5 + 5)
                dve.tensor_copy(ptr[0:GH * REST].rearrange("p g t -> p (g t)"), nps[0:GH * REST, :]).then_inc(ptr_out, 1)
                if before_end(t, 2):
                    take_queries(t + 2, s)
                if later:
                    norm(t - 1, 1 - s)
                if before_end(t, 2):
                    take_scores(t + 2, s)
            for t in range(2):
                take_queries(t, t)
                take_scores(t, t)
            reciprocals(0, 0)
            each_tile(dve, body)
            add_and_measure(NT - 1, (NT - 1) % 2)
            norm(NT - 1, (NT - 1) % 2)

        @block.scalar
        def _(act):
            def exps(t, s):
                for half in range(2):
                    act.wait_ge(max_done, t * 2 + (half + 1))
                    for h in range(half * HEADS // 2, (half + 1) * HEADS // 2):
                        nc.scalar.activation(sm[:, s, h], sm[:, s, h], ACT.Exp, bias=nmax[:, s, h:h + 1],
                                             accum_out=rsum[:, s, h:h + 1]).then_inc(exp_done, 1)

            def deviation(t, s):
                act.wait_ge(mv_done, t + 1)
                nc.scalar.activation(std[:, s:s + 1], mv[:, s, 1:2], ACT.Sqrt, bias=eps[:]).then_inc(std_done, 1)
                act.wait_ge(xn_done, t + 1)
                act.dma_start(x2[bass.ds(t * P, P), :], xn[:, s]).then_inc(xn_out[s], 16)

            def store_turned(t, s):
                act.wait_ge(t_done, t + 1)
                stored(act, xnT_out, t, s)
                nc.scalar.copy(xnT[:, s].rearrange("p k t -> p (k t)"), nps[:]).then_inc(xnT_done, 1)
                act.wait_ge(xnT_done, t + 1)
                act.dma_start(x2T[t], xnT[:, s]).then_inc(xnT_out[s], 16)

            def body(t, s):
                later = not isinstance(t, int) or t > 0
                if later:
                    deviation(t - 1, 1 - s)
                act.wait_ge(pv_done, t + 1)
                wait(act, o_done, t)
                nc.scalar.copy(oT[:].rearrange("p g t -> p (g t)"), pvps[:]).then_inc(oT_done, 1)
                if before_end(t, 2):
                    exps(t + 2, s)
                if later:
                    store_turned(t - 1, 1 - s)
            for t in range(2):
                exps(t, t)
            each_tile(act, body)
            deviation(NT - 1, (NT - 1) % 2)
            store_turned(NT - 1, (NT - 1) % 2)
            for s in range(2):
                act.wait_ge(xn_out[s], 16 * (NT // 2))
                act.wait_ge(xnT_out[s], 16 * (NT // 2))


def each_tile_by_batch(eng, body):
    def straight(t):
        body(t, t % 2, t // TPB, min(t + 2, NT - 1) // TPB)
    t = 0
    for b in range(BATCH):
        first = b * TPB + (LEAD if b == 0 else 0)
        last = (b + 1) * TPB - (2 if b < BATCH - 1 else TAIL)
        first += (last - first) % 2
        while t < first:
            straight(t)
            t += 1
        with eng.Fori(0, (last - first) // 2) as i:
            for s in range(2):
                body(eng.snap(i * 2 + (first + s)), (first + s) % 2, b, b)
        t = last
    while t < NT:
        straight(t)
        t += 1


SLOTS = E_ * CAP
KEYS = 4096
assert KEYS >= BATCH * SEQ
UNIT = 256
UPE = CAP // UNIT
UNITS = E_ * UPE
SCALING = 2.5
LIM = 1.0e6


def route_and_shared(nc, sems, x2, x2T, gateT, ebias, sgT, suT, sdT, res, table, slots, weights, worklist):
    with ExitStack() as ctx:
        def sb(name, shape, dt=F32):
            return ctx.enter_context(nc.sbuf_tensor("rt_" + name, shape, dt))

        sem = ctx.enter_context(own_semaphores(nc, "rt_"))
        passed = sem("passed")

        def ps(name):
            return ctx.enter_context(nc.psum_tensor("rt_" + name, [P, 512], F32))
        gate = sb("gate", [P, KT, E_]); ebb = sb("ebb", [P, E_])
        wg = sb("wg", [P, KT, DM]); wu = sb("wu", [P, KT, DM]); wd = sb("wd", [P, KT, DM])
        tri = sb("tri", [P, P], BF16); ones = sb("ones", [P, P], BF16)
        eb1 = sb("eb1", [P, E_]); eb1i = sb("eb1i", [P, E_], I32)
        tokall = sb("tokall", [P, NT], I32); tok = sb("tok", [P, 2], I32)
        zero = sb("zero", [P, SLOTS // P], I32)
        xT = sb("xT", [P, 2, KT, P]); xr = sb("xr", [P, 2, DM])
        sg = sb("sg", [P, DM]); hg = sb("hg", [P, DM]); hT = sb("hT", [P, 2, KT, P])
        r = sb("r", [P, 2, DM])
        sc = sb("sc", [P, 2, E_]); sfc = sb("sfc", [P, E_]); srt = sb("srt", [P, NGRP, 8])
        gs = sb("gs", [P, 12]); gr = sb("gr", [P, 12]); g8 = sb("g8", [P, 8]); rl = sb("rl", [P, 8])
        gm = sb("gm", [P, NGRP]); tmp = sb("tmp", [P, E_]); tmp2 = sb("tmp2", [P, E_]); t8 = sb("t8", [P, 8])
        sel = sb("sel", [P, 2, E_]); selb = sb("selb", [P, 2, E_], BF16); cum = sb("cum", [P, 2, E_], BF16)
        wden = sb("wden", [P, 2, E_]); wsum = sb("wsum", [P, 2]); wrec = sb("wrec", [P, 1])
        kk = sb("kk", [P, 2, E_]); k8 = sb("k8", [P, 2, 8]); eq = sb("eq", [P, 8, E_]); oh = sb("oh", [P, 8, E_])
        w8 = sb("w8", [P, 2, 8]); ki = sb("ki", [P, 8], I32); pi = sb("pi", [P, 8], I32)
        ov = sb("ov", [P, 8], I32); kp = sb("kp", [P, 8]); sl = sb("sl", [P, 2, 8], I32)
        gps = ps("gps"); pps = ps("pps")
        gg = [ps(f"gg{i}") for i in range(2)]; uu = [ps(f"uu{i}") for i in range(2)]; dd = [ps(f"dd{i}") for i in range(2)]

        w_in = sem("w_in"); pool_step = sem("pool_step"); consts = sem("consts"); table_zero = sem("table_zero")
        xT_in = [sem(f"xT_in{i}") for i in range(2)]; x_in = [sem(f"x_in{i}") for i in range(2)]
        gate_done = sem("gate_done"); gu_done = sem("gu_done"); pos_done = sem("pos_done"); dn_done = sem("dn_done")
        sc_done = sem("sc_done"); sg_done = sem("sg_done"); hg_done = sem("hg_done"); hT_done = sem("hT_done")
        pick = sem("pick"); sel_done = sem("sel_done"); wden_done = sem("wden_done"); place = sem("place"); kk_done = sem("kk_done"); k8_done = sem("k8_done")
        eq_done = sem("eq_done"); oh_done = sem("oh_done"); w8_done = sem("w8_done"); slot_done = sem("slot_done"); cum_done = sem("cum_done")
        r_done = sem("r_done"); tok_done = sem("tok_done")
        r_out = [sem(f"r_out{i}") for i in range(2)]; sw_out = [sem(f"sw_out{i}") for i in range(2)]
        scat = [kept_semaphore(nc, sems, f"scat{i}") for i in range(2)]
        with nc.Block() as block:
            @block.sync
            def _(sp):
                for dst, src in ((gate, gateT), (wg, sgT), (wu, suT), (wd, sdT)):
                    sp.dma_start(dst[:], src).then_inc(w_in, 16)
                sp.dma_start(ebb[:], ebias.partition_broadcast(P)).then_inc(w_in, 16)
                sp.wait_ge(consts, 1)
                sp.dma_start(table.rearrange("(p n) o -> p (n o)", p=P), zero[:]).then_inc(table_zero, 16)

                def body(t, s):
                    wait(sp, gu_done, t - 1)
                    sp.dma_start(xT[:, s], x2T[t]).then_inc(xT_in[s], 16)
                    wait(sp, r_done, t - 1)
                    sp.dma_start(xr[:, s], x2[bass.ds(t * P, P), :]).then_inc(x_in[s], 16)
                each_tile(sp, body)

            @block.gpsimd
            def _(pool):
                n = 0
                def step(ins):
                    nonlocal n
                    n += 1
                    ins.then_inc(pool_step, 1)
                    pool.wait_ge(pool_step, n)
                step(pool.memset(tri[:], 0.0))
                step(pool.memset(ones[:], 1.0))
                step(pool.affine_select(out=tri[:], in_=tri[:], compare_op=ALU.is_ge, fill=1.0, base=0,
                                        pattern=[[-1, P]], channel_multiplier=1))
                step(pool.iota(eb1i[:], pattern=[[KEYS, E_]], base=1, channel_multiplier=0))
                step(pool.tensor_copy(eb1[:], eb1i[:]))
                step(pool.iota(tokall[:], pattern=[[P, NT]], base=0, channel_multiplier=1))
                step(pool.memset(zero[:], 0))
                step(pool.memset(cum[:, 0], 0.0))
                for v in (gs, rl):
                    step(pool.memset(v[:], LOWEST))
                pool.sem_inc(consts, 1)
                pool.wait_ge(table_zero, 16)

                def body(t, s):
                    pool.wait_ge(eq_done, t + 1)
                    wait(pool, w8_done, t)
                    pool.tensor_tensor(oh[:], eq[:], wden[:, s].unsqueeze(1).broadcast_to([P, 8, E_]), ALU.mult).then_inc(oh_done, 1)
                    if not isinstance(t, int) or t >= 2:
                        pool.wait_ge(scat[s], ((t - s) // 2) * 128)
                    pool.tensor_copy(tok[:, s:s + 1], tokall[:, bass.ds(t, 1)]).then_inc(tok_done, 1)
                    pool.wait_ge(tok_done, t + 1)
                    pool.wait_ge(slot_done, t + 1)
                    apart(pool, passed)
                    for k in range(TOPK):
                        pool.indirect_dma_start(out=table, out_offset=bass.IndirectOffsetOnAxis(ap=sl[:, s, k:k + 1], axis=0),
                                                in_=tok[:, s:s + 1], in_offset=None, bounds_check=SLOTS - 1,
                                                oob_is_err=False).then_inc(scat[s], 16)
                each_tile(pool, body)
                for s in range(2):
                    pool.wait_ge(scat[s], 128 * (NT // 2))

            @block.tensor
            def _(pe):
                pe.wait_ge(w_in, 80)
                pe.wait_ge(consts, 1)
                def up(t, s):
                    fetched(pe, xT_in, t, s)
                    wait(pe, sc_done, t)
                    for k in range(KT):
                        mm = nc.tensor.matmul(gps[:, 0:E_], xT[:, s, k], gate[:, k], start=k == 0, stop=k == KT - 1)
                    mm.then_inc(gate_done, 1)
                    wait(pe, hT_done, t - 1)
                    for w, o in ((wg, gg[s]), (wu, uu[s])):
                        for f in range(KT):
                            for k in range(KT):
                                mm = nc.tensor.matmul(o[:, f * P:(f + 1) * P], w[:, k, f * P:(f + 1) * P], xT[:, s, k],
                                                      start=k == 0, stop=k == KT - 1)
                    mm.then_inc(gu_done, 1)

                def rank(t, s):
                    pe.wait_ge(sel_done, t + 1)
                    if not isinstance(t, int) or t > 0:
                        pe.wait_ge(cum_done, t)
                    wait(pe, kk_done, t * 2)
                    nc.tensor.matmul(pps[:, 0:E_], tri[:], selb[:, s], start=True, stop=False)
                    nc.tensor.matmul(pps[:, 0:E_], ones[:], cum[:, s], start=False, stop=True).then_inc(pos_done, 1)

                def down(t, s):
                    pe.wait_ge(hT_done, t + 1)
                    wait(pe, r_done, t - 1)
                    for k in range(KT):
                        mm = nc.tensor.matmul(dd[s][:], hT[:, s, k], wd[:, k], start=k == 0, stop=k == KT - 1)
                    mm.then_inc(dn_done, 1)

                up(0, 0)
                def body(t, s):
                    if before_end(t, 1):
                        up(t + 1, 1 - s)
                    rank(t, s)
                    down(t, s)
                each_tile(pe, body)

            @block.scalar
            def _(act):
                def up(t, s):
                    act.wait_ge(gate_done, t + 1)
                    wait(act, w8_done, t - 1)
                    nc.scalar.activation(sc[:, s], gps[:, 0:E_], ACT.Sigmoid).then_inc(sc_done, 1)
                    act.wait_ge(gu_done, t + 1)
                    wait(act, hg_done, t)
                    nc.scalar.activation(sg[:], gg[s][:], ACT.Sigmoid).then_inc(sg_done, 1)

                up(0, 0)
                def body(t, s):
                    if before_end(t, 1):
                        up(t + 1, 1 - s)
                    act.wait_ge(w8_done, t + 1)
                    act.wait_ge(slot_done, t + 1)
                    act.dma_start(slots[t], sl[:, s]).then_inc(sw_out[s], 16)
                    act.dma_start(weights[t], w8[:, s]).then_inc(sw_out[s], 16)
                    act.wait_ge(r_done, t + 1)
                    act.dma_start(res[bass.ds(t * P, P), :], r[:, s]).then_inc(r_out[s], 16)
                each_tile(act, body)
                for s in range(2):
                    act.wait_ge(sw_out[s], 32 * (NT // 2))
                    act.wait_ge(r_out[s], 16 * (NT // 2))

            @block.vector
            def _(dve):
                dve.wait_ge(w_in, 80)
                dve.wait_ge(consts, 1)
                PICKS, PLACES = 18, 9

                def choose(t, s):
                    n = 0
                    def step(ins):
                        nonlocal n
                        n += 1
                        ins.then_inc(pick, 1)
                        dve.wait_ge(pick, t * PICKS + n)
                    dve.wait_ge(sc_done, t + 1)
                    step(dve.tensor_tensor(sfc[:], sc[:, s], ebb[:], ALU.add))
                    apart(dve, passed)
                    for g in range(NGRP):
                        ins = dve.max(srt[:, g], sfc[:, g * EG:(g + 1) * EG])
                        if g < NGRP - 1:
                            ins.then_inc(pick, 1)
                            n += 1
                    step(ins)
                    step(dve.tensor_tensor(gs[:, 0:NGRP], srt[:, :, 0], srt[:, :, 1], ALU.add))
                    apart(dve, passed)
                    step(dve.max(g8[:], gs[:, 0:NGRP]))
                    step(dve.tensor_copy(rl[:, 0:TG], g8[:, 0:TG]))
                    apart(dve, passed)
                    step(dve.match_replace(out=gr[:], in_to_replace=rl[:], in_values=gs[:], imm_value=-1.0e38))
                    step(dve.tensor_tensor(gm[:], gr[:, 0:NGRP], gs[:, 0:NGRP], ALU.not_equal))
                    step(dve.tensor_tensor(tmp[:].rearrange("p (g e) -> p g e", g=NGRP), sfc[:].rearrange("p (g e) -> p g e", g=NGRP),
                                           gm[:].unsqueeze(2).broadcast_to([P, NGRP, EG]), ALU.mult))
                    apart(dve, passed)
                    step(dve.max(t8[:], tmp[:]))
                    apart(dve, passed)
                    step(dve.match_replace(out=tmp2[:], in_to_replace=t8[:], in_values=tmp[:], imm_value=LOWEST))
                    wait(dve, pos_done, t - 1)
                    wait(dve, oh_done, t - 1)
                    dve.tensor_tensor(sel[:, s], tmp2[:], tmp[:], ALU.not_equal).then_inc(pick, 1)
                    dve.wait_ge(pick, t * PICKS + PICKS)
                    assert n + 1 == PICKS, n

                def choose_end(t, s):
                    dve.tensor_copy(selb[:, s], sel[:, s]).then_inc(sel_done, 1)
                    dve.tensor_tensor_reduce(out=wden[:, s], in0=sel[:, s], in1=sc[:, s], scale=1.0, scalar=0.0,
                                             op0=ALU.mult, op1=ALU.add, accum_out=wsum[:, s:s + 1]).then_inc(wden_done, 1)
                    dve.wait_ge(wden_done, t + 1)

                def act_part(t, s):
                    dve.wait_ge(sg_done, t + 1)
                    dve.tensor_tensor(hg[:], sg[:], gg[s][:], ALU.mult).then_inc(hg_done, 1)
                    dve.wait_ge(hg_done, t + 1)
                    wait(dve, dn_done, t - 1)
                    dve.tensor_tensor(hT[:, s].rearrange("p k t -> p (k t)"), hg[:], uu[s][:], ALU.mult).then_inc(hT_done, 1)

                def locate(t, s):
                    dve.wait_ge(pos_done, t + 1)
                    dve.wait_ge(sel_done, t + 1)
                    dve.tensor_tensor(cum[:, 1 - s], cum[:, s], selb[:, s], ALU.add).then_inc(cum_done, 1)
                    dve.tensor_tensor(kk[:, s], pps[:, 0:E_], eb1[:], ALU.add).then_inc(kk_done, 1)
                    dve.wait_ge(kk_done, t * 2 + 1)
                    dve.tensor_tensor(kk[:, s], kk[:, s], sel[:, s], ALU.mult).then_inc(kk_done, 1)
                    dve.wait_ge(kk_done, t * 2 + 2)
                    apart(dve, passed)
                    dve.max(k8[:, s], kk[:, s]).then_inc(k8_done, 1)
                    dve.wait_ge(k8_done, t + 1)
                    wait(dve, oh_done, t)
                    dve.tensor_tensor(eq[:], kk[:, s].unsqueeze(1).broadcast_to([P, 8, E_]),
                                      k8[:, s].unsqueeze(2).broadcast_to([P, 8, E_]), ALU.is_equal).then_inc(eq_done, 1)
                    n = 0
                    def step(ins):
                        nonlocal n
                        n += 1
                        ins.then_inc(place, 1)
                        dve.wait_ge(place, t * PLACES + n)
                    step(dve.tensor_scalar(ki[:], k8[:, s], -1.0, None, ALU.add))
                    step(dve.tensor_scalar(pi[:], ki[:], KEYS - 1, None, ALU.bitwise_and))
                    step(dve.tensor_scalar(ki[:], ki[:], 12, 9, ALU.logical_shift_right, ALU.logical_shift_left))
                    step(dve.tensor_scalar(ov[:], pi[:], float(CAP), LIM, ALU.is_ge, ALU.mult))
                    step(dve.tensor_scalar(kp[:], pi[:], float(CAP), SCALING, ALU.is_lt, ALU.mult))
                    apart(dve, passed)
                    step(dve.tensor_tensor(pi[:], pi[:], ki[:], ALU.add))
                    if not isinstance(t, int) or t >= 2:
                        dve.wait_ge(scat[s], ((t - s) // 2) * 128)
                        dve.wait_ge(sw_out[s], ((t - s) // 2) * 32)
                    apart(dve, passed)
                    dve.tensor_tensor(sl[:, s], pi[:], ov[:], ALU.add).then_inc(slot_done, 1)
                    step(dve.tensor_scalar(wrec[:], wsum[:, s:s + 1], 1.0e-20, None, ALU.add))
                    step(dve.reciprocal(wrec[:], wrec[:]))
                    dve.wait_ge(oh_done, t + 1)
                    step(dve.tensor_reduce(w8[:, s], oh[:], AX.X, ALU.add))
                    assert n == PLACES
                    dve.scalar_tensor_tensor(out=w8[:, s], in0=w8[:, s], scalar=wrec[:], in1=kp[:], op0=ALU.mult,
                                             op1=ALU.mult).then_inc(w8_done, 1)
                    dve.wait_ge(w8_done, t + 1)

                def finish(t, s):
                    dve.wait_ge(dn_done, t + 1)
                    fetched(dve, x_in, t, s)
                    stored(dve, r_out, t, s)
                    dve.tensor_tensor(r[:, s], dd[s][:], xr[:, s], ALU.add).then_inc(r_done, 1)

                choose(0, 0)
                choose_end(0, 0)
                act_part(0, 0)
                def body(t, s):
                    if before_end(t, 1):
                        choose(t + 1, 1 - s)
                        choose_end(t + 1, 1 - s)
                        act_part(t + 1, 1 - s)
                    locate(t, s)
                    finish(t, s)
                each_tile(dve, body)

        tot = sb("tot", [P, E_]); actv = sb("actv", [P, UNITS]); incl = sb("incl", [P, UNITS])
        iou = sb("iou", [P, UNITS], I32); iouf = sb("iouf", [P, UNITS]); row = sb("row", [P, 1], I32); rowf = sb("rowf", [P, 1])
        hot = sb("hot", [P, UNITS]); zrow = sb("zrow", [P, UNITS]); wl = sb("wl", [P, 2]); wli = sb("wli", [P, 2], I32)
        tot_done = sem("tot_done"); lstep = sem("lstep"); lconst = sem("lconst"); wl_out = sem("wl_out")
        with nc.Block() as block:
            @block.gpsimd
            def _(pool):
                pool.iota(iou[:], pattern=[[1, UNITS]], base=0, channel_multiplier=0).then_inc(lconst, 1)
                pool.iota(row[:], pattern=[[0, 1]], base=1, channel_multiplier=1).then_inc(lconst, 1)
                pool.memset(zrow[:], 0.0).then_inc(lconst, 1)

            @block.tensor
            def _(pe):
                nc.tensor.matmul(pps[:, 0:E_], ones[:], cum[:, NT % 2], start=True, stop=True).then_inc(tot_done, 1)

            @block.vector
            def _(dve):
                n = 0
                def step(ins):
                    nonlocal n
                    n += 1
                    ins.then_inc(lstep, 1)
                    dve.wait_ge(lstep, n)
                dve.wait_ge(lconst, 3)
                step(dve.tensor_copy(iouf[:], iou[:]))
                step(dve.tensor_copy(rowf[:], row[:]))
                dve.wait_ge(tot_done, 1)
                step(dve.tensor_copy(tot[:], pps[:, 0:E_]))
                av = actv[:].rearrange("p (e u) -> p e u", u=UPE)
                for u in range(UPE):
                    step(dve.tensor_scalar(av[:, :, u], tot[:], float(u * UNIT), None, ALU.is_gt))
                step(dve.tensor_tensor_scan(incl[:], actv[:], zrow[:], 0.0, ALU.add, ALU.add))
                step(dve.tensor_scalar(hot[:], incl[:], rowf[:], None, ALU.is_equal))
                step(dve.tensor_tensor(hot[:], hot[:], actv[:], ALU.mult))
                step(dve.tensor_tensor_reduce(out=hot[:], in0=hot[:], in1=iouf[:], scale=1.0, scalar=0.0, op0=ALU.mult,
                                              op1=ALU.add, accum_out=wl[:, 0:1]))
                step(dve.tensor_copy(wl[:, 1:2], incl[:, UNITS - 1:UNITS]))
                step(dve.tensor_copy(wli[:], wl[:]))
                dve.sem_inc(tot_done, 1)

            @block.sync
            def _(sp):
                sp.wait_ge(tot_done, 2)
                sp.dma_start(worklist, wli[:]).then_inc(wl_out, 16)
                sp.wait_ge(wl_out, 16)


def experts(nc, sems, x2, table, worklist, w1T, w3T, w2T, ye, spare):
    J = UNIT // P
    FT = FF // P
    with ExitStack() as ctx:
        def sb(name, shape, dt=F32):
            return ctx.enter_context(nc.sbuf_tensor("ex_" + name, shape, dt))

        sem = ctx.enter_context(own_semaphores(nc, "ex_"))
        passed = sem("passed")

        def ps(name):
            return ctx.enter_context(nc.psum_tensor("ex_" + name, [P, 512], F32))
        wl = sb("wl", [1, 2 * (UNITS + 1)], I32)
        identf = sb("identf", [P, P])
        w1 = sb("w1", [P, 2, KT, FF]); w3 = sb("w3", [P, 2, KT, FF]); w2 = sb("w2", [P, 2, FT, DM])
        idx = sb("idx", [P, 2, J], I32); xe = sb("xe", [P, 2, J, DM]); xeT = sb("xeT", [P, 2, KT, UNIT])
        sig = sb("sig", [P, FT * UNIT]); hg = sb("hg", [P, FT * UNIT]); hT = sb("hT", [P, 2, FT, UNIT])
        y = sb("y", [P, 2, J, DM]); zero = sb("zero", [P, 2])
        tps = [ps(f"tps{i}") for i in range(2)]; h1 = [ps(f"h1{i}") for i in range(1)]; h3 = [ps(f"h3{i}") for i in range(1)]
        yps = [ps(f"yps{i}") for i in range(2)]
        wl_in = sem("wl_in"); consts = sem("consts"); pool_step = sem("pool_step")
        w_in = [sem(f"w_in{i}") for i in range(2)]
        idx_in = kept_semaphore(nc, sems, "idx_in"); xe_in = [kept_semaphore(nc, sems, f"xe_in{i}") for i in range(2)]
        t_done = sem("t_done"); ta_out = sem("ta_out"); tv_out = sem("tv_out")
        g1_done = sem("g1_done"); g3_done = sem("g3_done"); g2_done = sem("g2_done")
        sig_done = sem("sig_done"); hg_done = sem("hg_done"); hT_done = sem("hT_done")
        ya_done = sem("ya_done"); yv_done = sem("yv_done"); y_out = [sem(f"y_out{i}") for i in range(2)]
        block = ctx.enter_context(nc.Block())
        table_u = table.rearrange("(u j p) o -> u p (j o)", j=J, p=P)
        ye_u = ye.rearrange("(u j p) d -> u p j d", j=J, p=P)

        def each_unit(eng, first, body):
            eng.wait_ge(wl_in, 16)
            n = eng.value_load(wl[0:1, 1:2], min_val=0, max_val=UNITS)
            first()
            with eng.Fori(0, UNITS // 2) as i:
                for s in range(2):
                    w = eng.snap(i * 2 + s)
                    with eng.If(w < n):
                        body(w, s)

        def turn_of(w, s):
            return (w - s) // 2 + 1

        @block.sync
        def _(sp):
            sp.wait_ge(consts, 1)
            sp.dma_start(wl[:, 0:2 * UNITS], worklist.rearrange("u c -> (u c)").unsqueeze(0)).then_inc(wl_in, 16)

            def body(w, s):
                e = sp.value_load(wl[0:1, bass.ds(w * 2, 1)], min_val=0, max_val=UNITS - 1) // UPE
                sp.wait_ge(g2_done, w + 1)
                for dst, src in ((w1, w1T), (w3, w3T), (w2, w2T)):
                    sp.dma_start(dst[:, s], src[e]).then_inc(w_in[s], 16)
            each_unit(sp, lambda: None, body)

        @block.gpsimd
        def _(pool):
            n = 0
            def step(ins):
                nonlocal n
                n += 1
                ins.then_inc(pool_step, 1)
                pool.wait_ge(pool_step, n)
            step(pool.memset(wl[:], 0))
            step(pool.memset(zero[:], 0.0))
            step(pool.memset(identf[:], 0.0))
            step(pool.affine_select(out=identf[:], in_=identf[:], compare_op=ALU.not_equal, fill=1.0, base=0,
                                    pattern=[[-1, P]], channel_multiplier=1))
            pool.sem_inc(consts, 1)

            def gather(w, s):
                unit = pool.value_load(wl[0:1, bass.ds(w * 2, 1)], min_val=0, max_val=UNITS - 1)
                pool.wait_ge(t_done, w + 1)
                pool.dma_start(idx[:, s], table_u[unit], allow_slow_non_contiguous=True).then_inc(idx_in, 16)
                pool.wait_ge(idx_in, w * 16 + 16)
                apart(pool, passed)
                for j in range(J):
                    pool.indirect_dma_start(out=xe[:, s, j], out_offset=None, in_=x2,
                                            in_offset=bass.IndirectOffsetOnAxis(ap=idx[:, s, j:j + 1], axis=0)).then_inc(xe_in[s], 16)
            each_unit(pool, lambda: gather(0, 0), lambda w, s: gather(w + 1, 1 - s))

        @block.tensor
        def _(pe):
            pe.sem_inc(t_done, 2)
            pe.sem_inc(g2_done, 2)
            pe.wait_ge(consts, 1)

            def turn(w, s):
                pe.wait_ge(xe_in[s], turn_of(w, s) * (16 * J))
                pe.wait_ge(ta_out, w + 1)
                pe.wait_ge(tv_out, w + 1)
                for j in range(J):
                    for k in range(KT):
                        mm = nc.tensor.transpose(tps[j][:, k * P:(k + 1) * P], xe[:, s, j, k * P:(k + 1) * P], identf[:])
                mm.then_inc(t_done, 1)

            def body(w, s):
                pe.wait_ge(ta_out, w + 2)
                pe.wait_ge(tv_out, w + 2)
                pe.wait_ge(w_in[s], turn_of(w, s) * 48)
                pe.wait_ge(hT_done, w + 1)
                for wt, bank, done in ((w1, h1, g1_done), (w3, h3, g3_done)):
                    for f in range(FT):
                        for k in range(KT):
                            mm = nc.tensor.matmul(bank[0][:, f * UNIT:(f + 1) * UNIT], wt[:, s, k, f * P:(f + 1) * P],
                                                  xeT[:, s, k], start=k == 0, stop=k == KT - 1)
                    mm.then_inc(done, 1)
                turn(w + 1, 1 - s)
                pe.wait_ge(hT_done, w + 2)
                pe.wait_ge(ya_done, w + 1)
                pe.wait_ge(yv_done, w + 1)
                for j in range(J):
                    for f in range(FT):
                        mm = nc.tensor.matmul(yps[j][:], hT[:, s, f, j * P:(j + 1) * P], w2[:, s, f],
                                              start=f == 0, stop=f == FT - 1)
                mm.then_inc(g2_done, 1)
            each_unit(pe, lambda: turn(0, 0), body)

        @block.scalar
        def _(act):
            act.sem_inc(ta_out, 1)
            act.sem_inc(sig_done, 1)
            act.sem_inc(ya_done, 1)
            act.wait_ge(consts, 1)
            for s in range(2):
                act.dma_start(spare[s], zero[:, s:s + 1]).then_inc(y_out[s], 16)

            def take(w, s):
                act.wait_ge(t_done, w + 3)
                act.wait_ge(g2_done, w + 1)
                nc.scalar.copy(xeT[:, s, :, 0:P], tps[0][:].rearrange("p (k t) -> p k t", k=KT)).then_inc(ta_out, 1)

            def body(w, s):
                act.wait_ge(g1_done, w + 1)
                act.wait_ge(hg_done, w + 1)
                nc.scalar.activation(sig[:], h1[0][:], ACT.Sigmoid).then_inc(sig_done, 1)
                take(w + 1, 1 - s)
                act.wait_ge(g2_done, w + 3)
                act.wait_ge(y_out[s], turn_of(w, s) * 16)
                nc.scalar.copy(y[:, s, 0], yps[0][:]).then_inc(ya_done, 1)
                unit = act.value_load(wl[0:1, bass.ds(w * 2, 1)], min_val=0, max_val=UNITS - 1)
                act.wait_ge(ya_done, w + 2)
                act.wait_ge(yv_done, w + 2)
                act.dma_start(ye_u[unit], y[:, s]).then_inc(y_out[s], 16)
            each_unit(act, lambda: take(0, 0), body)
            n = act.value_load(wl[0:1, 1:2], min_val=0, max_val=UNITS)
            act.wait_ge(y_out[0], (n + 1) // 2 * 16 + 16)
            act.wait_ge(y_out[1], n // 2 * 16 + 16)
            apart(act, passed)

        @block.vector
        def _(dve):
            dve.sem_inc(tv_out, 1)
            dve.sem_inc(hg_done, 1)
            dve.sem_inc(hT_done, 1)
            dve.sem_inc(yv_done, 1)

            def take(w, s):
                dve.wait_ge(t_done, w + 3)
                dve.wait_ge(g2_done, w + 1)
                dve.tensor_copy(xeT[:, s, :, P:UNIT], tps[1][:].rearrange("p (k t) -> p k t", k=KT)).then_inc(tv_out, 1)

            def body(w, s):
                dve.wait_ge(sig_done, w + 2)
                dve.tensor_tensor(hg[:], sig[:], h1[0][:], ALU.mult).then_inc(hg_done, 1)
                dve.wait_ge(g3_done, w + 1)
                dve.wait_ge(hg_done, w + 2)
                dve.tensor_tensor(hT[:, s].rearrange("p f t -> p (f t)"), hg[:], h3[0][:], ALU.mult).then_inc(hT_done, 1)
                take(w + 1, 1 - s)
                dve.wait_ge(g2_done, w + 3)
                dve.wait_ge(y_out[s], turn_of(w, s) * 16)
                dve.tensor_copy(y[:, s, 1], yps[1][:]).then_inc(yv_done, 1)
            each_unit(dve, lambda: take(0, 0), body)


def combine_norm(nc, sems, res, ye, slots, weights, out):
    with ExitStack() as ctx:
        def sb(name, shape, dt=F32):
            return ctx.enter_context(nc.sbuf_tensor("cn_" + name, shape, dt))

        sem = ctx.enter_context(own_semaphores(nc, "cn_"))
        passed = sem("passed")
        G = sb("G", [P, 2, TOPK, DM]); sl = sb("sl", [P, 2, TOPK], I32); wt = sb("wt", [P, 2, TOPK])
        acc = sb("acc", [P, 2, DM]); stats = sb("stats", [P, 2, 6]); mv = sb("mv", [P, 2, 2])
        std = sb("std", [P, 2]); rstd = sb("rstd", [P, 2]); eps = sb("eps", [P, 1]); o = sb("o", [P, 2, DM])
        consts = sem("consts"); s_in = [sem(f"s_in{i}") for i in range(2)]; r_in = [sem(f"r_in{i}") for i in range(2)]
        y_in = [kept_semaphore(nc, sems, f"y_in{i}") for i in range(2)]
        sums = sem("sums"); nstep = sem("nstep"); mv_done = sem("mv_done"); std_done = sem("std_done")
        rstd_done = sem("rstd_done"); o_done = sem("o_done"); o_out = [sem(f"o_out{i}") for i in range(2)]
        block = ctx.enter_context(nc.Block())

        @block.sync
        def _(sp):
            def body(t, s):
                wait(sp, sums, (t - 1) * TOPK)
                sp.dma_start(sl[:, s], slots[t]).then_inc(s_in[s], 16)
                sp.dma_start(wt[:, s], weights[t]).then_inc(r_in[s], 16)
                wait(sp, o_done, t - 1)
                sp.dma_start(acc[:, s], res[bass.ds(t * P, P), :]).then_inc(r_in[s], 16)
            each_tile(sp, body)

        @block.gpsimd
        def _(pool):
            pool.memset(G[:], 0.0).then_inc(consts, 1)
            pool.memset(eps[:], EPS).then_inc(consts, 1)
            pool.wait_ge(consts, 2)
            def body(t, s):
                fetched(pool, s_in, t, s)
                wait(pool, sums, (t - 1) * TOPK)
                apart(pool, passed)
                for k in range(TOPK):
                    pool.indirect_dma_start(out=G[:, s, k], out_offset=None, in_=ye,
                                            in_offset=bass.IndirectOffsetOnAxis(ap=sl[:, s, k:k + 1], axis=0),
                                            bounds_check=SLOTS - 1, oob_is_err=False).then_inc(y_in[s], 16)
            each_tile(pool, body)

        @block.scalar
        def _(act):
            act.wait_ge(consts, 2)
            def body(t, s):
                act.wait_ge(mv_done, t + 1)
                nc.scalar.activation(std[:, s:s + 1], mv[:, s, 1:2], ACT.Sqrt, bias=eps[:]).then_inc(std_done, 1)
                act.wait_ge(o_done, t + 1)
                act.dma_start(out[bass.ds(t * P, P), :], o[:, s]).then_inc(o_out[s], 16)
            each_tile(act, body)
            for s in range(2):
                act.wait_ge(o_out[s], 16 * (NT // 2))

        @block.vector
        def _(dve):
            def gather_sum(t, s):
                fetched(dve, r_in, t, s, 2)
                fetched(dve, y_in, t, s, TOPK)
                for k in range(TOPK):
                    dve.scalar_tensor_tensor(out=acc[:, s], in0=G[:, s, k], scalar=wt[:, s, k:k + 1], in1=acc[:, s],
                                             op0=ALU.mult, op1=ALU.add).then_inc(sums, 1)
                    dve.wait_ge(sums, t * TOPK + (k + 1))
                dve.bn_stats(stats[:, s], acc[:, s]).then_inc(nstep, 1)
                dve.wait_ge(nstep, t + 1)
                apart(dve, passed)
                dve.bn_aggr(mv[:, s], stats[:, s]).then_inc(mv_done, 1)
            gather_sum(0, 0)
            def body(t, s):
                if before_end(t, 1):
                    gather_sum(t + 1, 1 - s)
                dve.wait_ge(std_done, t + 1)
                dve.reciprocal(rstd[:, s:s + 1], std[:, s:s + 1]).then_inc(rstd_done, 1)
                dve.wait_ge(rstd_done, t + 1)
                stored(dve, o_out, t, s)
                dve.tensor_scalar(o[:, s], acc[:, s], mv[:, s, 0:1], rstd[:, s:s + 1], ALU.subtract, ALU.mult).then_inc(o_done, 1)
            each_tile(dve, body)


def program(nc, t):
    def scratch(name, shape, dt=F32):
        return nc.dram_tensor("scratch_" + name, shape, dt, kind="Internal").ap()

    tokens = BATCH * SEQ
    aT = scratch("attention_T", [NG, P, tokens])
    x1, x2, res = (scratch(n, [tokens, DM]) for n in ("x1", "x2", "residual"))
    x1T, x2T = (scratch(n, [NT, P, KT, P]) for n in ("x1_T", "x2_T"))
    table = scratch("token_of_slot", [SLOTS, 1], I32)
    slots = scratch("slots", [NT, P, TOPK], I32)
    weights = scratch("weights", [NT, P, TOPK])
    worklist = scratch("worklist", [UNITS, 2], I32)
    ye = scratch("expert_out", [SLOTS, DM])
    spare = scratch("spare", [2, P, 1])
    with ExitStack() as sems:
        self_attention(nc, sems, t["xT"], t["a_wq"], t["a_wk"], t["a_wv"], t["a_bq"], t["a_bk"], t["a_bv"], t["a_scale"],
                       aT, ye)
        out_proj_norm(nc, sems, aT, t["x"], t["a_wo"], t["a_bo"], x1, x1T)
        cross_attention(nc, sems, t["ctxT"], t["mask"], t["c_wq"], t["c_wk"], t["c_wv"], t["c_wo"], t["c_bq"], t["c_bk"],
                        t["c_bv"], t["c_bo"], x1, x1T, x2, x2T)
        route_and_shared(nc, sems, x2, x2T, t["gate"], t["e_bias"], t["s_gate"], t["s_up"], t["s_down"], res, table, slots,
                         weights, worklist)
        experts(nc, sems, x2, table, worklist, t["w1"], t["w3"], t["w2"], ye, spare)
        combine_norm(nc, sems, res, ye, slots, weights, t["out"])


def kernel(**inputs):
    import numpy as np
    import concourse.bacc as bacc
    from concourse.bass_utils import run_bass_kernel_spmd

    inputs = {k: np.asarray(v) for k, v in inputs.items()}

    def contract_rows(w):
        return w.T.reshape(-1, P, w.shape[0]).transpose(1, 0, 2)

    def by_group(w):
        return w.T.reshape(KT, P, NG, P).transpose(2, 1, 0, 3)

    def by_expert(w):
        e, o, i = w.shape
        return w.transpose(0, 2, 1).reshape(e, i // P, P, o).transpose(0, 2, 1, 3)

    a, c, f = "L0_attn_", "L0_xattn_", "L0_ffn_"
    x = inputs["x"]
    laid = {
        "x": x.reshape(BATCH * SEQ, DM),
        "xT": x.transpose(0, 2, 1).reshape(BATCH, KT, P, SEQ).transpose(0, 2, 1, 3),
        "ctxT": inputs["ctx_1024"].transpose(0, 2, 1).reshape(BATCH, KT, P, CTX).transpose(0, 2, 1, 3),
        "mask": inputs["mask_SxS2_bk0"],
        "a_wq": by_group(inputs[a + "Wq"]), "a_wk": by_group(inputs[a + "Wk"]), "a_wv": by_group(inputs[a + "Wv"]),
        "a_bq": inputs[a + "bq"].reshape(NG, P, 1), "a_bk": inputs[a + "bk"].reshape(NG, P, 1),
        "a_bv": inputs[a + "bv"].reshape(NG, P), "a_scale": inputs[a + "attn_scale"],
        "a_wo": contract_rows(inputs[a + "Wo"]), "a_bo": inputs[a + "bo"],
        "c_wq": contract_rows(inputs[c + "wq"]), "c_wk": contract_rows(inputs[c + "wk"]),
        "c_wv": contract_rows(inputs[c + "wv"]), "c_wo": contract_rows(inputs[c + "wo"]),
        "c_bq": inputs[c + "bq"].reshape(NG, P).T, "c_bk": inputs[c + "bk"].reshape(NG, P).T,
        "c_bv": inputs[c + "bv"], "c_bo": inputs[c + "bo"],
        "gate": contract_rows(inputs[f + "gate_weight"]), "e_bias": inputs[f + "e_bias"],
        "s_gate": contract_rows(inputs[f + "shared_gate"]), "s_up": contract_rows(inputs[f + "shared_up"]),
        "s_down": contract_rows(inputs[f + "shared_down"]),
        "w1": by_expert(inputs[f + "w1"]), "w3": by_expert(inputs[f + "w3"]), "w2": by_expert(inputs[f + "w2"]),
    }
    nc = bacc.Bacc("TRN2", target_bir_lowering=False, num_devices=1)
    arrays = {"in_" + k: np.ascontiguousarray(v) for k, v in laid.items()}
    t = {k: nc.dram_tensor("in_" + k, arrays["in_" + k].shape, mybir.dt.from_np(arrays["in_" + k].dtype),
                           kind="ExternalInput").ap() for k in laid}
    t["out"] = nc.dram_tensor("out", [BATCH * SEQ, DM], F32, kind="ExternalOutput").ap()
    program(nc, t)
    r = run_bass_kernel_spmd(nc, [arrays], core_ids=[0])
    return r.results[0]["out"].reshape(BATCH, SEQ, DM)
```

```python
from contextlib import ExitStack, contextmanager

import concourse.bass as bass
from concourse import mybir

F32 = mybir.dt.float32
F32R = mybir.dt.float32r
BF16 = mybir.dt.bfloat16
ALU = mybir.AluOpType
ACT = mybir.ActivationFunctionType
AX = mybir.AxisListType
P = 128

BATCH, SEQ, DM = 2, 2048, 512
HEADS, HD = 16, 32
KT = DM // P
GH = P // HD
NG = HEADS // GH
CH = 512
NC = SEQ // CH
NKB = SEQ // P
QB = CH // P
NEG = -1.0e30
LOWEST = -3.0e38


@contextmanager
def own_semaphores(nc, prefix):
    handles = []

    def sem(name):
        handles.append(nc.alloc_semaphore(name=prefix + name))
        return handles[-1]

    yield sem
    nc.all_engine_barrier()
    nc.clear_and_free_semaphores(handles)
    nc.all_engine_barrier()


def kept_semaphore(nc, sems, name):
    return sems.enter_context(nc.semaphore("kept_" + name))


def apart(eng, passed):
    eng.sem_inc(passed, 1)


def self_attention(nc, sems, xT, wqT, wkT, wvT, bq, bk, bv, scale, aT):
    ITERS = BATCH * NG

    def chunk_q(c):
        return NC - 1 - c

    def kbs(c):
        return list(range(NKB - 1, QB * chunk_q(c) - 1, -1))

    def width(c, kb):
        j = kb - QB * chunk_q(c)
        return min((j + 1) * P, CH)

    def units(c):
        return [(kb, h) for kb in kbs(c) for h in range(GH)]

    def segments(c):
        return [(j, h, s) for j in range(QB) for h in range(GH) for s in range(c + 1)]

    NU = sum(len(units(c)) for c in range(NC))
    first_unit = [sum(len(units(b)) for b in range(c)) for c in range(NC)]
    def due(c, u):
        n, m = len(units(c)), len(segments(c + 1))
        n -= GH
        return range(min(m, u * m // n), min(m, (u + 1) * m // n))
    order = []
    def plan_proj(c):
        order.extend([("k", c), ("q", c), ("v", c)])
    def plan_max(c):
        order.extend(("m", c, i) for i in range(len(segments(c))))
    CUTS = (0, 3, 9, len(segments(0)))
    plan_proj(0); plan_proj(1)
    for n, name in enumerate(("k", "q", "v")):
        order.extend(("m", 0, i) for i in range(CUTS[n], CUTS[n + 1]))
        order.append((name, 2))
    order.append(("s", 0))
    plan_max(1); order.append(("s", 1)); plan_proj(3)
    plan_max(2); order.append(("s", 2)); plan_max(3); order.append(("s", 3))
    NWB = 3
    work = {key: i for i, key in enumerate(order)}
    NW = len(order)
    uses = [len(range(b, NW, NWB)) for b in range(NWB)]
    NSB = 3
    NPB = 5
    NDIST = 3 * GH * 16

    with ExitStack() as ctx:
        def sb(name, shape, dt=F32):
            return ctx.enter_context(nc.sbuf_tensor("sa_" + name, shape, dt))

        sem = ctx.enter_context(own_semaphores(nc, "sa_"))
        passed = sem("passed")

        xt = sb("xt", [P, 2, KT, CH])
        wraw = sb("wraw", [P, 3, KT, P])
        wq = sb("wq", [P, KT, P])
        bias = sb("bias", [P, 2])
        bqs = sb("bqs", [P, 1])
        bvb = sb("bvb", [P, P])
        scl = sb("scl", [P, 1])
        halves = sb("halves", [P, 2, 4, CH], F32R)
        parts = sb("parts", [P, 2, GH, SEQ], F32R)
        kparts, qparts = parts[:, 0], parts[:, 1]
        values = sb("values", [P, NKB, GH, HD])
        ones = sb("ones", [P, HD])
        probs = sb("probs", [P, NPB, CH])
        pmax = sb("pmax", [P, QB * GH, NC])
        mrow = sb("mrow", [P, QB * GH])
        mhi = sb("mhi", [P, QB * GH], F32R)
        mcol = sb("mcol", [P, QB, GH, HD])
        raw = sb("raw", [P, CH]); den = sb("den", [P, CH])
        rden = sb("rden", [P, CH])
        oT = sb("oT", [P, 2, CH])
        identb = sb("identb", [P, P], BF16)
        identf = sb("identf", [P, P])
        maskS = sb("maskS", [P, P], BF16)
        maskT = sb("maskT", [P, P], BF16)
        wbank = [ctx.enter_context(nc.psum_tensor(f"sa_w{i}", [P, CH], F32)) for i in range(NWB)]
        sbank = [ctx.enter_context(nc.psum_tensor(f"sa_s{i}", [P, CH], F32)) for i in range(NSB)]
        pvbank = [ctx.enter_context(nc.psum_tensor(f"sa_pv{i}", [P, CH], F32)) for i in range(2)]

        consts_set = sem("consts_set"); pool_step = sem("pool_step")
        w_loaded = sem("w_loaded"); w_used = sem("w_used"); bias_used = sem("bias_used"); scl_loaded = sem("scl_loaded")
        wq_scaled = sem("wq_scaled")
        x_loaded = [sem(f"x_loaded{i}") for i in range(2)]; x_used = sem("x_used")
        work_ready = sem("work_ready"); work_free = [sem(f"work_free{i}") for i in range(NWB)]
        hi_ready = sem("hi_ready"); lo_ready = sem("lo_ready"); stage_free = sem("stage_free")
        v_ready = sem("v_ready")
        spread = [sem(f"spread{i}") for i in range(NC)]
        mstep = sem("mstep"); mcol_ready = sem("mcol_ready")
        shift_ready = sem("shift_ready")
        s_ready = sem("s_ready"); exp_done = sem("exp_done"); pv_done = sem("pv_done")
        pv_free = sem("pv_free"); den_free = sem("den_free"); raw_used = sem("raw_used"); rden_ready = sem("rden_ready"); o_ready = sem("o_ready")
        o_free = sem("o_free"); o_stored = kept_semaphore(nc, sems, "o_stored")
        block = ctx.enter_context(nc.Block())

        def batch_group(i):
            return i // NG, i % NG

        @block.sync
        def _(sp):
            sp.dma_start(scl[:], scale.partition_broadcast(P)).then_inc(scl_loaded, 16)

            def load_weights(g):
                for n, w in enumerate((wqT, wkT, wvT)):
                    sp.dma_start(wraw[:, n], w[g]).then_inc(w_loaded, 16)
                for n, v in enumerate((bq, bk)):
                    sp.dma_start(bias[:, n:n + 1], v[g]).then_inc(w_loaded, 16)
                sp.dma_start(bvb[:], bv[g].partition_broadcast(P)).then_inc(w_loaded, 16)

            load_weights(0)
            with sp.Fori(0, ITERS) as it:
                b = sp.snap(it // NG)
                next_g = sp.snap((it + 1) % NG)

                def load_x(c):
                    sp.wait_ge(x_used, it * NC + (c + 1))
                    apart(sp, passed)
                    sp.dma_start(xt[:, c % 2], xT[b, :, :, chunk_q(c) * CH:(chunk_q(c) + 1) * CH]).then_inc(x_loaded[c % 2], 16)

                def spread_parts(c):
                    cols = slice(chunk_q(c) * CH, (chunk_q(c) + 1) * CH)
                    sp.wait_ge(lo_ready, it * (2 * NC) + 2 * (c + 1))
                    for p, pair in enumerate((slice(0, 3, 2), slice(1, 3), slice(0, 4, 3))):
                        for h in range(GH):
                            sp.dma_start(parts[HD * p:HD * (p + 1), :, h, cols].bitcast(F32),
                                         halves[HD * h:HD * (h + 1), c % 2, pair, :].bitcast(F32)).then_inc(spread[c], 16)

                load_x(0)
                load_x(1)
                sp.wait_ge(pv_done, it * NU + NPB)
                spread_parts(0)
                load_x(2)
                spread_parts(1)
                load_x(3)
                spread_parts(2)
                spread_parts(3)
                sp.wait_ge(w_used, it + 1)
                sp.wait_ge(bias_used, it + 1)
                load_weights(next_g)

        @block.gpsimd
        def _(pool):
            n = 0
            def step(ins):
                nonlocal n
                n += 1
                ins.then_inc(pool_step, 1)
                pool.wait_ge(pool_step, n)
            for t in (identb, identf, maskS, maskT, mcol):
                step(pool.memset(t[:], 0.0))
            step(pool.memset(pmax[:], LOWEST))
            step(pool.memset(ones[:], 1.0))
            for t in (qparts, kparts):
                step(pool.memset(t[3 * HD:P].bitcast(F32), 0.0))
            step(pool.memset(kparts[3 * HD:3 * HD + 2].bitcast(F32), 1.0))
            for t in (identb, identf):
                step(pool.affine_select(out=t[:], in_=t[:], compare_op=ALU.not_equal, fill=1.0, base=0,
                                        pattern=[[-1, P]], channel_multiplier=1))
            H = P // 2
            step(pool.memset(maskS[H:P, 0:H], NEG))
            step(pool.memset(maskT[0:H, H:P], NEG))
            for a in (0, H):
                v = maskS[a:a + H, a:a + H]
                step(pool.affine_select(out=v, in_=v, compare_op=ALU.is_ge, fill=NEG, base=0,
                                        pattern=[[-1, H]], channel_multiplier=1))
                v = maskT[a:a + H, a:a + H]
                step(pool.affine_select(out=v, in_=v, compare_op=ALU.is_ge, fill=NEG, base=0,
                                        pattern=[[1, H]], channel_multiplier=-1))
            pool.sem_inc(consts_set, 1)
            with pool.Fori(0, ITERS) as it:
                g = pool.snap(it % NG)
                b = pool.snap(it // NG)

                def spread_seen(c):
                    pool.wait_ge(spread[c], it * NDIST + NDIST)
                    pool.sem_inc(stage_free, 1)

                def store(c):
                    pool.wait_ge(o_ready, it * NC + (c + 1))
                    pool.dma_start(aT[g, :, ][:, bass.ds(b * SEQ + chunk_q(c) * CH, CH)], oT[:, c % 2]).then_inc(o_stored, 16)
                    pool.wait_ge(o_stored, it * (16 * NC) + 16 * (c + 1))
                    pool.sem_inc(o_free, 1)

                spread_seen(0)
                spread_seen(1)
                spread_seen(2)
                store(0)
                spread_seen(3)
                store(1)
                store(2)
                store(3)

        @block.tensor
        def _(pe):
            pe.sem_inc(pv_done, NPB)
            pe.sem_inc(x_used, 2)
            with pe.Fori(0, ITERS) as it:
                def bank(key):
                    w = work[key]
                    b = w % NWB
                    pe.wait_ge(work_free[b], it * uses[b] + (w // NWB + 1))
                    return wbank[b]

                def keys_queries(c, name):
                    if name == "k":
                        pe.wait_ge(x_loaded[c % 2], it * 32 + 16 * (c // 2 + 1))
                        if c == 0:
                            pe.wait_ge(w_loaded, it * 96 + 96)
                            pe.wait_ge(wq_scaled, it * 2 + 2)
                    w = wraw[:, 1] if name == "k" else wq
                    ps = bank((name, c))
                    for k in range(KT):
                        mm = nc.tensor.matmul(ps[:], w[:, k, :], xt[:, c % 2, k, :], start=k == 0, stop=k == KT - 1)
                    mm.then_inc(work_ready, 1)

                def project_values(c):
                    ps = bank(("v", c))
                    for t in range(QB):
                        for k in range(KT):
                            mm = nc.tensor.matmul(ps[:, t * P:(t + 1) * P], xt[:, c % 2, k, t * P:(t + 1) * P],
                                                  wraw[:, 2, k, :], start=k == 0, stop=k == KT - 1)
                    mm.then_inc(work_ready, 1)
                    pe.wait_ge(work_ready, it * NW + (work[("v", c)] + 1))
                    pe.sem_inc(x_used, 1)
                    if c == NC - 1:
                        pe.sem_inc(w_used, 1)

                def proj(c):
                    keys_queries(c, "k")
                    keys_queries(c, "q")
                    project_values(c)

                def max_segment(c, i):
                    j, h, s = segments(c)[i]
                    q0 = chunk_q(c) * CH + j * P
                    k0 = q0 + s * CH
                    w = min(CH, SEQ - k0)
                    ps = bank(("m", c, i))
                    mm = nc.tensor.matmul(ps[:, 0:w], qparts[0:3 * HD, h, q0:q0 + P], kparts[0:3 * HD, h, k0:k0 + w],
                                          start=True, stop=s != 0)
                    if s == 0:
                        mm = nc.tensor.matmul(ps[:, 0:P], identb[:], maskS[:], start=False, stop=True)
                    mm.then_inc(work_ready, 1)

                def shift(c):
                    ps = bank(("s", c))
                    pe.wait_ge(mcol_ready, it * NC + (c + 1))
                    for j in range(QB):
                        mm = nc.tensor.transpose(ps[:, j * P:(j + 1) * P], mcol[:, j].rearrange("p h d -> p (h d)"), identf[:])
                    mm.then_inc(work_ready, 1)

                def scores(c, u):
                    kb, h = units(c)[u]
                    n = first_unit[c] + u
                    w = width(c, kb)
                    q0 = chunk_q(c) * CH
                    if u < GH:
                        pe.wait_ge(shift_ready, it * (NC * GH) + (GH * c + h + 1))
                    pe.wait_ge(exp_done, it * NU + (n + 1))
                    ps = sbank[n % NSB]
                    diag = kb < QB * (chunk_q(c) + 1)
                    mm = nc.tensor.matmul(ps[:, 0:w], kparts[:, h, kb * P:(kb + 1) * P], qparts[:, h, q0:q0 + w],
                                          start=True, stop=not diag)
                    if diag:
                        mm = nc.tensor.matmul(ps[:, w - P:w], identb[:], maskT[:], start=False, stop=True)
                    mm.then_inc(s_ready, 1)

                def weighted(c, u):
                    kb, h = units(c)[u]
                    n = first_unit[c] + u
                    w = width(c, kb)
                    if u == 0:
                        pe.wait_ge(pv_free, it * NC + (c + 1))
                        pe.wait_ge(den_free, it * NC + (c + 1))
                        pe.wait_ge(v_ready, it * NC + (c + 1))
                    pe.wait_ge(exp_done, it * NU + (NSB + n + 1))
                    a = HD * h
                    first, last = kb == NKB - 1, kb == QB * chunk_q(c)
                    nc.tensor.matmul(pvbank[0][a:a + HD, 0:w], values[:, kb, h, :], probs[:, n % NPB, 0:w],
                                     start=first, stop=last)
                    nc.tensor.matmul(pvbank[1][a:a + HD, 0:w], ones[:], probs[:, n % NPB, 0:w],
                                     start=first, stop=last).then_inc(pv_done, 1)

                def attend(c):
                    n = len(units(c))
                    LAG = 3
                    for u in range(n + LAG):
                        if u < n:
                            scores(c, u)
                            if c + 1 < NC:
                                for i in due(c, u):
                                    max_segment(c + 1, i)
                        if u >= LAG:
                            weighted(c, u - LAG)
                    if c + 1 < NC:
                        shift(c + 1)

                proj(0)
                proj(1)
                pe.wait_ge(consts_set, 1)
                pe.wait_ge(spread[0], it * NDIST + NDIST)
                for n, name in enumerate(("k", "q", "v")):
                    for i in range(CUTS[n], CUTS[n + 1]):
                        max_segment(0, i)
                    if name == "v":
                        project_values(2)
                    else:
                        keys_queries(2, name)
                shift(0)
                pe.wait_ge(spread[1], it * NDIST + NDIST)
                attend(0)
                proj(3)
                pe.wait_ge(spread[2], it * NDIST + NDIST)
                attend(1)
                pe.wait_ge(spread[3], it * NDIST + NDIST)
                attend(2)
                attend(3)

        @block.scalar
        def _(act):
            act.sem_inc(exp_done, NSB)
            act.sem_inc(pv_free, 1)
            with act.Fori(0, ITERS) as it:
                def proj(c):
                    act.wait_ge(stage_free, it * NC + (c + 1))
                    for t, name in enumerate(("k", "q")):
                        w = work[(name, c)]
                        act.wait_ge(work_ready, it * NW + (w + 1))
                        if c == 0 and t == 1:
                            act.wait_ge(wq_scaled, it * 2 + 2)
                        nc.scalar.activation(halves[:, c % 2, 2 * t], wbank[w % NWB][:], ACT.Identity,
                                             bias=bias[:, 1:2] if t == 0 else bqs[:]).then_inc(hi_ready, 1)

                def shift(c):
                    w = work[("s", c)]
                    act.wait_ge(work_ready, it * NW + (w + 1))
                    cols = slice(chunk_q(c) * CH, (chunk_q(c) + 1) * CH)
                    for h in range(GH):
                        nc.scalar.copy(qparts[3 * HD:P, h, cols], wbank[w % NWB][HD * h:HD * (h + 1), :]).then_inc(shift_ready, 1)
                    act.wait_ge(shift_ready, it * (NC * GH) + GH * (c + 1))
                    act.sem_inc(work_free[w % NWB], 1)

                def attend(c):
                    for u, (kb, h) in enumerate(units(c)):
                        n = first_unit[c] + u
                        w = width(c, kb)
                        act.wait_ge(s_ready, it * NU + (n + 1))
                        act.wait_ge(pv_done, it * NU + (n + 1))
                        nc.scalar.activation(probs[:, n % NPB, 0:w], sbank[n % NSB][:, 0:w], ACT.Exp).then_inc(exp_done, 1)
                    act.wait_ge(pv_done, it * NU + (NPB + first_unit[c] + len(units(c))))
                    act.wait_ge(raw_used, it * NC + (c + 1))
                    nc.scalar.copy(raw[:], pvbank[0][:]).then_inc(pv_free, 1)
                    if c + 1 < NC:
                        shift(c + 1)

                proj(0)
                proj(1)
                proj(2)
                shift(0)
                attend(0)
                proj(3)
                attend(1)
                attend(2)
                attend(3)

        @block.vector
        def _(dve):
            for b in range(NWB):
                dve.sem_inc(work_free[b], 1)
            dve.sem_inc(den_free, 1)
            dve.sem_inc(raw_used, 1)
            dve.sem_inc(o_free, 2)
            dve.sem_inc(stage_free, 2)
            dve.wait_ge(scl_loaded, 16)

            def scale_queries(i):
                dve.wait_ge(w_loaded, i * 96 + 96)
                dve.tensor_scalar(wq[:], wraw[:, 0], scl[:], None, ALU.mult).then_inc(wq_scaled, 1)
                dve.tensor_scalar(bqs[:], bias[:, 0:1], scl[:], None, ALU.mult).then_inc(wq_scaled, 1)

            scale_queries(0)
            with dve.Fori(0, ITERS) as it:
                def low_half(c, name):
                    t = ("k", "q").index(name)
                    w = work[(name, c)]
                    dve.wait_ge(hi_ready, it * (2 * NC) + (2 * c + t + 1))
                    dve.scalar_tensor_tensor(out=halves[:, c % 2, 2 * t + 1], in0=wbank[w % NWB][:],
                                             scalar=bias[:, 1:2] if t == 0 else bqs[:], in1=halves[:, c % 2, 2 * t],
                                             op0=ALU.add, op1=ALU.subtract).then_inc(lo_ready, 1)
                    dve.wait_ge(lo_ready, it * (2 * NC) + (2 * c + t + 1))
                    dve.sem_inc(work_free[w % NWB], 1)

                def take_values(c):
                    w = work[("v", c)]
                    dve.wait_ge(work_ready, it * NW + (w + 1))
                    if c == 0:
                        dve.wait_ge(pv_done, it * NU + NPB)
                    kb = chunk_q(c) * QB
                    dve.tensor_tensor(values[:, kb:kb + QB],
                                      wbank[w % NWB][:].rearrange("p (t h d) -> p t h d", t=QB, h=GH),
                                      bvb[:].rearrange("p (h d) -> p h d", h=GH).unsqueeze(1).broadcast_to([P, QB, GH, HD]),
                                      ALU.add).then_inc(v_ready, 1)
                    dve.wait_ge(v_ready, it * NC + (c + 1))
                    dve.sem_inc(work_free[w % NWB], 1)
                    if c == NC - 1:
                        dve.sem_inc(bias_used, 1)

                def proj(c):
                    low_half(c, "k")
                    low_half(c, "q")
                    take_values(c)

                def max_segment(c, i):
                    j, h, s = segments(c)[i]
                    width_ = min(CH, SEQ - chunk_q(c) * CH - j * P - s * CH)
                    w = work[("m", c, i)]
                    dve.wait_ge(work_ready, it * NW + (w + 1))
                    dve.tensor_reduce(pmax[:, j * GH + h, s:s + 1], wbank[w % NWB][:, 0:width_], AX.X,
                                      ALU.max).then_inc(work_free[w % NWB], 1)

                def row_max(c):
                    last = work[("m", c, len(segments(c)) - 1)]
                    for w in range(last - NWB + 1, last + 1):
                        dve.wait_ge(work_free[w % NWB], it * uses[w % NWB] + (w // NWB + 2))
                    dve.tensor_reduce(mrow[:], pmax[:, :, 0:c + 1], AX.X, ALU.max).then_inc(mstep, 1)
                    dve.wait_ge(mstep, it * (3 * NC) + 3 * c + 1)
                    dve.tensor_scalar(mhi[:], mrow[:], -1.0, None, ALU.mult).then_inc(mstep, 1)
                    dve.wait_ge(mstep, it * (3 * NC) + 3 * c + 2)
                    hi32 = mhi[:].bitcast(F32).rearrange("p (j h) -> p j h", j=QB)
                    dve.tensor_copy(mcol[:, :, :, 0], hi32).then_inc(mstep, 1)
                    dve.scalar_tensor_tensor(out=mcol[:, :, :, 1], in0=mrow[:].rearrange("p (j h) -> p j h", j=QB),
                                             scalar=-1.0, in1=hi32, op0=ALU.mult, op1=ALU.subtract).then_inc(mcol_ready, 1)
                    dve.wait_ge(mstep, it * (3 * NC) + 3 * c + 3)

                def normalize(c):
                    dve.wait_ge(pv_done, it * NU + (NPB + first_unit[c] + len(units(c))))
                    dve.wait_ge(o_free, it * NC + (c + 1))
                    dve.tensor_copy(den[:], pvbank[1][:]).then_inc(den_free, 1)
                    dve.wait_ge(den_free, it * NC + (c + 2))
                    dve.reciprocal(rden[:], den[:]).then_inc(rden_ready, 1)
                    dve.wait_ge(rden_ready, it * NC + (c + 1))
                    dve.wait_ge(pv_free, it * NC + (c + 2))
                    dve.tensor_tensor(oT[:, c % 2], raw[:], rden[:], ALU.mult).then_inc(o_ready, 1)
                    dve.wait_ge(o_ready, it * NC + (c + 1))
                    dve.sem_inc(raw_used, 1)

                dve.wait_ge(wq_scaled, it * 2 + 2)
                proj(0)
                proj(1)
                dve.wait_ge(consts_set, 1)
                for n, name in enumerate(("k", "q", "v")):
                    for i in range(CUTS[n], CUTS[n + 1]):
                        max_segment(0, i)
                    if name == "v":
                        row_max(0)
                        take_values(2)
                    else:
                        low_half(2, name)
                for c in range(NC):
                    if c == 1:
                        proj(3)
                    if c + 1 < NC:
                        for i in range(len(segments(c + 1))):
                            max_segment(c + 1, i)
                        row_max(c + 1)
                    else:
                        scale_queries(it + 1)
                    normalize(c)


I32 = mybir.dt.int32
U8 = mybir.dt.uint8
CTX = 154
NT = BATCH * SEQ // P
TPB = SEQ // P
EPS = 1.0e-5
E_, TOPK, NGRP, EG, TG, CAP, FF = 64, 8, 8, 8, 4, 512, 256
REST = CTX - P
LEAD = TAIL = 3


def each_tile(eng, body, count=NT):
    for t in range(LEAD):
        body(t, t % 2)
    with eng.Fori(0, (count - LEAD - TAIL) // 2) as i:
        for s in range(2):
            body(eng.snap(i * 2 + (LEAD + s)), (LEAD + s) % 2)
    for t in range(count - TAIL, count):
        body(t, t % 2)


def before_end(t, ahead=0):
    return not isinstance(t, int) or t + ahead < NT


def wait(eng, sem, value):
    if not isinstance(value, int) or value > 0:
        eng.wait_ge(sem, value)


def out_proj_norm(nc, sems, aT, x, woT, bo, x1, x1T):
    with ExitStack() as ctx:
        def sb(name, shape, dt=F32):
            return ctx.enter_context(nc.sbuf_tensor("on_" + name, shape, dt))

        sem = ctx.enter_context(own_semaphores(nc, "on_"))
        passed = sem("passed")
        wo = sb("wo", [P, KT, DM]); bob = sb("bob", [P, DM])
        identf = sb("identf", [P, P])
        at = sb("at", [P, 2, KT, P]); xr = sb("xr", [P, 2, DM]); xb = sb("xb", [P, 2, DM])
        y = sb("y", [P, 2, DM]); stats = sb("stats", [P, 2, 6]); mv = sb("mv", [P, 2, 2])
        rstd = sb("rstd", [P, 2]); std = sb("std", [P, 2]); eps = sb("eps", [P, 1])
        xn = sb("xn", [P, 2, DM]); xnT = sb("xnT", [P, 2, KT, P])
        ops = [ctx.enter_context(nc.psum_tensor(f"on_o{i}", [P, DM], F32)) for i in range(2)]
        tps = [ctx.enter_context(nc.psum_tensor(f"on_t{i}", [P, DM], F32)) for i in range(2)]
        w_in = sem("w_in"); ident_set = sem("ident_set"); a_in = [sem(f"a_in{i}") for i in range(2)]
        x_in = [sem(f"x_in{i}") for i in range(2)]
        o_done = sem("o_done"); xb_done = sem("xb_done"); y_done = sem("y_done"); nstep = sem("nstep"); mv_done = sem("mv_done"); std_done = sem("std_done"); rstd_done = sem("rstd_done")
        xn_done = sem("xn_done"); t_done = sem("t_done"); xnT_done = sem("xnT_done")
        xn_out = [sem(f"xn_out{i}") for i in range(2)]; xnT_out = [sem(f"xnT_out{i}") for i in range(2)]
        block = ctx.enter_context(nc.Block())

        def fetched(eng, sems, t, s):
            eng.wait_ge(sems[s], ((t - s) // 2) * 16 + 16)

        def stored(eng, sems, t, s):
            if isinstance(t, int) and t < 2:
                return
            eng.wait_ge(sems[s], ((t - s) // 2) * 16)

        @block.sync
        def _(sp):
            sp.dma_start(wo[:], woT).then_inc(w_in, 16)
            sp.dma_start(bob[:], bo.partition_broadcast(P)).then_inc(w_in, 16)
            def body(t, s):
                wait(sp, o_done, t - 1)
                sp.dma_start(at[:, s], aT.rearrange("k p t -> p k t")[:, :, bass.ds(t * P, P)]).then_inc(a_in[s], 16)
                wait(sp, xb_done, t - 1)
                sp.dma_start(xr[:, s], x[bass.ds(t * P, P), :]).then_inc(x_in[s], 16)
            each_tile(sp, body)

        @block.gpsimd
        def _(pool):
            pool.memset(identf[:], 0.0).then_inc(ident_set, 1)
            pool.memset(eps[:], EPS).then_inc(ident_set, 1)
            pool.wait_ge(ident_set, 2)
            pool.affine_select(out=identf[:], in_=identf[:], compare_op=ALU.not_equal, fill=1.0, base=0,
                               pattern=[[-1, P]], channel_multiplier=1).then_inc(ident_set, 1)
            pool.wait_ge(w_in, 32)
            def add(t, s):
                fetched(pool, x_in, t, s)
                wait(pool, y_done, t - 1)
                pool.tensor_tensor(xb[:, s], xr[:, s], bob[:], ALU.add).then_inc(xb_done, 1)

            def body(t, s):
                if isinstance(t, int) and t == 0:
                    add(t, s)
                if before_end(t, 1):
                    add(t + 1, 1 - s)
            each_tile(pool, body)

        @block.tensor
        def _(pe):
            pe.wait_ge(w_in, 32)
            pe.wait_ge(ident_set, 3)
            def product(t, s):
                fetched(pe, a_in, t, s)
                wait(pe, y_done, t - 1)
                for k in range(KT):
                    mm = nc.tensor.matmul(ops[s][:], at[:, s, k], wo[:, k], start=k == 0, stop=k == KT - 1)
                mm.then_inc(o_done, 1)
            def turn(t, s):
                pe.wait_ge(xn_done, t + 1)
                wait(pe, xnT_done, t - 1)
                for k in range(KT):
                    mm = nc.tensor.transpose(tps[s][:, k * P:(k + 1) * P], xn[:, s, k * P:(k + 1) * P], identf[:])
                mm.then_inc(t_done, 1)
            product(0, 0)
            def body(t, s):
                if before_end(t, 1):
                    product(t + 1, 1 - s)
                turn(t, s)
            each_tile(pe, body)

        @block.vector
        def _(dve):
            def body(t, s):
                dve.wait_ge(o_done, t + 1)
                dve.wait_ge(xb_done, t + 1)
                dve.tensor_tensor(y[:, s], ops[s][:], xb[:, s], ALU.add).then_inc(y_done, 1)
                dve.wait_ge(y_done, t + 1)
                dve.bn_stats(stats[:, s], y[:, s]).then_inc(nstep, 1)
                dve.wait_ge(nstep, t + 1)
                apart(dve, passed)
                dve.bn_aggr(mv[:, s], stats[:, s]).then_inc(mv_done, 1)
                dve.wait_ge(std_done, t + 1)
                dve.reciprocal(rstd[:, s:s + 1], std[:, s:s + 1]).then_inc(rstd_done, 1)
                dve.wait_ge(rstd_done, t + 1)
                stored(dve, xn_out, t, s)
                wait(dve, t_done, t - 1)
                dve.tensor_scalar(xn[:, s], y[:, s], mv[:, s, 0:1], rstd[:, s:s + 1], ALU.subtract, ALU.mult).then_inc(xn_done, 1)
            each_tile(dve, body)

        @block.scalar
        def _(act):
            act.wait_ge(ident_set, 3)
            def body(t, s):
                act.wait_ge(mv_done, t + 1)
                nc.scalar.activation(std[:, s:s + 1], mv[:, s, 1:2], ACT.Sqrt, bias=eps[:]).then_inc(std_done, 1)
                act.wait_ge(xn_done, t + 1)
                act.dma_start(x1[bass.ds(t * P, P), :], xn[:, s]).then_inc(xn_out[s], 16)
                act.wait_ge(t_done, t + 1)
                stored(act, xnT_out, t, s)
                nc.scalar.copy(xnT[:, s].rearrange("p k t -> p (k t)"), tps[s][:]).then_inc(xnT_done, 1)
                act.wait_ge(xnT_done, t + 1)
                act.dma_start(x1T[t], xnT[:, s]).then_inc(xnT_out[s], 16)
            each_tile(act, body)
            for s in range(2):
                act.wait_ge(xn_out[s], 16 * (NT // 2))
                act.wait_ge(xnT_out[s], 16 * (NT // 2))


def fetched(eng, sems, t, s, n=1):
    eng.wait_ge(sems[s], ((t - s) // 2) * (16 * n) + 16 * n)


def stored(eng, sems, t, s, n=1):
    if not isinstance(t, int) or t >= 2:
        eng.wait_ge(sems[s], ((t - s) // 2) * (16 * n))


def cross_attention(nc, sems, ctxT, mask, wqT, wkT, wvT, woT, bq, bk, bv, bo, x1, x1T, x2, x2T):
    HP = 2
    NSC = HEADS // HP
    KEEP, DROP = 3.0e38, -1.0e9
    with ExitStack() as ctx:
        def sb(name, shape, dt=F32):
            return ctx.enter_context(nc.sbuf_tensor("xa_" + name, shape, dt))

        sem = ctx.enter_context(own_semaphores(nc, "xa_"))
        passed = sem("passed")

        def ps(name):
            return ctx.enter_context(nc.psum_tensor("xa_" + name, [P, 512], F32))
        wq = sb("wq", [P, KT, DM]); wo = sb("wo", [P, KT, DM])
        kz = sb("kz", [P, BATCH, NG, GH, CTX])
        vmain = sb("vmain", [P, BATCH, DM]); vrest = sb("vrest", [P, BATCH, NG, P])
        bqb = sb("bqb", [P, NG]); bkb = sb("bkb", [P, NG]); bvb = sb("bvb", [P, DM]); bob = sb("bob", [P, DM])
        identf = sb("identf", [P, P]); eps = sb("eps", [P, 1])
        xT = sb("xT", [P, 2, KT, P]); xr = sb("xr", [P, 2, DM]); xb = sb("xb", [P, 2, DM])
        mk = sb("mk", [P, 2, CTX], U8); cap = sb("cap", [P, 2, CTX])
        qT = sb("qT", [P, 2, NG, P])
        sm = sb("sm", [P, 2, HEADS, CTX])
        nmax = sb("nmax", [P, 2, HEADS]); rsum = sb("rsum", [P, 2, HEADS]); rrec = sb("rrec", [P, 2, HEADS])
        pmain = sb("pmain", [P, HEADS, P]); prest = sb("prest", [P, HEADS * REST])
        ptm = sb("ptm", [P, HEADS, P]); ptr = sb("ptr", [P, NG, P])
        oT = sb("oT", [P, NG, P])
        y = sb("y", [P, 2, DM]); stats = sb("stats", [P, 2, 6]); mv = sb("mv", [P, 2, 2])
        std = sb("std", [P, 2]); rstd = sb("rstd", [P, 2])
        xn = sb("xn", [P, 2, DM]); xnT = sb("xnT", [P, 2, KT, P])
        qps = ps("qps"); sps = [ps(f"sps{i}") for i in range(2)]; tps = [ps(f"tps{i}") for i in range(2)]
        pvps = ps("pvps"); ops = ps("ops"); nps = ps("nps")

        w_in = sem("w_in"); consts = sem("consts"); pool_step = sem("pool_step")
        kw_in = sem("kw_in")
        kv_done = sem("kv_done"); kv_out = sem("kv_out"); vr_in = sem("vr_in")
        xT_in = [sem(f"xT_in{i}") for i in range(2)]; x_in = [sem(f"x_in{i}") for i in range(2)]
        q_done = sem("q_done"); qT_done = sem("qT_done"); s_done = sem("s_done"); sm_done = sem("sm_done")
        cap_done = sem("cap_done"); xb_done = sem("xb_done"); max_done = sem("max_done"); exp_done = sem("exp_done")
        rec_done = sem("rec_done"); pm_done = sem("pm_done"); pt_done = sem("pt_done")
        ptm_out = sem("ptm_out"); ptr_out = sem("ptr_out"); pv_done = sem("pv_done"); oT_done = sem("oT_done")
        o_done = sem("o_done"); y_done = sem("y_done"); nstep = sem("nstep"); mv_done = sem("mv_done")
        std_done = sem("std_done"); rstd_done = sem("rstd_done"); xn_done = sem("xn_done")
        t_done = sem("t_done"); xnT_done = sem("xnT_done")
        xn_out = [sem(f"xn_out{i}") for i in range(2)]; xnT_out = [sem(f"xnT_out{i}") for i in range(2)]

        wk = sm[:, 0].rearrange("p h c -> p (h c)")[:, 0:KT * DM].rearrange("p (k n) -> p k n", k=KT)
        wv = sm[:, 1].rearrange("p h c -> p (h c)")[:, 0:KT * DM].rearrange("p (k n) -> p k n", k=KT)
        cx = pmain[:].rearrange("p h k -> p (h k)")[:, 0:BATCH * KT * CTX].rearrange("p (b k c) -> p b k c", b=BATCH, k=KT)
        vtmp = y

        def batch_of(t):
            return t // TPB

        with nc.Block() as block:
            @block.sync
            def _(sp):
                sp.dma_start(wk, wkT).then_inc(kw_in, 16)
                sp.dma_start(wv, wvT).then_inc(kw_in, 16)
                for b in range(BATCH):
                    sp.dma_start(cx[:, b], ctxT[b]).then_inc(kw_in, 16)
                sp.dma_start(bkb[:], bk).then_inc(kw_in, 16)
                sp.dma_start(bvb[:], bv.partition_broadcast(P)).then_inc(kw_in, 16)
                sp.dma_start(bqb[:], bq).then_inc(w_in, 16)
                sp.dma_start(wq[:], wqT).then_inc(w_in, 16)
                sp.dma_start(wo[:], woT).then_inc(w_in, 16)
                sp.dma_start(bob[:], bo.partition_broadcast(P)).then_inc(w_in, 16)
                for b in range(BATCH):
                    sp.wait_ge(kv_out, NG * (b + 1) + b * 2 + 2)
                    sp.wait_ge(consts, 1)
                    by_group = vtmp[0:REST, b].rearrange("p (g c) -> p g c", g=NG)
                    for h in range(GH):
                        sp.dma_start(vrest[REST * h:REST * (h + 1), b, :, HD * h:HD * (h + 1)],
                                     by_group[:, :, HD * h:HD * (h + 1)]).then_inc(vr_in, 16)
                sp.wait_ge(vr_in, BATCH * GH * 16)
                sp.wait_ge(w_in, 64)

            @block.gpsimd
            def _(pool):
                n = 0
                def step(ins):
                    nonlocal n
                    n += 1
                    ins.then_inc(pool_step, 1)
                    pool.wait_ge(pool_step, n)
                step(pool.memset(kz[:], 0.0))
                step(pool.memset(vrest[:], 0.0))
                step(pool.memset(eps[:], EPS))
                step(pool.memset(identf[:], 0.0))
                step(pool.affine_select(out=identf[:], in_=identf[:], compare_op=ALU.not_equal, fill=1.0, base=0,
                                        pattern=[[-1, P]], channel_multiplier=1))
                pool.sem_inc(consts, 1)

            @block.tensor
            def _(pe):
                pe.wait_ge(kw_in, 96)
                n = 0
                banks = [qps, sps[0], sps[1], tps[0], tps[1], pvps, ops, nps]
                for b in range(BATCH):
                    for g in range(NG):
                        if n >= 6:
                            pe.wait_ge(kv_out, n - 5)
                        for k in range(KT):
                            mm = nc.tensor.matmul(banks[n % 6][:, 0:CTX], wk[:, k, g * P:(g + 1) * P], cx[:, b, k],
                                                  start=k == 0, stop=k == KT - 1)
                        mm.then_inc(kv_done, 1)
                        n += 1
                    for m, (a, z) in enumerate(((0, P), (P, CTX))):
                        if n >= 6:
                            pe.wait_ge(kv_out, n - 5)
                        for k in range(KT):
                            mm = nc.tensor.matmul(banks[n % 6][0:z - a, :], cx[:, b, k, a:z], wv[:, k],
                                                  start=k == 0, stop=k == KT - 1)
                        mm.then_inc(kv_done, 1)
                        n += 1

            @block.vector
            def _(dve):
                banks = [qps, sps[0], sps[1], tps[0], tps[1], pvps, ops, nps]
                dve.wait_ge(kw_in, 96)
                dve.wait_ge(consts, 1)
                n = 0
                for b in range(BATCH):
                    for g in range(NG):
                        dve.wait_ge(kv_done, n + 1)
                        for h in range(GH):
                            r = slice(HD * h, HD * (h + 1))
                            op = dve.tensor_scalar(kz[r, b, g, h], banks[n % 6][r, 0:CTX], bkb[r, g:g + 1],
                                                   float(HD) ** -0.5, ALU.add, ALU.mult)
                        op.then_inc(kv_out, 1)
                        n += 1
                    dve.wait_ge(kv_done, n + 1)
                    dve.tensor_tensor(vmain[:, b], banks[n % 6][:], bvb[:], ALU.add).then_inc(kv_out, 1)
                    n += 1
                    dve.wait_ge(kv_done, n + 1)
                    dve.tensor_tensor(vtmp[0:REST, b], banks[n % 6][0:REST], bvb[0:REST], ALU.add).then_inc(kv_out, 1)
                    n += 1
                dve.wait_ge(kv_out, n)

        block = ctx.enter_context(nc.Block())

        quad = [sps[0], sps[1], tps[0], tps[1]]

        @block.sync
        def _(sp):
            def body(t, s):
                wait(sp, q_done, t - 1)
                sp.dma_start(xT[:, s], x1T[t]).then_inc(xT_in[s], 16)
                wait(sp, xb_done, t - 1)
                sp.dma_start(xr[:, s], x1[bass.ds(t * P, P), :]).then_inc(x_in[s], 16)
                sp.dma_start(mk[:, s], mask[bass.ds((t % TPB) * P, P), :]).then_inc(x_in[s], 16)
            each_tile(sp, body)

        @block.gpsimd
        def _(pool):
            def caps(t, s):
                fetched(pool, x_in, t, s, 2)
                wait(pool, sm_done, (t - 1) * NSC)
                apart(pool, passed)
                pool.tensor_scalar(cap[:, s], mk[:, s], KEEP, DROP, ALU.mult, ALU.add).then_inc(cap_done, 1)

            def normalise(t, s):
                wait(pool, pt_done, t * 5)
                pool.wait_ge(exp_done, (t + 1) * HEADS)
                pool.wait_ge(rec_done, t + 1)
                pool.tensor_tensor(pmain[:], sm[:, s, :, 0:P], rrec[:, s].unsqueeze(2).broadcast_to([P, HEADS, P]),
                                   ALU.mult).then_inc(pm_done, 1)
                pool.tensor_tensor(prest[:].rearrange("p (h c) -> p h c", h=HEADS), sm[:, s, :, P:CTX],
                                   rrec[:, s].unsqueeze(2).broadcast_to([P, HEADS, REST]), ALU.mult).then_inc(pm_done, 1)

            def add_bias(t, s):
                fetched(pool, x_in, t, s, 2)
                wait(pool, y_done, t - 1)
                pool.tensor_tensor(xb[:, s], xr[:, s], bob[:], ALU.add).then_inc(xb_done, 1)

            def body(t, s):
                if before_end(t, 2):
                    caps(t + 2, s)
                if before_end(t, 1):
                    normalise(t + 1, 1 - s)
                    add_bias(t + 1, 1 - s)
            for t in range(2):
                caps(t, t)
            normalise(0, 0)
            add_bias(0, 0)
            each_tile(pool, body)

        @block.tensor
        def _(pe):
            def queries(t, s, between=lambda: None):
                fetched(pe, xT_in, t, s)
                wait(pe, qT_done, t)
                for g in range(NG):
                    if g == NG // 2:
                        between()
                    for k in range(KT):
                        mm = nc.tensor.matmul(qps[:, g * P:(g + 1) * P], wq[:, k, g * P:(g + 1) * P], xT[:, s, k],
                                              start=k == 0, stop=k == KT - 1)
                mm.then_inc(q_done, 1)

            def scores(t, s, b):
                pe.wait_ge(qT_done, t + 1)
                for n in range(NSC):
                    wait(pe, sm_done, t * NSC + (n - 3))
                    g, h = n // 2, 2 * (n % 2)
                    nc.tensor.matmul(quad[n % 4][:, 0:HP * CTX], qT[:, s, g], kz[:, b, g, h:h + HP].rearrange("p h c -> p (h c)"),
                                     start=True, stop=True).then_inc(s_done, 1)

            def turn_probabilities(t):
                pe.wait_ge(pm_done, (t + 1) * 2)
                pe.wait_ge(sm_done, (t + 2) * NSC if before_end(t, 1) else NT * NSC)
                for n in range(4):
                    for h in range(GH):
                        mm = nc.tensor.transpose(quad[n][:, h * P:(h + 1) * P], pmain[:, GH * n + h], identf[:])
                    mm.then_inc(pt_done, 1)

            def turn_rest(t):
                wait(pe, xnT_done, t - 1)
                for g in range(NG):
                    mm = nc.tensor.transpose(nps[0:GH * REST, g * P:(g + 1) * P],
                                             prest[:, g * GH * REST:(g + 1) * GH * REST], identf[:])
                mm.then_inc(pt_done, 1)

            def mix(t, b):
                wait(pe, oT_done, t)
                pe.wait_ge(ptm_out, (t + 1) * 4)
                pe.wait_ge(ptr_out, t + 1)
                for g in range(NG):
                    for h in range(GH):
                        r = HD * h
                        nc.tensor.matmul(pvps[r:r + HD, g * P:(g + 1) * P], vmain[:, b, g * P + r:g * P + r + HD],
                                         ptm[:, GH * g + h], start=True, stop=False, skip_group_check=True)
                    mm = nc.tensor.matmul(pvps[:, g * P:(g + 1) * P], vrest[0:GH * REST, b, g], ptr[0:GH * REST, g],
                                          start=False, stop=True, skip_group_check=True)
                mm.then_inc(pv_done, 1)

            def project(t):
                pe.wait_ge(oT_done, t + 1)
                wait(pe, y_done, t)
                for k in range(KT):
                    mm = nc.tensor.matmul(ops[:], oT[:, k], wo[:, k], start=k == 0, stop=k == KT - 1)
                mm.then_inc(o_done, 1)

            def turn(t, s):
                pe.wait_ge(xn_done, t + 1)
                for k in range(KT):
                    mm = nc.tensor.transpose(nps[:, k * P:(k + 1) * P], xn[:, s, k * P:(k + 1) * P], identf[:])
                mm.then_inc(t_done, 1)

            for t in range(2):
                queries(t, t)
                scores(t, t, 0)

            def body(t, s, b, ahead):
                turn_probabilities(t)
                if before_end(t, 2):
                    queries(t + 2, s, lambda: turn_rest(t))
                else:
                    turn_rest(t)
                mix(t, b)
                if before_end(t, 2):
                    scores(t + 2, s, ahead)
                if not isinstance(t, int) or t > 0:
                    turn(t - 1, 1 - s)
                project(t)
            each_tile_by_batch(pe, body)
            turn(NT - 1, (NT - 1) % 2)

        @block.vector
        def _(dve):
            def take_queries(t, s):
                dve.wait_ge(q_done, t + 1)
                wait(dve, s_done, (t - 1) * NSC)
                dve.tensor_tensor(qT[:, s], qps[:].rearrange("p (g t) -> p g t", g=NG),
                                  bqb[:].unsqueeze(2).broadcast_to([P, NG, P]), ALU.add).then_inc(qT_done, 1)

            def take_scores(t, s):
                dve.wait_ge(cap_done, t + 1)
                wait(dve, pm_done, (t - 1) * 2)
                for half in range(2):
                    for n in range(half * NSC // 2, (half + 1) * NSC // 2):
                        dve.wait_ge(s_done, t * NSC + (n + 1))
                        dve.tensor_tensor(sm[:, s, HP * n:HP * (n + 1)],
                                          quad[n % 4][:, 0:HP * CTX].rearrange("p (h c) -> p h c", h=HP),
                                          cap[:, s].unsqueeze(1).broadcast_to([P, HP, CTX]), ALU.min).then_inc(sm_done, 1)
                    r = slice(half * HEADS // 2, (half + 1) * HEADS // 2)
                    dve.wait_ge(sm_done, t * NSC + (half + 1) * NSC // 2)
                    dve.tensor_reduce(nmax[:, s, r], sm[:, s, r], AX.X, ALU.max, negate=True).then_inc(max_done, 1)

            def reciprocals(t, s):
                dve.wait_ge(exp_done, (t + 1) * HEADS)
                dve.reciprocal(rrec[:, s], rsum[:, s]).then_inc(rec_done, 1)

            def add_and_measure(t, s):
                dve.wait_ge(o_done, t + 1)
                dve.wait_ge(xb_done, t + 1)
                dve.tensor_tensor(y[:, s], ops[:], xb[:, s], ALU.add).then_inc(y_done, 1)
                dve.wait_ge(y_done, t + 1)
                dve.bn_stats(stats[:, s], y[:, s]).then_inc(nstep, 1)
                dve.wait_ge(nstep, t + 1)
                apart(dve, passed)
                dve.bn_aggr(mv[:, s], stats[:, s]).then_inc(mv_done, 1)

            def norm(t, s):
                dve.wait_ge(std_done, t + 1)
                dve.reciprocal(rstd[:, s:s + 1], std[:, s:s + 1]).then_inc(rstd_done, 1)
                dve.wait_ge(rstd_done, t + 1)
                stored(dve, xn_out, t, s)
                wait(dve, t_done, t - 1)
                dve.tensor_scalar(xn[:, s], y[:, s], mv[:, s, 0:1], rstd[:, s:s + 1], ALU.subtract, ALU.mult).then_inc(xn_done, 1)

            def body(t, s):
                later = not isinstance(t, int) or t > 0
                wait(dve, pv_done, t)
                for n in range(4):
                    dve.wait_ge(pt_done, t * 5 + (n + 1))
                    dve.tensor_copy(ptm[:, GH * n:GH * (n + 1)].rearrange("p h t -> p (h t)"), quad[n][:]).then_inc(ptm_out, 1)
                    if n == 2 and later:
                        add_and_measure(t - 1, 1 - s)
                    if n == 3 and before_end(t, 1):
                        reciprocals(t + 1, 1 - s)
                dve.wait_ge(pt_done, t * 5 + 5)
                dve.tensor_copy(ptr[0:GH * REST].rearrange("p g t -> p (g t)"), nps[0:GH * REST, :]).then_inc(ptr_out, 1)
                if before_end(t, 2):
                    take_queries(t + 2, s)
                if later:
                    norm(t - 1, 1 - s)
                if before_end(t, 2):
                    take_scores(t + 2, s)
            for t in range(2):
                take_queries(t, t)
                take_scores(t, t)
            reciprocals(0, 0)
            each_tile(dve, body)
            add_and_measure(NT - 1, (NT - 1) % 2)
            norm(NT - 1, (NT - 1) % 2)

        @block.scalar
        def _(act):
            def exps(t, s):
                for half in range(2):
                    act.wait_ge(max_done, t * 2 + (half + 1))
                    for h in range(half * HEADS // 2, (half + 1) * HEADS // 2):
                        nc.scalar.activation(sm[:, s, h], sm[:, s, h], ACT.Exp, bias=nmax[:, s, h:h + 1],
                                             accum_out=rsum[:, s, h:h + 1]).then_inc(exp_done, 1)

            def deviation(t, s):
                act.wait_ge(mv_done, t + 1)
                nc.scalar.activation(std[:, s:s + 1], mv[:, s, 1:2], ACT.Sqrt, bias=eps[:]).then_inc(std_done, 1)
                act.wait_ge(xn_done, t + 1)
                act.dma_start(x2[bass.ds(t * P, P), :], xn[:, s]).then_inc(xn_out[s], 16)

            def store_turned(t, s):
                act.wait_ge(t_done, t + 1)
                stored(act, xnT_out, t, s)
                nc.scalar.copy(xnT[:, s].rearrange("p k t -> p (k t)"), nps[:]).then_inc(xnT_done, 1)
                act.wait_ge(xnT_done, t + 1)
                act.dma_start(x2T[t], xnT[:, s]).then_inc(xnT_out[s], 16)

            def body(t, s):
                later = not isinstance(t, int) or t > 0
                if later:
                    deviation(t - 1, 1 - s)
                act.wait_ge(pv_done, t + 1)
                wait(act, o_done, t)
                nc.scalar.copy(oT[:].rearrange("p g t -> p (g t)"), pvps[:]).then_inc(oT_done, 1)
                if before_end(t, 2):
                    exps(t + 2, s)
                if later:
                    store_turned(t - 1, 1 - s)
            for t in range(2):
                exps(t, t)
            each_tile(act, body)
            deviation(NT - 1, (NT - 1) % 2)
            store_turned(NT - 1, (NT - 1) % 2)
            for s in range(2):
                act.wait_ge(xn_out[s], 16 * (NT // 2))
                act.wait_ge(xnT_out[s], 16 * (NT // 2))


def each_tile_by_batch(eng, body):
    def straight(t):
        body(t, t % 2, t // TPB, min(t + 2, NT - 1) // TPB)
    t = 0
    for b in range(BATCH):
        first = b * TPB + (LEAD if b == 0 else 0)
        last = (b + 1) * TPB - (2 if b < BATCH - 1 else TAIL)
        first += (last - first) % 2
        while t < first:
            straight(t)
            t += 1
        with eng.Fori(0, (last - first) // 2) as i:
            for s in range(2):
                body(eng.snap(i * 2 + (first + s)), (first + s) % 2, b, b)
        t = last
    while t < NT:
        straight(t)
        t += 1


SLOTS = E_ * CAP
KEYS = 4096
assert KEYS >= BATCH * SEQ
UNIT = 256
UPE = CAP // UNIT
UNITS = E_ * UPE
SCALING = 2.5
SPARE = UNIT
LIM = 1.0e6


def route_and_shared(nc, sems, x2, x2T, gateT, ebias, sgT, suT, sdT, res, table, worklist):
    with ExitStack() as ctx:
        def sb(name, shape, dt=F32):
            return ctx.enter_context(nc.sbuf_tensor("rt_" + name, shape, dt))

        sem = ctx.enter_context(own_semaphores(nc, "rt_"))
        passed = sem("passed")

        def ps(name):
            return ctx.enter_context(nc.psum_tensor("rt_" + name, [P, 512], F32))
        gate = sb("gate", [P, KT, E_]); ebb = sb("ebb", [P, E_])
        wg = sb("wg", [P, KT, DM]); wu = sb("wu", [P, KT, DM]); wd = sb("wd", [P, KT, DM])
        tri = sb("tri", [P, P], BF16); ones = sb("ones", [P, P], BF16)
        eb1 = sb("eb1", [P, E_]); eb1i = sb("eb1i", [P, E_], I32)
        tokall = sb("tokall", [P, NT], I32); entry = sb("entry", [P, 2, TOPK, 2])
        vacant = sb("vacant", [P, SLOTS // P, 2]); spare_row = sb("spare_row", [P, SLOTS // P], I32)
        zero = sb("zero", [P, SPARE // P * DM])
        xT = sb("xT", [P, 2, KT, P]); xr = sb("xr", [P, 2, DM])
        sg = sb("sg", [P, DM]); hg = sb("hg", [P, DM]); hT = sb("hT", [P, 2, KT, P])
        r = sb("r", [P, 2, DM])
        sc = sb("sc", [P, 2, E_]); sfc = sb("sfc", [P, E_]); srt = sb("srt", [P, NGRP, 8])
        gs = sb("gs", [P, 12]); gr = sb("gr", [P, 12]); g8 = sb("g8", [P, 8]); rl = sb("rl", [P, 8])
        gm = sb("gm", [P, NGRP]); tmp = sb("tmp", [P, E_]); tmp2 = sb("tmp2", [P, E_]); t8 = sb("t8", [P, 8])
        sel = sb("sel", [P, 2, E_]); selb = sb("selb", [P, 2, E_], BF16); cum = sb("cum", [P, 2, E_], BF16)
        wden = sb("wden", [P, 2, E_]); wsum = sb("wsum", [P, 2]); wrec = sb("wrec", [P, 1])
        kk = sb("kk", [P, 2, E_]); k8 = sb("k8", [P, 2, 8]); eq = sb("eq", [P, 8, E_]); oh = sb("oh", [P, 8, E_])
        w8 = sb("w8", [P, 2, 8]); ki = sb("ki", [P, 8], I32); pi = sb("pi", [P, 8], I32)
        ov = sb("ov", [P, 8], I32); sl = sb("sl", [P, 2, 8], I32)
        gps = ps("gps"); pps = ps("pps")
        gg = [ps(f"gg{i}") for i in range(2)]; uu = [ps(f"uu{i}") for i in range(2)]; dd = [ps(f"dd{i}") for i in range(2)]

        gate_in = sem("gate_in"); up_in = sem("up_in"); w_in = sem("w_in"); pool_step = sem("pool_step"); consts = sem("consts"); table_set = sem("table_set"); spare_set = sem("spare_set")
        xT_in = [sem(f"xT_in{i}") for i in range(2)]; x_in = [sem(f"x_in{i}") for i in range(2)]
        gate_done = sem("gate_done"); gu_done = sem("gu_done"); pos_done = sem("pos_done"); dn_done = sem("dn_done")
        sc_done = sem("sc_done"); sg_done = sem("sg_done"); hg_done = sem("hg_done"); hT_done = sem("hT_done")
        pick = sem("pick"); sel_done = sem("sel_done"); wden_done = sem("wden_done"); place = sem("place"); kk_done = sem("kk_done"); k8_done = sem("k8_done")
        eq_done = sem("eq_done"); oh_done = sem("oh_done"); w8_done = sem("w8_done"); slot_done = sem("slot_done"); cum_done = sem("cum_done")
        r_done = sem("r_done"); tok_done = sem("tok_done")
        r_out = [sem(f"r_out{i}") for i in range(2)]
        scat = [kept_semaphore(nc, sems, f"scat{i}") for i in range(2)]
        with nc.Block() as block:
            @block.sync
            def _(sp):
                sp.dma_start(gate[:], gateT).then_inc(gate_in, 16)
                sp.dma_start(ebb[:], ebias.partition_broadcast(P)).then_inc(gate_in, 16)
                sp.dma_start(wg[:], sgT).then_inc(up_in, 16)
                sp.dma_start(wu[:], suT).then_inc(up_in, 16)
                sp.dma_start(wd[:], sdT).then_inc(w_in, 16)
                sp.wait_ge(consts, 1)
                sp.dma_start(table.rearrange("(p n) c -> p (n c)", p=P), vacant[:].rearrange("p n c -> p (n c)")).then_inc(table_set, 16)
                for rows in (x2, res):
                    sp.dma_start(rows[BATCH * SEQ:].rearrange("(p n) d -> p (n d)", p=P), zero[:]).then_inc(spare_set, 16)

                def body(t, s):
                    wait(sp, gu_done, t - 1)
                    sp.dma_start(xT[:, s], x2T[t]).then_inc(xT_in[s], 16)
                    wait(sp, r_done, t - 1)
                    sp.dma_start(xr[:, s], x2[bass.ds(t * P, P), :]).then_inc(x_in[s], 16)
                each_tile(sp, body)
                sp.wait_ge(spare_set, 32)

            @block.gpsimd
            def _(pool):
                n = 0
                def step(ins):
                    nonlocal n
                    n += 1
                    ins.then_inc(pool_step, 1)
                    pool.wait_ge(pool_step, n)
                step(pool.memset(tri[:], 0.0))
                step(pool.memset(ones[:], 1.0))
                step(pool.affine_select(out=tri[:], in_=tri[:], compare_op=ALU.is_ge, fill=1.0, base=0,
                                        pattern=[[-1, P]], channel_multiplier=1))
                step(pool.iota(eb1i[:], pattern=[[KEYS, E_]], base=1, channel_multiplier=0))
                step(pool.tensor_copy(eb1[:], eb1i[:]))
                step(pool.iota(tokall[:], pattern=[[P, NT]], base=0, channel_multiplier=1))
                step(pool.iota(spare_row[:].rearrange("p (n u) -> p n u", u=SPARE), pattern=[[0, SLOTS // P // SPARE], [1, SPARE]],
                               base=BATCH * SEQ, channel_multiplier=0))
                step(pool.memset(vacant[:], 0.0))
                step(pool.tensor_copy(vacant[:, :, 0], spare_row[:]))
                step(pool.memset(zero[:], 0.0))
                step(pool.memset(cum[:, 0], 0.0))
                for v in (gs, rl):
                    step(pool.memset(v[:], LOWEST))
                pool.sem_inc(consts, 1)
                pool.wait_ge(table_set, 16)

                def body(t, s):
                    pool.wait_ge(eq_done, t + 1)
                    wait(pool, w8_done, t)
                    pool.tensor_tensor(oh[:], eq[:], wden[:, s].unsqueeze(1).broadcast_to([P, 8, E_]), ALU.mult).then_inc(oh_done, 1)
                    if not isinstance(t, int) or t >= 2:
                        pool.wait_ge(scat[s], ((t - s) // 2) * 128)
                    pool.tensor_copy(entry[:, s, :, 0], tokall[:, bass.ds(t, 1)].broadcast_to([P, TOPK])).then_inc(tok_done, 1)
                    pool.wait_ge(tok_done, t + 1)
                    pool.wait_ge(slot_done, t + 1)
                    pool.wait_ge(w8_done, t + 1)
                    apart(pool, passed)
                    for k in range(TOPK):
                        pool.indirect_dma_start(out=table, out_offset=bass.IndirectOffsetOnAxis(ap=sl[:, s, k:k + 1], axis=0),
                                                in_=entry[:, s, k], in_offset=None, bounds_check=SLOTS - 1,
                                                oob_is_err=False).then_inc(scat[s], 16)
                each_tile(pool, body)
                for s in range(2):
                    pool.wait_ge(scat[s], 128 * (NT // 2))

            @block.tensor
            def _(pe):
                pe.wait_ge(gate_in, 32)
                pe.wait_ge(consts, 1)
                def up(t, s):
                    fetched(pe, xT_in, t, s)
                    wait(pe, sc_done, t)
                    for k in range(KT):
                        mm = nc.tensor.matmul(gps[:, 0:E_], xT[:, s, k], gate[:, k], start=k == 0, stop=k == KT - 1)
                    mm.then_inc(gate_done, 1)
                    if isinstance(t, int) and t == 0:
                        pe.wait_ge(up_in, 32)
                    wait(pe, hT_done, t - 1)
                    for w, o in ((wg, gg[s]), (wu, uu[s])):
                        for f in range(KT):
                            for k in range(KT):
                                mm = nc.tensor.matmul(o[:, f * P:(f + 1) * P], w[:, k, f * P:(f + 1) * P], xT[:, s, k],
                                                      start=k == 0, stop=k == KT - 1)
                    mm.then_inc(gu_done, 1)

                def rank(t, s):
                    pe.wait_ge(sel_done, t + 1)
                    if not isinstance(t, int) or t > 0:
                        pe.wait_ge(cum_done, t)
                    wait(pe, kk_done, t * 2)
                    nc.tensor.matmul(pps[:, 0:E_], tri[:], selb[:, s], start=True, stop=False)
                    nc.tensor.matmul(pps[:, 0:E_], ones[:], cum[:, s], start=False, stop=True).then_inc(pos_done, 1)

                def down(t, s):
                    pe.wait_ge(hT_done, t + 1)
                    if isinstance(t, int) and t == 0:
                        pe.wait_ge(w_in, 16)
                    wait(pe, r_done, t - 1)
                    for k in range(KT):
                        mm = nc.tensor.matmul(dd[s][:], hT[:, s, k], wd[:, k], start=k == 0, stop=k == KT - 1)
                    mm.then_inc(dn_done, 1)

                up(0, 0)
                def body(t, s):
                    if before_end(t, 1):
                        up(t + 1, 1 - s)
                    rank(t, s)
                    down(t, s)
                each_tile(pe, body)

            @block.scalar
            def _(act):
                def up(t, s):
                    act.wait_ge(gate_done, t + 1)
                    wait(act, w8_done, t - 1)
                    nc.scalar.activation(sc[:, s], gps[:, 0:E_], ACT.Sigmoid).then_inc(sc_done, 1)
                    act.wait_ge(gu_done, t + 1)
                    wait(act, hg_done, t)
                    nc.scalar.activation(sg[:], gg[s][:], ACT.Sigmoid).then_inc(sg_done, 1)

                up(0, 0)
                def body(t, s):
                    if before_end(t, 1):
                        up(t + 1, 1 - s)
                    act.wait_ge(r_done, t + 1)
                    act.dma_start(res[bass.ds(t * P, P), :], r[:, s]).then_inc(r_out[s], 16)
                each_tile(act, body)
                for s in range(2):
                    act.wait_ge(r_out[s], 16 * (NT // 2))

            @block.vector
            def _(dve):
                dve.wait_ge(gate_in, 32)
                dve.wait_ge(consts, 1)
                PICKS, PLACES = 18, 8

                def choose(t, s):
                    n = 0
                    def step(ins):
                        nonlocal n
                        n += 1
                        ins.then_inc(pick, 1)
                        dve.wait_ge(pick, t * PICKS + n)
                    dve.wait_ge(sc_done, t + 1)
                    step(dve.tensor_tensor(sfc[:], sc[:, s], ebb[:], ALU.add))
                    apart(dve, passed)
                    for g in range(NGRP):
                        ins = dve.max(srt[:, g], sfc[:, g * EG:(g + 1) * EG])
                        if g < NGRP - 1:
                            ins.then_inc(pick, 1)
                            n += 1
                    step(ins)
                    step(dve.tensor_tensor(gs[:, 0:NGRP], srt[:, :, 0], srt[:, :, 1], ALU.add))
                    apart(dve, passed)
                    step(dve.max(g8[:], gs[:, 0:NGRP]))
                    step(dve.tensor_copy(rl[:, 0:TG], g8[:, 0:TG]))
                    apart(dve, passed)
                    step(dve.match_replace(out=gr[:], in_to_replace=rl[:], in_values=gs[:], imm_value=-1.0e38))
                    step(dve.tensor_tensor(gm[:], gr[:, 0:NGRP], gs[:, 0:NGRP], ALU.not_equal))
                    step(dve.tensor_tensor(tmp[:].rearrange("p (g e) -> p g e", g=NGRP), sfc[:].rearrange("p (g e) -> p g e", g=NGRP),
                                           gm[:].unsqueeze(2).broadcast_to([P, NGRP, EG]), ALU.mult))
                    apart(dve, passed)
                    step(dve.max(t8[:], tmp[:]))
                    apart(dve, passed)
                    step(dve.match_replace(out=tmp2[:], in_to_replace=t8[:], in_values=tmp[:], imm_value=LOWEST))
                    wait(dve, pos_done, t - 1)
                    wait(dve, oh_done, t - 1)
                    dve.tensor_tensor(sel[:, s], tmp2[:], tmp[:], ALU.not_equal).then_inc(pick, 1)
                    dve.wait_ge(pick, t * PICKS + PICKS)
                    assert n + 1 == PICKS, n

                def choose_end(t, s):
                    dve.tensor_copy(selb[:, s], sel[:, s]).then_inc(sel_done, 1)
                    dve.tensor_tensor_reduce(out=wden[:, s], in0=sel[:, s], in1=sc[:, s], scale=1.0, scalar=0.0,
                                             op0=ALU.mult, op1=ALU.add, accum_out=wsum[:, s:s + 1]).then_inc(wden_done, 1)
                    dve.wait_ge(wden_done, t + 1)

                def act_part(t, s):
                    dve.wait_ge(sg_done, t + 1)
                    dve.tensor_tensor(hg[:], sg[:], gg[s][:], ALU.mult).then_inc(hg_done, 1)
                    dve.wait_ge(hg_done, t + 1)
                    wait(dve, dn_done, t - 1)
                    dve.tensor_tensor(hT[:, s].rearrange("p k t -> p (k t)"), hg[:], uu[s][:], ALU.mult).then_inc(hT_done, 1)

                def locate(t, s):
                    dve.wait_ge(pos_done, t + 1)
                    dve.wait_ge(sel_done, t + 1)
                    dve.tensor_tensor(cum[:, 1 - s], cum[:, s], selb[:, s], ALU.add).then_inc(cum_done, 1)
                    dve.tensor_tensor(kk[:, s], pps[:, 0:E_], eb1[:], ALU.add).then_inc(kk_done, 1)
                    dve.wait_ge(kk_done, t * 2 + 1)
                    dve.tensor_tensor(kk[:, s], kk[:, s], sel[:, s], ALU.mult).then_inc(kk_done, 1)
                    dve.wait_ge(kk_done, t * 2 + 2)
                    apart(dve, passed)
                    dve.max(k8[:, s], kk[:, s]).then_inc(k8_done, 1)
                    dve.wait_ge(k8_done, t + 1)
                    wait(dve, oh_done, t)
                    dve.tensor_tensor(eq[:], kk[:, s].unsqueeze(1).broadcast_to([P, 8, E_]),
                                      k8[:, s].unsqueeze(2).broadcast_to([P, 8, E_]), ALU.is_equal).then_inc(eq_done, 1)
                    n = 0
                    def step(ins):
                        nonlocal n
                        n += 1
                        ins.then_inc(place, 1)
                        dve.wait_ge(place, t * PLACES + n)
                    step(dve.tensor_scalar(ki[:], k8[:, s], -1.0, None, ALU.add))
                    step(dve.tensor_scalar(pi[:], ki[:], KEYS - 1, None, ALU.bitwise_and))
                    step(dve.tensor_scalar(ki[:], ki[:], 12, 9, ALU.logical_shift_right, ALU.logical_shift_left))
                    step(dve.tensor_scalar(ov[:], pi[:], float(CAP), LIM, ALU.is_ge, ALU.mult))
                    apart(dve, passed)
                    step(dve.tensor_tensor(pi[:], pi[:], ki[:], ALU.add))
                    if not isinstance(t, int) or t >= 2:
                        dve.wait_ge(scat[s], ((t - s) // 2) * 128)
                    apart(dve, passed)
                    dve.tensor_tensor(sl[:, s], pi[:], ov[:], ALU.add).then_inc(slot_done, 1)
                    step(dve.tensor_scalar(wrec[:], wsum[:, s:s + 1], 1.0e-20, None, ALU.add))
                    step(dve.reciprocal(wrec[:], wrec[:]))
                    dve.wait_ge(oh_done, t + 1)
                    step(dve.tensor_reduce(w8[:, s], oh[:], AX.X, ALU.add))
                    assert n == PLACES
                    dve.tensor_scalar(entry[:, s, :, 1], w8[:, s], wrec[:], SCALING, ALU.mult, ALU.mult).then_inc(w8_done, 1)
                    dve.wait_ge(w8_done, t + 1)

                def finish(t, s):
                    dve.wait_ge(dn_done, t + 1)
                    fetched(dve, x_in, t, s)
                    stored(dve, r_out, t, s)
                    dve.tensor_tensor(r[:, s], dd[s][:], xr[:, s], ALU.add).then_inc(r_done, 1)

                choose(0, 0)
                choose_end(0, 0)
                act_part(0, 0)
                def body(t, s):
                    if before_end(t, 1):
                        choose(t + 1, 1 - s)
                        choose_end(t + 1, 1 - s)
                        act_part(t + 1, 1 - s)
                    locate(t, s)
                    finish(t, s)
                each_tile(dve, body)

        tot = sb("tot", [P, E_]); actv = sb("actv", [P, UNITS]); incl = sb("incl", [P, UNITS])
        iou = sb("iou", [P, UNITS], I32); iouf = sb("iouf", [P, UNITS]); row = sb("row", [P, 1], I32); rowf = sb("rowf", [P, 1])
        hot = sb("hot", [P, UNITS]); zrow = sb("zrow", [P, UNITS]); wl = sb("wl", [P, 2]); wli = sb("wli", [P, 2], I32)
        tot_done = sem("tot_done"); lstep = sem("lstep"); lconst = sem("lconst"); wl_out = sem("wl_out")
        with nc.Block() as block:
            @block.gpsimd
            def _(pool):
                pool.iota(iou[:], pattern=[[1, UNITS]], base=0, channel_multiplier=0).then_inc(lconst, 1)
                pool.iota(row[:], pattern=[[0, 1]], base=1, channel_multiplier=1).then_inc(lconst, 1)
                pool.memset(zrow[:], 0.0).then_inc(lconst, 1)

            @block.tensor
            def _(pe):
                nc.tensor.matmul(pps[:, 0:E_], ones[:], cum[:, NT % 2], start=True, stop=True).then_inc(tot_done, 1)

            @block.vector
            def _(dve):
                n = 0
                def step(ins):
                    nonlocal n
                    n += 1
                    ins.then_inc(lstep, 1)
                    dve.wait_ge(lstep, n)
                dve.wait_ge(lconst, 3)
                step(dve.tensor_copy(iouf[:], iou[:]))
                step(dve.tensor_copy(rowf[:], row[:]))
                dve.wait_ge(tot_done, 1)
                step(dve.tensor_copy(tot[:], pps[:, 0:E_]))
                av = actv[:].rearrange("p (e u) -> p e u", u=UPE)
                for u in range(UPE):
                    step(dve.tensor_scalar(av[:, :, u], tot[:], float(u * UNIT), None, ALU.is_gt))
                step(dve.tensor_tensor_scan(incl[:], actv[:], zrow[:], 0.0, ALU.add, ALU.add))
                step(dve.tensor_scalar(hot[:], incl[:], rowf[:], None, ALU.is_equal))
                step(dve.tensor_tensor(hot[:], hot[:], actv[:], ALU.mult))
                step(dve.tensor_tensor_reduce(out=hot[:], in0=hot[:], in1=iouf[:], scale=1.0, scalar=0.0, op0=ALU.mult,
                                              op1=ALU.add, accum_out=wl[:, 0:1]))
                step(dve.tensor_copy(wl[:, 1:2], incl[:, UNITS - 1:UNITS]))
                step(dve.tensor_copy(wli[:], wl[:]))
                dve.sem_inc(tot_done, 1)

            @block.sync
            def _(sp):
                sp.wait_ge(tot_done, 2)
                sp.dma_start(worklist, wli[:]).then_inc(wl_out, 16)
                sp.wait_ge(wl_out, 16)


def experts(nc, sems, x2, table, worklist, w1T, w3T, w2T, res, unused):
    J = UNIT // P
    FT = FF // P
    with ExitStack() as ctx:
        def sb(name, shape, dt=F32):
            return ctx.enter_context(nc.sbuf_tensor("ex_" + name, shape, dt))

        sem = ctx.enter_context(own_semaphores(nc, "ex_"))
        passed = sem("passed")

        def ps(name):
            return ctx.enter_context(nc.psum_tensor("ex_" + name, [P, 512], F32))
        AHEAD = 2
        HALVES = SLOTS // P // P
        TERMS = ((0, 0), (0, 1), (1, 0))
        BUNDLE = 8
        wl = sb("wl", [1, 2 * (UNITS + AHEAD)], I32)
        entries = sb("entries", [P, HALVES, P, 2]); token = sb("token", [P, HALVES * P], I32); weight = sb("weight", [P, HALVES * P])
        identf = sb("identf", [P, P])
        w1 = sb("w1", [P, 2, KT, FF]); w3 = sb("w3", [P, 2, KT, FF]); w2 = sb("w2", [P, 2, FT, DM])
        w1h = sb("w1h", [P, 2, 2, KT, FF], F32R); w3h = sb("w3h", [P, 2, 2, KT, FF], F32R); w2h = sb("w2h", [P, 2, 2, FT, DM], F32R)
        source = sb("source", [P, 2, J], I32); target = sb("target", [P, 2, J], I32); factor = sb("factor", [P, 2, J])
        xe = sb("xe", [P, 2, J, DM]); xeT = sb("xeT", [P, 2, 2, KT, UNIT], F32R)
        sig = sb("sig", [P, FT * UNIT]); hg = sb("hg", [P, FT * UNIT]); hT = sb("hT", [P, FT * UNIT]); hTh = sb("hTh", [P, 2, 2, FT, UNIT], F32R)
        y = sb("y", [P, 2, J, DM]); zero = sb("zero", [P, 1])
        tps = [ps(f"tps{i}") for i in range(2)]; h1 = [ps(f"h1{i}") for i in range(1)]; h3 = [ps(f"h3{i}") for i in range(1)]
        yps = [ps(f"yps{i}") for i in range(2)]
        wl_in = sem("wl_in"); consts = sem("consts"); pool_step = sem("pool_step")
        w_in = [sem(f"w_in{i}") for i in range(2)]; w_high = sem("w_high"); w_low_v = sem("w_low_v"); w_low_p = sem("w_low_p")
        entries_in = sem("entries_in"); entries_turned = sem("entries_turned"); listed = sem("listed")
        source_set = sem("source_set"); target_set = sem("target_set"); factor_set = sem("factor_set")
        xe_in = [kept_semaphore(nc, sems, f"xe_in{i}") for i in range(2)]
        t_done = sem("t_done"); ta_out = sem("ta_out"); tv_out = sem("tv_out")
        g1_done = sem("g1_done"); g3_done = sem("g3_done"); g2_done = sem("g2_done")
        sig_done = sem("sig_done"); hg_done = sem("hg_done"); h_done = sem("h_done"); h_high = sem("h_high"); h_low = sem("h_low")
        y_done = sem("y_done"); added = kept_semaphore(nc, sems, "added")
        block = ctx.enter_context(nc.Block())

        def each_unit(eng, first, body):
            eng.wait_ge(wl_in, 16)
            n = eng.value_load(wl[0:1, 1:2], min_val=0, max_val=UNITS)
            first()
            with eng.Fori(0, UNITS // BUNDLE) as o:
                with eng.If(o * BUNDLE < n):
                    with eng.Fori(0, BUNDLE // 2) as i:
                        for s in range(2):
                            w = eng.snap(o * BUNDLE + i * 2 + s)
                            with eng.If(w < n):
                                body(w, s)

        def added_all(w):
            return w * (16 * J) + 2 * 16 * J

        def turn_of(w, s):
            return (w - s) // 2 + 1

        @block.sync
        def _(sp):
            sp.wait_ge(consts, 1)
            sp.dma_start(entries[:].rearrange("b a p c -> b a (p c)"),
                         table.rearrange("(a b p) c -> b a (p c)", a=HALVES, b=P)).then_inc(entries_in, 16)
            sp.dma_start(wl[:, 0:2 * UNITS], worklist.rearrange("u c -> (u c)").unsqueeze(0)).then_inc(wl_in, 16)

            def load(w, s):
                e = sp.value_load(wl[0:1, bass.ds(w * 2, 1)], min_val=0, max_val=UNITS - 1) // UPE
                sp.wait_ge(w_low_v, w * 2 + 2)
                apart(sp, passed)
                sp.wait_ge(w_low_p, w + 1)
                for dst, src in ((w1, w1T), (w3, w3T), (w2, w2T)):
                    sp.dma_start(dst[:, s], src[e]).then_inc(w_in[s], 16)
            each_unit(sp, lambda: load(0, 0), lambda w, s: load(w + 1, 1 - s))

        @block.gpsimd
        def _(pool):
            n = 0
            def step(ins):
                nonlocal n
                n += 1
                ins.then_inc(pool_step, 1)
                pool.wait_ge(pool_step, n)
            step(pool.memset(wl[:], 0))
            step(pool.memset(zero[:], 0.0))
            step(pool.memset(identf[:], 0.0))
            step(pool.affine_select(out=identf[:], in_=identf[:], compare_op=ALU.not_equal, fill=1.0, base=0,
                                    pattern=[[-1, P]], channel_multiplier=1))
            pool.sem_inc(consts, 1)

            for n in range(2 * J):
                pool.dma_start(unused[n], zero[:]).then_inc(added, 16)
            pool.wait_ge(added, 2 * J * 16)
            pool.wait_ge(listed, 2)

            def unit_of(w):
                return pool.value_load(wl[0:1, bass.ds(w * 2, 1)], min_val=0, max_val=UNITS - 1)

            def gather(w, s):
                unit = unit_of(w)
                pool.wait_ge(t_done, w + 1)
                apart(pool, passed)
                pool.tensor_copy(source[:, s], token[:, bass.ds(unit * J, J)]).then_inc(source_set, 1)
                pool.wait_ge(source_set, w + 1)
                apart(pool, passed)
                for j in range(J):
                    pool.indirect_dma_start(out=xe[:, s, j], out_offset=None, in_=x2,
                                            in_offset=bass.IndirectOffsetOnAxis(ap=source[:, s, j:j + 1], axis=0)).then_inc(xe_in[s], 16)

            def prepare(w, s):
                unit = unit_of(w)
                pool.wait_ge(added, added_all(w - 1))
                apart(pool, passed)
                pool.tensor_copy(target[:, s], token[:, bass.ds(unit * J, J)]).then_inc(target_set, 1)
                pool.tensor_copy(factor[:, s], weight[:, bass.ds(unit * J, J)]).then_inc(factor_set, 1)

            def add(w, s):
                pool.wait_ge(target_set, w + 1)
                pool.wait_ge(y_done, w * J + 2 * J)
                pool.wait_ge(added, added_all(w))
                apart(pool, passed)
                for j in range(J):
                    pool.indirect_dma_start(out=res, out_offset=bass.IndirectOffsetOnAxis(ap=target[:, s, j:j + 1], axis=0),
                                            in_=y[:, s, j], in_offset=None, compute_op=ALU.add).then_inc(added, 16)

            pool.sem_inc(w_low_p, 2)

            def split_low(w, s):
                pool.wait_ge(w_high, w * 3 + 3)
                pool.tensor_tensor(w2h[:, s, 1], w2[:, s], w2h[:, s, 0], ALU.subtract).then_inc(w_low_p, 1)

            def first():
                for w in range(AHEAD):
                    gather(w, w)
                split_low(0, 0)

            def body(w, s):
                prepare(w, s)
                gather(w + AHEAD, s)
                split_low(w + 1, 1 - s)
                add(w, s)
            each_unit(pool, first, body)
            n = pool.value_load(wl[0:1, 1:2], min_val=0, max_val=UNITS)
            pool.wait_ge(xe_in[0], (n + 3) // 2 * (16 * J))
            pool.wait_ge(xe_in[1], (n + 2) // 2 * (16 * J))
            pool.wait_ge(added, added_all(n))
            apart(pool, passed)

        @block.tensor
        def _(pe):
            pe.sem_inc(t_done, 2)
            pe.sem_inc(g2_done, 2)
            pe.wait_ge(consts, 1)
            pe.wait_ge(entries_in, 16)
            for c in range(2):
                for a in range(HALVES):
                    mm = nc.tensor.transpose(h1[0][:, (c * HALVES + a) * P:(c * HALVES + a + 1) * P], entries[:, a, :, c], identf[:])
            mm.then_inc(entries_turned, 1)
            pe.wait_ge(listed, 2)

            def turn(w, s):
                pe.wait_ge(xe_in[s], turn_of(w, s) * (16 * J))
                pe.wait_ge(ta_out, w * J + J)
                pe.wait_ge(tv_out, w * J + J)
                for j in range(J):
                    for k in range(KT):
                        mm = nc.tensor.transpose(tps[j][:, k * P:(k + 1) * P], xe[:, s, j, k * P:(k + 1) * P], identf[:])
                mm.then_inc(t_done, 1)

            def body(w, s):
                pe.wait_ge(ta_out, w * J + 2 * J)
                pe.wait_ge(tv_out, w * J + 2 * J)
                pe.wait_ge(w_high, w * 3 + 3)
                pe.wait_ge(w_low_v, w * 2 + 4)
                pe.wait_ge(w_low_p, w + 3)
                pe.wait_ge(h_low, w + 1)
                for wt, bank, done in ((w1h, h1, g1_done), (w3h, h3, g3_done)):
                    for f in range(FT):
                        for k in range(KT):
                            for n, (a, b) in enumerate(TERMS):
                                mm = nc.tensor.matmul(bank[0][:, f * UNIT:(f + 1) * UNIT], wt[:, s, a, k, f * P:(f + 1) * P],
                                                      xeT[:, s, b, k], start=k == 0 and n == 0,
                                                      stop=k == KT - 1 and n == len(TERMS) - 1)
                    mm.then_inc(done, 1)
                turn(w + 1, 1 - s)
                pe.wait_ge(h_high, w + 1)
                pe.wait_ge(y_done, w * J + J)
                for n, (a, b) in enumerate(TERMS):
                    if a == 1:
                        pe.wait_ge(h_low, w + 2)
                    for j in range(J):
                        for f in range(FT):
                            mm = nc.tensor.matmul(yps[j][:], hTh[:, s, a, f, j * P:(j + 1) * P], w2h[:, s, b, f],
                                                  start=n == 0 and f == 0, stop=n == len(TERMS) - 1 and f == FT - 1,
                                                  skip_group_check=True)
                mm.then_inc(g2_done, 1)
            each_unit(pe, lambda: turn(0, 0), body)

        @block.scalar
        def _(act):
            act.sem_inc(ta_out, J)
            act.sem_inc(sig_done, 1)
            act.wait_ge(consts, 1)

            def split_high(w, s, n):
                for wt, halves in ((w1, w1h), (w3, w3h), (w2, w2h))[n]:
                    nc.scalar.copy(halves[:, s, 0], wt[:, s]).then_inc(w_high, 1)

            def take(w, s):
                act.wait_ge(t_done, w + 3)
                act.wait_ge(g2_done, w + 1)
                for j in range(J):
                    nc.scalar.copy(xeT[:, s, 0, :, j * P:(j + 1) * P], tps[j][:].rearrange("p (k t) -> p k t", k=KT)).then_inc(ta_out, 1)

            def first():
                act.wait_ge(w_in[0], 48)
                split_high(0, 0, slice(0, 3))
                take(0, 0)

            def body(w, s):
                act.wait_ge(w_in[1 - s], turn_of(w + 1, 1 - s) * 48)
                act.wait_ge(g2_done, w + 2)
                split_high(w + 1, 1 - s, slice(0, 2))
                act.wait_ge(g1_done, w + 1)
                act.wait_ge(hg_done, w + 1)
                nc.scalar.activation(sig[:], h1[0][:], ACT.Sigmoid).then_inc(sig_done, 1)
                split_high(w + 1, 1 - s, slice(2, 3))
                act.wait_ge(h_done, w + 1)
                nc.scalar.copy(hTh[:, s, 0].rearrange("p f t -> p (f t)"), hT[:]).then_inc(h_high, 1)
                take(w + 1, 1 - s)
            each_unit(act, first, body)

        @block.vector
        def _(dve):
            dve.sem_inc(tv_out, J)
            dve.sem_inc(w_low_v, 4)
            dve.sem_inc(hg_done, 1)
            dve.sem_inc(h_low, 1)
            dve.sem_inc(y_done, J)
            dve.wait_ge(added, 2 * J * 16)
            dve.wait_ge(entries_turned, 1)
            dve.tensor_copy(token[:], h1[0][:, 0:HALVES * P]).then_inc(listed, 1)
            dve.tensor_copy(weight[:], h1[0][:, HALVES * P:2 * HALVES * P]).then_inc(listed, 1)

            def split_low(w, s):
                for n, (wt, halves) in enumerate(((w1, w1h), (w3, w3h))):
                    dve.wait_ge(w_high, w * 3 + (n + 1))
                    dve.tensor_tensor(halves[:, s, 1], wt[:, s], halves[:, s, 0], ALU.subtract).then_inc(w_low_v, 1)

            def take(w, s):
                for j in range(J):
                    dve.wait_ge(ta_out, w * J + (J + j + 1))
                    dve.tensor_tensor(xeT[:, s, 1, :, j * P:(j + 1) * P], tps[j][:].rearrange("p (k t) -> p k t", k=KT),
                                      xeT[:, s, 0, :, j * P:(j + 1) * P], ALU.subtract).then_inc(tv_out, 1)

            def first():
                split_low(0, 0)
                take(0, 0)

            def body(w, s):
                split_low(w + 1, 1 - s)
                dve.wait_ge(sig_done, w + 2)
                dve.tensor_tensor(hg[:], sig[:], h1[0][:], ALU.mult).then_inc(hg_done, 1)
                dve.wait_ge(g3_done, w + 1)
                dve.wait_ge(hg_done, w + 2)
                dve.tensor_tensor(hT[:], hg[:], h3[0][:], ALU.mult).then_inc(h_done, 1)
                dve.wait_ge(h_high, w + 1)
                dve.tensor_tensor(hTh[:, s, 1].rearrange("p f t -> p (f t)"), hT[:], hTh[:, s, 0].rearrange("p f t -> p (f t)"),
                                  ALU.subtract).then_inc(h_low, 1)
                take(w + 1, 1 - s)
                dve.wait_ge(g2_done, w + 3)
                dve.wait_ge(added, added_all(w - 1))
                dve.wait_ge(factor_set, w + 1)
                for j in range(J):
                    dve.tensor_scalar(y[:, s, j], yps[j][:], factor[:, s, j:j + 1], None, ALU.mult).then_inc(y_done, 1)
            each_unit(dve, first, body)


def last_norm(nc, sems, res, out):
    PAIR = 2
    RING = 4
    ROUNDS = NT // PAIR // RING
    with ExitStack() as ctx:
        def sb(name, shape, dt=F32):
            return ctx.enter_context(nc.sbuf_tensor("ln_" + name, shape, dt))

        sem = ctx.enter_context(own_semaphores(nc, "ln_"))
        passed = sem("passed")
        r = sb("r", [P, RING, PAIR, DM]); stats = sb("stats", [P, RING, PAIR, 6]); mv = sb("mv", [P, RING, PAIR, 2])
        std = sb("std", [P, RING, PAIR]); rstd = sb("rstd", [P, RING, PAIR]); eps = sb("eps", [P, 1])
        consts = sem("consts"); r_in = [sem(f"r_in{i}") for i in range(RING)]; stats_done = sem("stats_done")
        mv_done = sem("mv_done"); std_done = sem("std_done"); rstd_done = sem("rstd_done"); o_done = sem("o_done")
        o_out = [sem(f"o_out{i}") for i in range(RING)]
        block = ctx.enter_context(nc.Block())

        def rows(dram, t):
            return dram[bass.ds(t * (PAIR * P), PAIR * P), :].rearrange("(n p) d -> p n d", p=P)

        @block.sync
        def _(sp):
            for s in range(RING):
                sp.dma_start(r[:, s], rows(res, s)).then_inc(r_in[s], 16)
            with sp.Fori(1, ROUNDS) as i:
                for s in range(RING):
                    sp.wait_ge(o_out[s], i * 16)
                    sp.dma_start(r[:, s], rows(res, i * RING + s)).then_inc(r_in[s], 16)

        @block.gpsimd
        def _(pool):
            pool.memset(eps[:], EPS).then_inc(consts, 1)

        @block.scalar
        def _(act):
            act.wait_ge(consts, 1)
            def deviation(t, s):
                act.wait_ge(mv_done, t * PAIR + PAIR)
                nc.scalar.activation(std[:, s], mv[:, s, :, 1], ACT.Sqrt, bias=eps[:]).then_inc(std_done, 1)

            def store(t, s):
                act.wait_ge(o_done, t * PAIR + PAIR)
                act.dma_start(rows(out, t), r[:, s]).then_inc(o_out[s], 16)

            with act.Fori(0, ROUNDS) as i:
                deviation(i * RING, 0)
                for s in range(RING):
                    if s + 1 < RING:
                        deviation(i * RING + (s + 1), s + 1)
                    store(i * RING + s, s)
            for s in range(RING):
                act.wait_ge(o_out[s], 16 * ROUNDS)

        @block.vector
        def _(dve):
            def measure(t, i, s):
                dve.wait_ge(r_in[s], i * 16 + 16)
                for n in range(PAIR):
                    dve.bn_stats(stats[:, s, n], r[:, s, n]).then_inc(stats_done, 1)
                for n in range(PAIR):
                    dve.wait_ge(stats_done, t * PAIR + (n + 1))
                    apart(dve, passed)
                    dve.bn_aggr(mv[:, s, n], stats[:, s, n]).then_inc(mv_done, 1)

            def normalise(t, s):
                dve.wait_ge(std_done, t + 1)
                dve.reciprocal(rstd[:, s], std[:, s]).then_inc(rstd_done, 1)
                dve.wait_ge(rstd_done, t + 1)
                for n in range(PAIR):
                    dve.tensor_scalar(r[:, s, n], r[:, s, n], mv[:, s, n, 0:1], rstd[:, s, n:n + 1], ALU.subtract,
                                      ALU.mult).then_inc(o_done, 1)

            with dve.Fori(0, ROUNDS) as i:
                measure(i * RING, i, 0)
                for s in range(RING):
                    if s + 1 < RING:
                        measure(i * RING + (s + 1), i, s + 1)
                    normalise(i * RING + s, s)


def program(nc, t):
    def scratch(name, shape, dt=F32):
        return nc.dram_tensor("scratch_" + name, shape, dt, kind="Internal").ap()

    tokens = BATCH * SEQ
    aT = scratch("attention_T", [NG, P, tokens])
    x1 = scratch("x1", [tokens, DM])
    x2, res = (scratch(n, [tokens + SPARE, DM]) for n in ("x2", "residual"))
    x1T, x2T = (scratch(n, [NT, P, KT, P]) for n in ("x1_T", "x2_T"))
    table = scratch("token_and_weight_of_slot", [SLOTS, 2])
    worklist = scratch("worklist", [UNITS, 2], I32)
    unused = scratch("unused", [2 * UNIT // P, P, 1])
    with ExitStack() as sems:
        self_attention(nc, sems, t["xT"], t["a_wq"], t["a_wk"], t["a_wv"], t["a_bq"], t["a_bk"], t["a_bv"], t["a_scale"],
                       aT)
        out_proj_norm(nc, sems, aT, t["x"], t["a_wo"], t["a_bo"], x1, x1T)
        cross_attention(nc, sems, t["ctxT"], t["mask"], t["c_wq"], t["c_wk"], t["c_wv"], t["c_wo"], t["c_bq"], t["c_bk"],
                        t["c_bv"], t["c_bo"], x1, x1T, x2, x2T)
        route_and_shared(nc, sems, x2, x2T, t["gate"], t["e_bias"], t["s_gate"], t["s_up"], t["s_down"], res, table,
                         worklist)
        experts(nc, sems, x2, table, worklist, t["w1"], t["w3"], t["w2"], res, unused)
        last_norm(nc, sems, res, t["out"])


def kernel(**inputs):
    import numpy as np
    import concourse.bacc as bacc
    from concourse.bass_utils import run_bass_kernel_spmd

    inputs = {k: np.asarray(v) for k, v in inputs.items()}

    def contract_rows(w):
        return w.T.reshape(-1, P, w.shape[0]).transpose(1, 0, 2)

    def by_group(w):
        return w.T.reshape(KT, P, NG, P).transpose(2, 1, 0, 3)

    def by_expert(w):
        e, o, i = w.shape
        return w.transpose(0, 2, 1).reshape(e, i // P, P, o).transpose(0, 2, 1, 3)

    a, c, f = "L0_attn_", "L0_xattn_", "L0_ffn_"
    x = inputs["x"]
    laid = {
        "x": x.reshape(BATCH * SEQ, DM),
        "xT": x.transpose(0, 2, 1).reshape(BATCH, KT, P, SEQ).transpose(0, 2, 1, 3),
        "ctxT": inputs["ctx_1024"].transpose(0, 2, 1).reshape(BATCH, KT, P, CTX).transpose(0, 2, 1, 3),
        "mask": inputs["mask_SxS2_bk0"],
        "a_wq": by_group(inputs[a + "Wq"]), "a_wk": by_group(inputs[a + "Wk"]), "a_wv": by_group(inputs[a + "Wv"]),
        "a_bq": inputs[a + "bq"].reshape(NG, P, 1), "a_bk": inputs[a + "bk"].reshape(NG, P, 1),
        "a_bv": inputs[a + "bv"].reshape(NG, P), "a_scale": inputs[a + "attn_scale"],
        "a_wo": contract_rows(inputs[a + "Wo"]), "a_bo": inputs[a + "bo"],
        "c_wq": contract_rows(inputs[c + "wq"]), "c_wk": contract_rows(inputs[c + "wk"]),
        "c_wv": contract_rows(inputs[c + "wv"]), "c_wo": contract_rows(inputs[c + "wo"]),
        "c_bq": inputs[c + "bq"].reshape(NG, P).T, "c_bk": inputs[c + "bk"].reshape(NG, P).T,
        "c_bv": inputs[c + "bv"], "c_bo": inputs[c + "bo"],
        "gate": contract_rows(inputs[f + "gate_weight"]), "e_bias": inputs[f + "e_bias"],
        "s_gate": contract_rows(inputs[f + "shared_gate"]), "s_up": contract_rows(inputs[f + "shared_up"]),
        "s_down": contract_rows(inputs[f + "shared_down"]),
        "w1": by_expert(inputs[f + "w1"]), "w3": by_expert(inputs[f + "w3"]), "w2": by_expert(inputs[f + "w2"]),
    }
    nc = bacc.Bacc("TRN2", target_bir_lowering=False, num_devices=1)
    arrays = {"in_" + k: np.ascontiguousarray(v) for k, v in laid.items()}
    t = {k: nc.dram_tensor("in_" + k, arrays["in_" + k].shape, mybir.dt.from_np(arrays["in_" + k].dtype),
                           kind="ExternalInput").ap() for k in laid}
    t["out"] = nc.dram_tensor("out", [BATCH * SEQ, DM], F32, kind="ExternalOutput").ap()
    program(nc, t)
    r = run_bass_kernel_spmd(nc, [arrays], core_ids=[0])
    return r.results[0]["out"].reshape(BATCH, SEQ, DM)
```
